# Optimizing a Trainium2 kernel written in Bass

```python
import numpy as np
import jax
import jax.numpy as jnp

def _softmax(x, axis=-1):
    return jax.nn.softmax(x, axis=axis)

def _gelu(x):
    return jax.nn.gelu(x, approximate=True)

def _silu(x):
    return jax.nn.silu(x)

def _sigmoid(x):
    return jax.nn.sigmoid(x)

def _layernorm(x, axis=-1, eps=1e-05):
    m = jnp.mean(x, axis=axis, keepdims=True)
    v = jnp.var(x, axis=axis, keepdims=True)
    return (x - m) / jnp.sqrt(v + eps)

def _scatter_add(tgt, idx, src, axis=0):
    return tgt.at[idx].add(src)

def _segment_sum(src, seg, n):
    return jax.ops.segment_sum(src, seg, n)
kernel_name = 'mk_conv_preact_d4_conv_nhwc128_r2_d8515e'

def setup_inputs(seed: int=0):
    np.random.seed(seed)
    _w = jnp.asarray

    def _rec_inputs():
        import jax
        import jax.numpy as jnp
        _gk = jax.random.key(seed)
        x = -0.000125 + 0.9999 * jax.random.normal(jax.random.fold_in(_gk, 1), (1, 256, 256, 64), jnp.float32)
        return x
    x = _rec_inputs()

    def _L0_conv_setup():
        import jax, jax.numpy as jnp
        import numpy as np
        EPS = 1e-05

        def _ln(x, g, b):
            m = jnp.mean(x, axis=-1, keepdims=True)
            v = jnp.var(x, axis=-1, keepdims=True)
            return (x - m) / jnp.sqrt(v + EPS) * g + b
        key = jax.random.key(seed)
        ks = jax.random.split(key, 16)
        B, N, CZ, C = (1, 256, 64, 16)
        s_cz = 1.0 / np.sqrt(CZ)
        s_c = 1.0 / np.sqrt(C)

        def lin(k, fan_in, shape):
            return jax.random.uniform(k, shape, jnp.float32, -1.0, 1.0) / np.sqrt(fan_in)
        return {'x': jax.random.normal(ks[0], (B, N, N, CZ), jnp.float32), 'Wa1': lin(ks[1], CZ, (CZ, C)), 'ba1': lin(ks[2], CZ, (C,)), 'Wa2': lin(ks[3], CZ, (CZ, C)), 'ba2': lin(ks[4], CZ, (C,)), 'Wb1': lin(ks[5], CZ, (CZ, C)), 'bb1': lin(ks[6], CZ, (C,)), 'Wb2': lin(ks[7], CZ, (CZ, C)), 'bb2': lin(ks[8], CZ, (C,)), 'ln2_g': jnp.ones((C,), jnp.float32), 'ln2_b': jnp.zeros((C,), jnp.float32), 'Wg': lin(ks[9], CZ, (CZ, CZ)), 'bg': lin(ks[10], CZ, (CZ,)), 'Wz': lin(ks[11], C, (C, CZ)), 'bz': lin(ks[12], C, (CZ,))}
    _L0_conv_all = _L0_conv_setup()
    _L0_conv_in = {k: v for k, v in _L0_conv_all.items() if k in ('Wa1', 'ba1', 'Wa2', 'ba2', 'Wb1', 'bb1', 'Wb2', 'bb2', 'ln2_g', 'ln2_b', 'Wg', 'bg', 'Wz', 'bz')}
    del _L0_conv_all

    def _L1_conv_setup():
        import jax, jax.numpy as jnp
        import numpy as np
        DIM = 64

        def layer_norm(x, w, b, eps=1e-05):
            mu = jnp.mean(x, axis=-1, keepdims=True)
            var = jnp.var(x, axis=-1, keepdims=True)
            return (x - mu) * jax.lax.rsqrt(var + eps) * w + b
        key = jax.random.key(seed)
        ks = jax.random.split(key, 8)
        B, N, D = (1, 256, DIM)
        x = jax.random.normal(ks[0], (B, N, N, D), dtype=jnp.float32)
        mask = jnp.ones((B, N, N), dtype=jnp.float32)
        pi_w = jax.random.normal(ks[1], (D, D), dtype=jnp.float32) * (1.0 / np.sqrt(D))
        gi_w = jax.random.normal(ks[2], (D, D), dtype=jnp.float32) * 0.02
        pi_b = jnp.zeros((D,), dtype=jnp.float32)
        gi_b = jnp.ones((D,), dtype=jnp.float32)
        po_w = jax.random.normal(ks[3], (D, D // 2), dtype=jnp.float32) * 0.02
        go_w = jax.random.normal(ks[4], (D, D // 2), dtype=jnp.float32) * 0.02
        po_b = jnp.zeros((D,), dtype=jnp.float32)
        go_b = jnp.ones((D,), dtype=jnp.float32)
        ni_w = jnp.ones((D,), dtype=jnp.float32)
        ni_b = jnp.zeros((D,), dtype=jnp.float32)
        no_w = jnp.ones((D // 2,), dtype=jnp.float32)
        no_b = jnp.zeros((D // 2,), dtype=jnp.float32)
        return dict(x=x, mask=mask, pi_w=pi_w, gi_w=gi_w, pi_b=pi_b, gi_b=gi_b, po_w=po_w, go_w=go_w, po_b=po_b, go_b=go_b, ni_w=ni_w, ni_b=ni_b, no_w=no_w, no_b=no_b)
    _L1_conv_all = _L1_conv_setup()
    _L1_conv_in = {k: v for k, v in _L1_conv_all.items() if k in ('mask', 'pi_w', 'gi_w', 'pi_b', 'gi_b', 'po_w', 'go_w', 'po_b', 'go_b', 'ni_w', 'ni_b', 'no_w', 'no_b')}
    del _L1_conv_all

    def _L2_conv_setup():
        import jax, jax.numpy as jnp
        import numpy as np
        B, N, C = (1, 256, 64)
        EPS = 1e-05
        ENDING = False

        def layer_norm(x, w, b):
            mu = jnp.mean(x, axis=-1, keepdims=True)
            var = jnp.mean(jnp.square(x - mu), axis=-1, keepdims=True)
            return (x - mu) * jax.lax.rsqrt(var + EPS) * w + b
        key = jax.random.key(seed)
        ks = jax.random.split(key, 10)
        s = 0.02
        return {'x': jax.random.normal(ks[0], (B, N, N, C), dtype=jnp.float32), 'norm_in_w': jnp.ones((C,), jnp.float32), 'norm_in_b': jnp.zeros((C,), jnp.float32), 'g_in_w': jax.random.normal(ks[1], (2 * C, C), jnp.float32) * s, 'p_in_w': jax.random.normal(ks[2], (2 * C, C), jnp.float32) * s, 'g_out_w': jax.random.normal(ks[3], (C, C), jnp.float32) * s, 'norm_out_w': jnp.ones((C,), jnp.float32), 'norm_out_b': jnp.zeros((C,), jnp.float32), 'p_out_w': jax.random.normal(ks[4], (C, C), jnp.float32) * s}
    _L2_conv_all = _L2_conv_setup()
    _L2_conv_in = {k: v for k, v in _L2_conv_all.items() if k in ('norm_in_w', 'norm_in_b', 'g_in_w', 'p_in_w', 'g_out_w', 'norm_out_w', 'norm_out_b', 'p_out_w')}
    del _L2_conv_all

    def _L3_conv_setup():
        import jax, jax.numpy as jnp
        import numpy as np
        DIM = 64
        HID = 64
        EPS = 1e-06

        def _layernorm(x, scale, bias):
            mu = jnp.mean(x, axis=-1, keepdims=True)
            var = jnp.mean(jnp.square(x - mu), axis=-1, keepdims=True)
            return (x - mu) * jax.lax.rsqrt(var + EPS) * scale + bias
        key = jax.random.key(seed)
        ks = jax.random.split(key, 16)
        B, N = (1, 256)
        s = 1.0 / np.sqrt(DIM)
        inp = {'x': jax.random.normal(ks[0], (B, N, N, DIM), dtype=jnp.float32), 'src_mask': jnp.ones((B, N), dtype=jnp.float32), 'norm_scale': jnp.ones((DIM,), jnp.float32), 'norm_bias': jnp.zeros((DIM,), jnp.float32), 'W_left': jax.random.normal(ks[1], (DIM, HID), jnp.float32) * s, 'b_left': jnp.zeros((HID,), jnp.float32), 'W_right': jax.random.normal(ks[2], (DIM, HID), jnp.float32) * s, 'b_right': jnp.zeros((HID,), jnp.float32), 'W_lgate': jax.random.normal(ks[3], (DIM, HID), jnp.float32) * s, 'b_lgate': jnp.zeros((HID,), jnp.float32), 'W_rgate': jax.random.normal(ks[4], (DIM, HID), jnp.float32) * s, 'b_rgate': jnp.zeros((HID,), jnp.float32), 'W_ogate': jax.random.normal(ks[5], (DIM, HID), jnp.float32) * s, 'b_ogate': jnp.zeros((HID,), jnp.float32), 'out_norm_scale': jnp.ones((HID,), jnp.float32), 'out_norm_bias': jnp.zeros((HID,), jnp.float32), 'W_out': jax.random.normal(ks[6], (HID, DIM), jnp.float32) * (1.0 / np.sqrt(HID)), 'b_out': jnp.zeros((DIM,), jnp.float32)}
        return inp
    _L3_conv_all = _L3_conv_setup()
    _L3_conv_in = {k: v for k, v in _L3_conv_all.items() if k in ('src_mask', 'norm_scale', 'norm_bias', 'W_left', 'b_left', 'W_right', 'b_right', 'W_lgate', 'b_lgate', 'W_rgate', 'b_rgate', 'W_ogate', 'b_ogate', 'out_norm_scale', 'out_norm_bias', 'W_out', 'b_out')}
    del _L3_conv_all
    return {'x': x, 'L0_conv_Wa1': _L0_conv_in['Wa1'], 'L0_conv_ba1': _L0_conv_in['ba1'], 'L0_conv_Wa2': _L0_conv_in['Wa2'], 'L0_conv_ba2': _L0_conv_in['ba2'], 'L0_conv_Wb1': _L0_conv_in['Wb1'], 'L0_conv_bb1': _L0_conv_in['bb1'], 'L0_conv_Wb2': _L0_conv_in['Wb2'], 'L0_conv_bb2': _L0_conv_in['bb2'], 'L0_conv_ln2_g': _L0_conv_in['ln2_g'], 'L0_conv_ln2_b': _L0_conv_in['ln2_b'], 'L0_conv_Wg': _L0_conv_in['Wg'], 'L0_conv_bg': _L0_conv_in['bg'], 'L0_conv_Wz': _L0_conv_in['Wz'], 'L0_conv_bz': _L0_conv_in['bz'], 'L1_conv_mask': _L1_conv_in['mask'], 'L1_conv_pi_w': _L1_conv_in['pi_w'], 'L1_conv_gi_w': _L1_conv_in['gi_w'], 'L1_conv_pi_b': _L1_conv_in['pi_b'], 'L1_conv_gi_b': _L1_conv_in['gi_b'], 'L1_conv_po_w': _L1_conv_in['po_w'], 'L1_conv_go_w': _L1_conv_in['go_w'], 'L1_conv_po_b': _L1_conv_in['po_b'], 'L1_conv_go_b': _L1_conv_in['go_b'], 'L1_conv_ni_w': _L1_conv_in['ni_w'], 'L1_conv_ni_b': _L1_conv_in['ni_b'], 'L1_conv_no_w': _L1_conv_in['no_w'], 'L1_conv_no_b': _L1_conv_in['no_b'], 'L2_conv_norm_in_w': _L2_conv_in['norm_in_w'], 'L2_conv_norm_in_b': _L2_conv_in['norm_in_b'], 'L2_conv_g_in_w': _L2_conv_in['g_in_w'], 'L2_conv_p_in_w': _L2_conv_in['p_in_w'], 'L2_conv_g_out_w': _L2_conv_in['g_out_w'], 'L2_conv_norm_out_w': _L2_conv_in['norm_out_w'], 'L2_conv_norm_out_b': _L2_conv_in['norm_out_b'], 'L2_conv_p_out_w': _L2_conv_in['p_out_w'], 'L3_conv_src_mask': _L3_conv_in['src_mask'], 'L3_conv_norm_scale': _L3_conv_in['norm_scale'], 'L3_conv_norm_bias': _L3_conv_in['norm_bias'], 'L3_conv_W_left': _L3_conv_in['W_left'], 'L3_conv_b_left': _L3_conv_in['b_left'], 'L3_conv_W_right': _L3_conv_in['W_right'], 'L3_conv_b_right': _L3_conv_in['b_right'], 'L3_conv_W_lgate': _L3_conv_in['W_lgate'], 'L3_conv_b_lgate': _L3_conv_in['b_lgate'], 'L3_conv_W_rgate': _L3_conv_in['W_rgate'], 'L3_conv_b_rgate': _L3_conv_in['b_rgate'], 'L3_conv_W_ogate': _L3_conv_in['W_ogate'], 'L3_conv_b_ogate': _L3_conv_in['b_ogate'], 'L3_conv_out_norm_scale': _L3_conv_in['out_norm_scale'], 'L3_conv_out_norm_bias': _L3_conv_in['out_norm_bias'], 'L3_conv_W_out': _L3_conv_in['W_out'], 'L3_conv_b_out': _L3_conv_in['b_out']}

def reference(x, L0_conv_Wa1, L0_conv_ba1, L0_conv_Wa2, L0_conv_ba2, L0_conv_Wb1, L0_conv_bb1, L0_conv_Wb2, L0_conv_bb2, L0_conv_ln2_g, L0_conv_ln2_b, L0_conv_Wg, L0_conv_bg, L0_conv_Wz, L0_conv_bz, L1_conv_mask, L1_conv_pi_w, L1_conv_gi_w, L1_conv_pi_b, L1_conv_gi_b, L1_conv_po_w, L1_conv_go_w, L1_conv_po_b, L1_conv_go_b, L1_conv_ni_w, L1_conv_ni_b, L1_conv_no_w, L1_conv_no_b, L2_conv_norm_in_w, L2_conv_norm_in_b, L2_conv_g_in_w, L2_conv_p_in_w, L2_conv_g_out_w, L2_conv_norm_out_w, L2_conv_norm_out_b, L2_conv_p_out_w, L3_conv_src_mask, L3_conv_norm_scale, L3_conv_norm_bias, L3_conv_W_left, L3_conv_b_left, L3_conv_W_right, L3_conv_b_right, L3_conv_W_lgate, L3_conv_b_lgate, L3_conv_W_rgate, L3_conv_b_rgate, L3_conv_W_ogate, L3_conv_b_ogate, L3_conv_out_norm_scale, L3_conv_out_norm_bias, L3_conv_W_out, L3_conv_b_out):
    import jax
    import jax.numpy as jnp

    def _L0_conv_ref(x, Wa1, ba1, Wa2, ba2, Wb1, bb1, Wb2, bb2, ln2_g, ln2_b, Wg, bg, Wz, bz):
        import jax, jax.numpy as jnp
        import numpy as np
        EPS = 1e-05

        def _ln(x, g, b):
            m = jnp.mean(x, axis=-1, keepdims=True)
            v = jnp.var(x, axis=-1, keepdims=True)
            return (x - m) / jnp.sqrt(v + EPS) * g + b
        direction = 'outgoing'
        a = jax.nn.sigmoid((x @ Wa1 + ba1) * (x @ Wa2 + ba2))
        b = jax.nn.sigmoid((x @ Wb1 + bb1) * (x @ Wb2 + bb2))
        if direction == 'incoming':
            a = jnp.swapaxes(a, 1, 2)
            b = jnp.swapaxes(b, 1, 2)
        g = jax.nn.sigmoid(x @ Wg + bg)
        z = jnp.einsum('bikc,bkjc->bijc', a, b)
        return g * (_ln(z, ln2_g, ln2_b) @ Wz + bz)

    def _L1_conv_ref(x, mask, pi_w, gi_w, pi_b, gi_b, po_w, go_w, po_b, go_b, ni_w, ni_b, no_w, no_b):
        import jax, jax.numpy as jnp
        import numpy as np
        DIM = 64

        def layer_norm(x, w, b, eps=1e-05):
            mu = jnp.mean(x, axis=-1, keepdims=True)
            var = jnp.var(x, axis=-1, keepdims=True)
            return (x - mu) * jax.lax.rsqrt(var + eps) * w + b
        h = layer_norm(x, ni_w, ni_b)
        h = (h @ pi_w.T + pi_b) * jax.nn.sigmoid(h @ gi_w.T + gi_b)
        h = h * mask[..., None]
        a1, b1, a2, b2 = jnp.split(h.astype(jnp.float32), 4, axis=-1)
        x1 = jnp.einsum('bikd,bjkd->bijd', a1, b1)
        x2 = jnp.einsum('bkid,bkjd->bijd', a2, b2)
        h = jnp.concatenate([x1, x2], axis=-1).astype(h.dtype)
        h = layer_norm(h, no_w, no_b)
        return (h @ po_w.T + po_b) * jax.nn.sigmoid(h @ go_w.T + go_b)

    def _L2_conv_ref(x, norm_in_w, norm_in_b, g_in_w, p_in_w, g_out_w, norm_out_w, norm_out_b, p_out_w):
        import jax, jax.numpy as jnp
        import numpy as np
        B, N, C = (1, 256, 64)
        EPS = 1e-05
        ENDING = False

        def layer_norm(x, w, b):
            mu = jnp.mean(x, axis=-1, keepdims=True)
            var = jnp.mean(jnp.square(x - mu), axis=-1, keepdims=True)
            return (x - mu) * jax.lax.rsqrt(var + EPS) * w + b
        xn = layer_norm(x, norm_in_w, norm_in_b)
        g_in = jax.nn.sigmoid(jnp.einsum('bijc,dc->bijd', xn, g_in_w))
        p_in = jnp.einsum('bijc,dc->bijd', xn, p_in_w)
        pg = p_in * g_in
        a = pg[..., :C]
        b = pg[..., C:]
        if ENDING:
            tri = jnp.einsum('bkic,bkjc->bijc', a, b)
        else:
            tri = jnp.einsum('bikc,bjkc->bijc', a, b)
        out = layer_norm(tri, norm_out_w, norm_out_b)
        out = jnp.einsum('bijc,dc->bijd', out, p_out_w)
        gate = jax.nn.sigmoid(jnp.einsum('bijc,dc->bijd', xn, g_out_w))
        return out * gate

    def _L3_conv_ref(x, src_mask, norm_scale, norm_bias, W_left, b_left, W_right, b_right, W_lgate, b_lgate, W_rgate, b_rgate, W_ogate, b_ogate, out_norm_scale, out_norm_bias, W_out, b_out):
        import jax, jax.numpy as jnp
        import numpy as np
        DIM = 64
        HID = 64
        EPS = 1e-06

        def _layernorm(x, scale, bias):
            mu = jnp.mean(x, axis=-1, keepdims=True)
            var = jnp.mean(jnp.square(x - mu), axis=-1, keepdims=True)
            return (x - mu) * jax.lax.rsqrt(var + EPS) * scale + bias
        m = src_mask.astype(jnp.float32)
        mask = (m[:, :, None] * m[:, None, :])[..., None]
        xn = _layernorm(x, norm_scale, norm_bias)
        left = (xn @ W_left + b_left) * mask
        right = (xn @ W_right + b_right) * mask
        left = left * jax.nn.sigmoid(xn @ W_lgate + b_lgate)
        right = right * jax.nn.sigmoid(xn @ W_rgate + b_rgate)
        out_gate = jax.nn.sigmoid(xn @ W_ogate + b_ogate)
        out = jnp.einsum('bkid,bkjd->bijd', left, right)
        out = _layernorm(out, out_norm_scale, out_norm_bias) * out_gate
        return out @ W_out + b_out

    def _gn(v, G=32, eps=1e-05):
        B_, H_, W_, C_ = v.shape
        g = v.reshape(B_, H_, W_, G, C_ // G)
        m = jnp.mean(g, axis=(1, 2, 4), keepdims=True)
        s = jnp.var(g, axis=(1, 2, 4), keepdims=True)
        return ((g - m) / jnp.sqrt(s + eps)).reshape(v.shape)

    def _ln_c(v, eps=1e-06):
        m = jnp.mean(v, axis=-1, keepdims=True)
        s = jnp.var(v, axis=-1, keepdims=True)
        return (v - m) / jnp.sqrt(s + eps)

    def _ln_t(v, eps=1e-05):
        m = jnp.mean(v, axis=-1, keepdims=True)
        s = jnp.var(v, axis=-1, keepdims=True)
        return (v - m) / jnp.sqrt(s + eps)

    def _to_tokens(v):
        B_, H_, W_, C_ = v.shape
        return v.reshape(B_, H_ * W_, C_)

    def _from_tokens(t, like):
        return t.reshape(like.shape)
    x = x + _L0_conv_ref(_gn(x), L0_conv_Wa1, L0_conv_ba1, L0_conv_Wa2, L0_conv_ba2, L0_conv_Wb1, L0_conv_bb1, L0_conv_Wb2, L0_conv_bb2, L0_conv_ln2_g, L0_conv_ln2_b, L0_conv_Wg, L0_conv_bg, L0_conv_Wz, L0_conv_bz)
    x = x + _L1_conv_ref(_gn(x), L1_conv_mask, L1_conv_pi_w, L1_conv_gi_w, L1_conv_pi_b, L1_conv_gi_b, L1_conv_po_w, L1_conv_go_w, L1_conv_po_b, L1_conv_go_b, L1_conv_ni_w, L1_conv_ni_b, L1_conv_no_w, L1_conv_no_b)
    x = x + _L2_conv_ref(_gn(x), L2_conv_norm_in_w, L2_conv_norm_in_b, L2_conv_g_in_w, L2_conv_p_in_w, L2_conv_g_out_w, L2_conv_norm_out_w, L2_conv_norm_out_b, L2_conv_p_out_w)
    x = x + _L3_conv_ref(_gn(x), L3_conv_src_mask, L3_conv_norm_scale, L3_conv_norm_bias, L3_conv_W_left, L3_conv_b_left, L3_conv_W_right, L3_conv_b_right, L3_conv_W_lgate, L3_conv_b_lgate, L3_conv_W_rgate, L3_conv_b_rgate, L3_conv_W_ogate, L3_conv_b_ogate, L3_conv_out_norm_scale, L3_conv_out_norm_bias, L3_conv_W_out, L3_conv_b_out)
    return x

_drawn_inputs = setup_inputs


def setup_inputs(seed=0):
    import zlib

    import numpy as np

    out = dict(_drawn_inputs(seed))
    spreads = {'L0_conv_ln2_g': (1.0, 0.2),
     'L0_conv_ln2_b': (0.0, 0.1),
     'L1_conv_pi_b': (0.0, 0.1),
     'L1_conv_gi_b': (1.0, 0.6),
     'L1_conv_po_b': (0.0, 0.1),
     'L1_conv_go_b': (1.0, 0.6),
     'L1_conv_ni_w': (1.0, 0.6),
     'L1_conv_ni_b': (0.0, 0.1),
     'L1_conv_no_w': (1.0, 0.6),
     'L1_conv_no_b': (0.0, 0.582),
     'L2_conv_norm_in_w': (1.0, 0.561),
     'L2_conv_norm_in_b': (0.0, 0.1),
     'L2_conv_norm_out_w': (1.0, 0.535),
     'L2_conv_norm_out_b': (0.0, 0.8),
     'L3_conv_norm_scale': (1.0, 0.2),
     'L3_conv_norm_bias': (0.0, 0.1),
     'L3_conv_b_left': (0.0, 0.1),
     'L3_conv_b_right': (0.0, 0.1),
     'L3_conv_b_lgate': (0.0, 0.523),
     'L3_conv_b_rgate': (0.0, 0.536),
     'L3_conv_b_ogate': (0.0, 0.504),
     'L3_conv_out_norm_scale': (1.0, 0.2),
     'L3_conv_out_norm_bias': (0.0, 0.1),
     'L3_conv_b_out': (0.0, 0.1)}
    factors = {'L0_conv_bg': 3.669,
     'L1_conv_gi_w': 8.0,
     'L1_conv_go_w': 8.0,
     'L2_conv_g_in_w': 5.207,
     'L2_conv_g_out_w': 7.675}
    for name, (base, spread) in spreads.items():
        noise = np.random.default_rng([zlib.crc32(name.encode()), seed]).standard_normal(out[name].shape)
        drawn = base * np.exp(spread * noise) if base else spread * noise
        out[name] = jnp.asarray(drawn.astype(out[name].dtype))
    for name, factor in factors.items():
        out[name] = (out[name] * factor).astype(out[name].dtype)
    return out
```

```python
from contextlib import ExitStack

import numpy as np

import concourse.bass as bass
from concourse import mybir

F32 = mybir.dt.float32
BF16 = mybir.dt.bfloat16
ALU = mybir.AluOpType
ACT = mybir.ActivationFunctionType
ds = bass.ds

P = 128
N = 256
C = 64
HALF = N * N // 2
T = 512
NT = HALF // T
J = 4
PITCH = HALF + 1024

K_ID, K_C64, K_C32, K_C16, K_GRP, K_SUM, K_EPS5, K_EPS6, K_POW, K_SEL = (
    0, 128, 256, 384, 512, 640, 774, 775, 776, 777)
K_ALL = K_SEL + 3 * J * P
SEL = {1: 0, 2: J, 4: 2 * J}


def constants():
    k = np.zeros((P, K_ALL), np.float32)
    row = np.arange(P)
    k[:, K_ID:K_ID + P] = np.eye(P)
    for at, n in ((K_C64, 64), (K_C32, 32), (K_C16, 16)):
        k[:, at:at + P] = np.eye(P) - (row[:, None] // n == row[None] // n) / n
    k[:, K_GRP:K_GRP + P] = (row[:, None] % C // 2 == row[None] % C // 2) / 4
    k[row, K_SUM + 2 * (J - 1) + row // C] = 1 / C
    k[:, K_EPS5], k[:, K_EPS6], k[:, K_POW] = 1e-5, 1e-6, -0.5
    for nq, at in SEL.items():
        cz = C // nq
        for j in range(J):
            for part in range(3):
                for q in range(nq):
                    for h in range(2):
                        col = K_SEL + (at + j) * P + q * 2 * cz + h * cz
                        k[part * 32 + q * 2 * J + 2 * j + h, col:col + cz] = 1
    return k


def known(eng, value):
    return value if isinstance(value, int) else eng.snap(value)


def at_least(eng, sem, value):
    if not isinstance(value, int) or value > 0:
        eng.wait_ge(sem, value)


class Steps:

    def __init__(self, sem):
        self.sem, self.n = sem, 0

    def done(self, instruction):
        instruction.then_inc(self.sem, 1)
        self.n += 1

    def wait(self, eng):
        at_least(eng, self.sem, self.n)


WEIGHTS = (["w12", "wg"] + [f"wz{q}" for q in range(4)]
           + ["gi", "pi", "po0", "po1", "go0", "go1"]
           + ["gl", "gr", "gate", "pl", "pr", "pout"]
           + ["lg", "rg", "og", "left", "right", "zc", "wout"]
           + ["w12s", "wgs", "center"])
SLOT = {name: n for n, name in enumerate(WEIGHTS)}
VECTORS = ["b12", "bg", "bz", "ln2_g", "ln2_b",
           "pi_b", "gi_b", "po_b", "go_b", "ni_w", "ni_b", "no_w", "no_b",
           "norm_in_w", "norm_in_b", "norm_out_w", "norm_out_b",
           "norm_scale", "norm_bias", "b_left", "b_right", "b_lgate", "b_rgate", "b_ogate",
           "out_norm_scale", "out_norm_bias", "b_out"]
VEC = {name: n for n, name in enumerate(VECTORS)}
FOLDS = ([(f"wz{q}", "ln2_g", "ln2_b", "bz", K_C16) for q in range(4)]
         + [("gi", "ni_w", "ni_b", "gi_b", None), ("pi", "ni_w", "ni_b", "pi_b", None)]
         + [(f"{w}{q}", "no_w", "no_b", f"{w}_b", K_C32) for w in ("po", "go") for q in range(2)]
         + [(w, "norm_in_w", "norm_in_b", None, None) for w in ("gl", "gr", "gate", "pl", "pr")]
         + [("pout", "norm_out_w", "norm_out_b", None, K_C64)]
         + [(w, "norm_scale", "norm_bias", b, None) for w, b in (
             ("lg", "b_lgate"), ("rg", "b_rgate"), ("og", "b_ogate"), ("left", "b_left"), ("right", "b_right"))])
BIAS = {f[0]: n for n, f in enumerate(FOLDS)}


class Core:

    def __init__(self, nc, ctx, ins, out):
        self.nc, self.ins, self.out = nc, ins, out
        self.spent = []

        def sb(name, shape, dt=F32):
            return ctx.enter_context(nc.sbuf_tensor(name, shape, dt))

        self.xT = sb("xT", [P, HALF])
        self.w = sb("w", [P, len(WEIGHTS), P])
        self.ident = sb("ident", [P, P])
        self.c64 = sb("c64", [P, P])
        self.grp = sb("grp", [P, P])
        self.summer = sb("summer", [P, 2 * (J - 1) + P])
        self.cols = sb("cols", [P, 3])
        self.sel = sb("sel", [P, 3 * J, P], BF16)
        self.vec = sb("vec", [P, len(VECTORS)])
        self.bias = sb("bias", [P, len(FOLDS)])
        self.stats = sb("stats", [P, NT, 6])
        self.fold = sb("fold", [P, 16])
        self.work = sb("work", [P, 14400])
        self.bank = [ctx.enter_context(nc.psum_tensor(f"bank{n}", [P, T], F32)) for n in range(8)]

        self.hid_d = nc.dram_tensor("hidden_rows", (2 * P, PITCH), F32).ap()
        self.z_d = nc.dram_tensor("z_rows", (P, PITCH), F32).ap()
        self.gate_d = nc.dram_tensor("gate_rows", (P, PITCH), F32).ap()
        self.rstd_d = nc.dram_tensor("rstd_parts", (3, 2 * HALF), BF16).ap()

    def area(self, shape, at, dt=F32):
        n = int(np.prod(shape))
        words = n if dt == F32 else (n + 1) // 2
        ap = self.work[:, at:at + words]
        if dt != F32:
            ap = ap.bitcast(dt)
        if len(shape) == 2:
            ap = ap.rearrange("p (a b) -> p a b", a=shape[0])
        if len(shape) == 3:
            ap = ap.rearrange("p (a b c) -> p a b c", a=shape[0], b=shape[1])
        assert at + words <= self.work.shape[1], (shape, at)
        return ap, at + words

    def sems(self, phase, names):
        if not self.spent or self.spent[-1][0] != phase:
            if len(self.spent) >= 2:
                for s in self.spent[-2][1]:
                    self.nc.gpsimd.sem_clear(s)
            if len(self.spent) >= 3:
                for s in self.spent[-3][1]:
                    self.nc.release_semaphore(s)
            self.spent.append((phase, []))
        found = [self.nc.alloc_semaphore(f"{phase}_{n}") for n in names.split()]
        self.spent[-1][1].extend(found)
        return found


def weight_blocks(ins):
    for h in range(2):
        for s in range(2):
            for k, ab in enumerate("ab"):
                yield "w12", False, h * C, s * 64 + h * 32 + k * 16, ins[f"L0_conv_W{ab}{s + 1}"]
        yield "wg", False, h * C, h * C, ins["L0_conv_Wg"]
        for q in range(4):
            yield f"wz{q}", False, q * 32 + h * 16, h * C, ins["L0_conv_Wz"]
        for name in ("gi", "pi"):
            yield name, True, h * C, h * C, ins[f"L1_conv_{name}_w"]
        for name in ("po", "go"):
            for q in range(2):
                yield f"{name}{q}", True, h * C, q * 64 + h * 32, ins[f"L1_conv_{name}_w"]
        for name, raw, at in (("gl", "g_in_w", 0), ("gr", "g_in_w", C), ("pl", "p_in_w", 0), ("pr", "p_in_w", C),
                              ("gate", "g_out_w", 0), ("pout", "p_out_w", 0)):
            yield name, True, h * C, h * C, ins[f"L2_conv_{raw}"][at:at + C, :]
        for name, raw in (("lg", "lgate"), ("rg", "rgate"), ("og", "ogate"), ("left", "left"), ("right", "right"),
                          ("wout", "out")):
            yield name, False, h * C, h * C, ins[f"L3_conv_W_{raw}"]


def vector_blocks(ins):
    for s in range(2):
        for h in range(2):
            for k, ab in enumerate("ab"):
                yield "b12", s * 64 + h * 32 + k * 16, ins[f"L0_conv_b{ab}{s + 1}"]
    layer = {**dict.fromkeys(VECTORS[1:5], "L0"), **dict.fromkeys(VECTORS[5:13], "L1"),
             **dict.fromkeys(VECTORS[13:17], "L2"), **dict.fromkeys(VECTORS[17:], "L3")}
    for name, l in layer.items():
        v = ins[f"{l}_conv_{name}"]
        for k in range(P // v.shape[0]):
            yield name, k * v.shape[0], v


def load_weights(core):
    nc, ins, bank = core.nc, core.ins, core.bank
    blocks, vectors = list(weight_blocks(ins)), list(vector_blocks(ins))
    turned = sorted({b[0] for b in blocks if b[1]}, key=SLOT.get) + ["zc"]
    consts, at = core.area([K_ALL], 0)
    raw, at = core.area([len(turned), P], at)
    rows, at = core.area([P], at)
    tmp, at = core.area([2, P], at)
    raw_of = {name: raw[:, n, :] for n, name in enumerate(turned)}
    w = lambda name: core.w[:, SLOT[name], :]
    col = lambda name: core.vec[:, VEC[name]:VEC[name] + 1]
    centred = [f for f in FOLDS if f[4] is not None]

    with ExitStack() as ctx:
        cleared, landed, vec_in, pe_s, dve_s, made = core.sems("prep", "cleared landed vec_in pe dve scaled")
        block = ctx.enter_context(nc.Block())

        @block.sync
        def _(sp):
            sp.dma_start(consts, ins["constants"]).then_inc(landed, 16)
            sp.wait_ge(cleared, 3)
            for name, turn, r, c, src in blocks:
                dst = raw_of[name] if turn else w(name)
                n, m = src.shape
                sp.dma_start(dst[r:r + n, c:c + m], src).then_inc(landed, 16)

        @block.scalar
        def _(act):
            act.wait_ge(cleared, 3)
            for name, r, src in vectors:
                n = src.shape[0]
                act.dma_start(rows[VEC[name]:VEC[name] + 1, r:r + n],
                              src.rearrange("(a n) -> a n", a=1)).then_inc(vec_in, 16)

        n_landed = 16 * (len(blocks) + 1)

        @block.tensor
        def _(pe):
            step = Steps(pe_s)
            pe.wait_ge(landed, n_landed)
            pe.wait_ge(vec_in, 16 * len(vectors))
            step.done(pe.transpose(bank[0][:, 0:P], rows, consts[:, K_ID:K_ID + P]))
            for n, name in enumerate(turned):
                if name == "zc":
                    pe.wait_ge(made, 1)
                if n >= 4:
                    pe.wait_ge(dve_s, 7 + n - 3)
                step.done(pe.transpose(bank[1 + n % 4][:, 0:P], raw_of[name], consts[:, K_ID:K_ID + P]))
            pe.wait_ge(dve_s, 7 + len(turned))
            for n, (name, _, shift, _, _) in enumerate(FOLDS):
                mm = pe.matmul(bank[5][:, n:n + 1], w(name), col(shift), start=True, stop=True)
            step.done(mm)
            for n, (name, _, _, _, centre) in enumerate(centred):
                pe.wait_ge(made, 2 + n)
                if n >= 2:
                    pe.wait_ge(cleared, 3 + n - 1)
                step.done(pe.matmul(bank[6 + n % 2][:, 0:P], consts[:, centre:centre + P], tmp[:, n % 2, :],
                                    start=True, stop=True))

        @block.vector
        def _(dve):
            dve.memset(core.w[:, :, :], 0.0).then_inc(cleared, 1)
            dve.memset(raw[:, :, :], 0.0).then_inc(cleared, 1)
            dve.memset(rows, 0.0).then_inc(cleared, 1)
            step = Steps(dve_s)
            dve.wait_ge(landed, n_landed)
            for dst, at, n in ((core.ident, K_ID, P), (core.c64, K_C64, P), (core.grp, K_GRP, P),
                               (core.summer, K_SUM, 2 * (J - 1) + P), (core.cols, K_EPS5, 3)):
                step.done(dve.tensor_copy(dst[:, :], consts[:, at:at + n]))
            step.done(dve.tensor_copy(core.sel[:, :, :].rearrange("p a b -> p (a b)"), consts[:, K_SEL:K_ALL]))
            dve.wait_ge(pe_s, 1)
            step.done(dve.tensor_copy(core.vec[:, :], bank[0][:, 0:len(VECTORS)]))
            step.wait(dve)
            dve.tensor_scalar(raw_of["zc"], consts[:, K_C64:K_C64 + P], col("out_norm_scale"), None,
                              ALU.mult).then_inc(made, 1)
            for n, name in enumerate(turned):
                dve.wait_ge(pe_s, 2 + n)
                step.done(dve.tensor_copy(w(name), bank[1 + n % 4][:, 0:P]))
            step.wait(dve)
            dve.wait_ge(pe_s, 2 + len(turned))
            for n, (name, _, _, b, _) in enumerate(FOLDS):
                if b:
                    step.done(dve.tensor_tensor(core.bias[:, n:n + 1], bank[5][:, n:n + 1], col(b), ALU.add))
                else:
                    step.done(dve.tensor_copy(core.bias[:, n:n + 1], bank[5][:, n:n + 1]))
            first = 2 + len(turned)
            for name, scale, _, _, centre in FOLDS:
                if centre is None:
                    step.done(dve.tensor_scalar(w(name), w(name), col(scale), None, ALU.mult))
            for n, (name, scale, _, _, _) in enumerate(centred):
                if n >= 2:
                    dve.wait_ge(pe_s, first + n - 1)
                    dve.wait_ge(cleared, 3 + n - 1)
                dve.tensor_scalar(tmp[:, n % 2, :], w(name), col(scale), None, ALU.mult).then_inc(made, 1)
                if n >= 1:
                    dve.wait_ge(pe_s, first + n)
                    dve.tensor_copy(w(centred[n - 1][0]), bank[6 + (n - 1) % 2][:, 0:P]).then_inc(cleared, 1)
            dve.wait_ge(pe_s, first + len(centred))
            dve.tensor_copy(w(centred[-1][0]), bank[6 + (len(centred) - 1) % 2][:, 0:P]).then_inc(cleared, 1)


def enter(core):
    nc, bank = core.nc, core.bank
    KC = 8
    x = core.ins["x"].rearrange("a (h p) (n k) c -> (a n) p h k c", h=2, k=KC)
    loads = N // KC
    xin = [core.area([2, KC, C], b * 2 * KC * C)[0] for b in range(2)]
    xpix = [core.area([KC, 2, C], (2 + b) * 2 * KC * C)[0] for b in range(2)]
    xT = core.xT[:, :].rearrange("q (p k) -> q p k", k=N)
    with ExitStack() as ctx:
        in0, in1, paired, turned, kept, counted = core.sems("enter", "in0 in1 paired turned kept counted")
        landed = [in0, in1]
        block = ctx.enter_context(nc.Block())

        @block.sync
        def _(sp):
            def load(n, b):
                n_at = known(sp, n)
                at_least(sp, paired, n - 1)
                for h in range(2):
                    sp.dma_start(xin[b][:, h, :, :], x[ds(n_at, 1), :, h, :, :].rearrange("a p k c -> p (a k) c")
                                 ).then_inc(landed[b], 16)
            for b in range(2):
                load(b, b)
            with sp.Fori(1, loads // 2) as i:
                for b in range(2):
                    load(2 * i + b, b)

        @block.tensor
        def _(pe):
            def turn(n, b):
                pe.wait_ge(paired, n + 1)
                for half in range(2):
                    at_least(pe, kept, 2 * n + half - 1)
                    at_least(pe, counted, 2 * n + half - 1)
                    for k in range(4):
                        mm = pe.transpose(bank[half][:, k * P:(k + 1) * P], xpix[b][:, 4 * half + k, :, :].rearrange("p h c -> p (h c)"), core.ident[:, :])
                    mm.then_inc(turned, 1)
            for b in range(2):
                turn(b, b)
            with pe.Fori(1, loads // 2) as i:
                for b in range(2):
                    turn(2 * i + b, b)

        @block.scalar
        def _(act):
            with act.Fori(0, loads // 2) as i:
                for b in range(4):
                    act.wait_ge(turned, 4 * i + b + 1)
                    act.wait_ge(counted, 4 * i + b + 1)
                    nc.scalar.copy(xT[:, :, ds((4 * i + b) * 4, 4)],
                                   bank[b % 2][:, :].rearrange("q (k p) -> q p k", p=P)).then_inc(kept, 1)

        @block.vector
        def _(dve):
            def load(n, b):
                dve.wait_ge(landed[b], (n - b) * 16 + 32)
                at_least(dve, turned, 2 * n - 2)
                dve.tensor_copy(xpix[b].rearrange("p k h c -> p h k c"), xin[b]).then_inc(paired, 1)
                for half in range(2):
                    dve.wait_ge(turned, 2 * n + half + 1)
                    dve.bn_stats(core.stats[:, ds(2 * n + half, 1), :].rearrange("p a s -> p (a s)"),
                                 bank[half][:, :]).then_inc(counted, 1)
            for b in range(2):
                load(b, b)
            with dve.Fori(1, loads // 2) as i:
                for b in range(2):
                    load(2 * i + b, b)


def fold_group_norm(core, layer):
    nc, bank = core.nc, core.bank
    f = core.fold
    mean_var, gmean, dev, spread, gvar, r, b = (f[:, 0:2], f[:, 2:3], f[:, 3:4], f[:, 4:5], f[:, 5:6], f[:, 6:7], f[:, 7:8])
    b12, bg, ub = f[:, 8:9], f[:, 9:10], f[:, 10:11]
    w = lambda name: core.w[:, SLOT[name], :]
    with ExitStack() as ctx:
        dve_s, pe_s, pow_s = core.sems(f"fold{layer}", "dve pe pow")
        block = ctx.enter_context(nc.Block())

        @block.vector
        def _(dve):
            step = Steps(dve_s)
            step.done(dve.bn_aggr(mean_var, core.stats[:, :, :].rearrange("p n s -> p (n s)")))
            dve.wait_ge(pe_s, 1)
            step.done(dve.tensor_copy(gmean, bank[0][:, 0:1]))
            step.wait(dve)
            step.done(dve.tensor_tensor(dev, mean_var[:, 0:1], gmean, ALU.subtract))
            step.wait(dve)
            step.done(dve.scalar_tensor_tensor(out=spread, in0=dev, scalar=dev, in1=mean_var[:, 1:2],
                                               op0=ALU.mult, op1=ALU.add))
            dve.wait_ge(pe_s, 2)
            step.done(dve.tensor_scalar(gvar, bank[1][:, 0:1], core.cols[:, 0:1], None, ALU.add))
            dve.wait_ge(pow_s, 1)
            step.done(dve.scalar_tensor_tensor(out=b, in0=gmean, scalar=-1.0, in1=r, op0=ALU.mult, op1=ALU.mult))
            if layer == 0:
                step.done(dve.tensor_scalar(w("w12s"), w("w12"), r, None, ALU.mult))
                step.done(dve.tensor_scalar(w("wgs"), w("wg"), r, None, ALU.mult))
                dve.wait_ge(pe_s, 4)
                step.done(dve.tensor_tensor(b12, bank[2][:, 0:1], core.vec[:, VEC["b12"]:VEC["b12"] + 1], ALU.add))
                step.done(dve.tensor_tensor(bg, bank[3][:, 0:1], core.vec[:, VEC["bg"]:VEC["bg"] + 1], ALU.add))
            else:
                step.done(dve.tensor_scalar(w("center"), core.c64[:, :], r, None, ALU.mult))
                dve.wait_ge(pe_s, 3)
                step.done(dve.tensor_copy(ub, bank[2][:, 0:1]))

        @block.gpsimd
        def _(pool):
            pool.wait_ge(dve_s, 5)
            pool.tensor_tensor(r, gvar, core.cols[:, 2:3], ALU.pow).then_inc(pow_s, 1)

        @block.tensor
        def _(pe):
            pe.wait_ge(dve_s, 1)
            pe.matmul(bank[0][:, 0:1], core.grp[:, :], mean_var[:, 0:1], start=True, stop=True).then_inc(pe_s, 1)
            pe.wait_ge(dve_s, 4)
            pe.matmul(bank[1][:, 0:1], core.grp[:, :], spread, start=True, stop=True).then_inc(pe_s, 1)
            pe.wait_ge(dve_s, 6)
            if layer == 0:
                pe.matmul(bank[2][:, 0:1], w("w12"), b, start=True, stop=True).then_inc(pe_s, 1)
                pe.matmul(bank[3][:, 0:1], w("wg"), b, start=True, stop=True).then_inc(pe_s, 1)
            else:
                pe.matmul(bank[2][:, 0:1], core.c64[:, :], b, start=True, stop=True).then_inc(pe_s, 1)
    return b12, bg, ub


def project0(core, b12):
    nc, bank, xT = core.nc, core.bank, core.xT
    first, at = core.area([2, T], 0)
    prod, at = core.area([2, T], at)
    hid, at = core.area([2, T], at)
    wst = core.w[:, SLOT["w12s"], :]
    dst = core.hid_d[0:64, 0:HALF].rearrange("q (n s t) -> n q s t", s=4, t=T)
    with ExitStack() as ctx:
        mm, one, two, act_s, st0, st1 = core.sems("proj0", "mm one two act st0 st1")
        stored = [st0, st1]
        block = ctx.enter_context(nc.Block())

        @block.tensor
        def _(pe):
            def tile(t, b):
                at_least(pe, one, t - 1)
                at_least(pe, two, t - 1)
                pe.matmul(bank[b % 2][:, :], wst, xT[:, ds(t * T, T)], start=True, stop=True).then_inc(mm, 1)
            for b in range(4):
                tile(b, b)
            with pe.Fori(1, NT // 4) as i:
                for b in range(4):
                    tile(4 * i + b, b)

        @block.scalar
        def _(act):
            def pair(t, b):
                for k in range(2):
                    act.wait_ge(mm, t + k + 1)
                    at_least(act, two, t + k - 1)
                    nc.scalar.activation(first[0:64, k, :], bank[k][0:64, :], ACT.Identity,
                                         bias=b12[0:64, :]).then_inc(one, 1)
                act.wait_ge(two, t + 2)
                at_least(act, stored[b], 8 * (t - 2 * b))
                nc.scalar.activation(hid[:, b, :], prod[:, b, :], ACT.Sigmoid).then_inc(act_s, 1)
            for b in range(2):
                pair(2 * b, b)
            with act.Fori(1, NT // 4) as i:
                for b in range(2):
                    pair(4 * i + 2 * b, b)

        @block.vector
        def _(dve):
            def tile(t, p, b):
                k = b % 2
                dve.wait_ge(one, t + 1)
                at_least(dve, act_s, p - 1)
                dve.scalar_tensor_tensor(out=prod[64 * k:64 * k + 64, b // 2, :], in0=bank[k][64:128, :],
                                         scalar=b12[64:128, :], in1=first[0:64, k, :], op0=ALU.add,
                                         op1=ALU.mult).then_inc(two, 1)
            for b in range(4):
                tile(b, b // 2, b)
            with dve.Fori(1, NT // 4) as i:
                for b in range(4):
                    tile(4 * i + b, 2 * i + b // 2, b)

        @block.sync
        def _(sp):
            with sp.Fori(0, NT // 4) as i:
                for b in range(2):
                    i_at = known(sp, i)
                    sp.wait_ge(act_s, 2 * i + b + 1)
                    for k in range(2):
                        sp.dma_start(dst[ds(i_at, 1), :, 2 * b + k, :].rearrange("a q t -> q (a t)"),
                                     hid[64 * k:64 * k + 64, b, :]).then_inc(stored[b], 16)
            for s in stored:
                sp.wait_ge(s, 32 * (NT // 4))


def project(core, layer, gates, values, ub):
    nc, bank, xT = core.nc, core.bank, core.xT
    NG, NV = len(gates), len(values)
    U, STAT, FAC, GB, VB = [bank[0], bank[1]], bank[2], bank[3], [bank[4], bank[5]], [bank[6], bank[7]]
    u, at = core.area([2 * J, T], 0)
    sq, at = core.area([2, T], at)
    h, at = core.area([2, T], at)
    sd, at = core.area([T], at)
    rec, at = core.area([T], at)
    rest, at = core.area([T], at)
    parts, at = core.area([2, T], at, BF16)
    res, at = core.area([2, NG, 2 * T], at)
    groups = NT // J
    eps = core.cols[0:32, 1:2] if layer == 3 else core.cols[0:32, 0:1]
    w = lambda name: core.w[:, SLOT[name], :]
    bias = lambda name: core.bias[:, BIAS[name]:BIAS[name] + 1]
    of_gate = {0: 0, NG - 1: NV - 1}
    gate_of = [0, NG - 1][:NV]
    dsts = [core.hid_d[of_gate[m] * P:(of_gate[m] + 1) * P, :] if m in of_gate else core.gate_d for m in range(NG)]

    def schedule(normalise, both, last, loop):
        normalise(0, 0)
        for g in range(2):
            both(g, g % 2)
        with loop(1, groups // 2 - 1) as i:
            for e in range(2):
                both(2 * i + e, e)
        both(groups - 2, 0)
        last(groups - 1, 1)

    with ExitStack() as ctx:
        (u_mm, u_sb, sq_sb, sum_mm, sd_sb, split_s, fac_mm, h_sb, gate_mm, val_mm, gate_sb, val_sb, st0, st1,
         zeroed) = core.sems(f"proj{layer}", "u_mm u_sb sq_sb sum_mm sd_sb split fac_mm h_sb gate_mm val_mm "
                             "gate_sb val_sb st0 st1 zeroed")
        stored = [st0, st1]
        block = ctx.enter_context(nc.Block())

        @block.tensor
        def _(pe):
            def mean_square(g, e, j):
                t = g * J + j
                pe.wait_ge(sq_sb, t + 1)
                if j == 0:
                    at_least(pe, sd_sb, g)
                pe.matmul(STAT[:, :], core.summer[:, 2 * (J - 1 - j):2 * (J - 1 - j) + P], sq[:, j % 2, :],
                          start=(j == 0), stop=(j == J - 1)).then_inc(sum_mm, 1)

            def normalise(g, e):
                for j in range(J):
                    t = g * J + j
                    at_least(pe, u_sb, t - 1)
                    pe.matmul(U[j % 2][:, :], w("center"), xT[:, ds(t * T, T)], start=True, stop=True).then_inc(u_mm, 1)
                    if j:
                        mean_square(g, e, j - 1)
                mean_square(g, e, J - 1)

            def factor(g, e, j):
                t = g * J + j
                if j == 0:
                    pe.wait_ge(split_s, 5 * g + 5)
                at_least(pe, h_sb, t)
                pe.matmul(FAC[:, :], core.sel[:, j, :], parts[:, e, :], start=True, stop=True).then_inc(fac_mm, 1)

            def spread(g, e):
                factor(g, e, 0)
                for j in range(J):
                    t = g * J + j
                    if j < J - 1:
                        factor(g, e, j + 1)
                    pe.wait_ge(h_sb, t + 1)
                    for m in range(NG):
                        n = NG * t + m
                        at_least(pe, gate_sb, n - 1)
                        pe.matmul(GB[(NG * j + m) % 2][:, :], w(gates[m]), h[:, j % 2, :], start=True,
                                  stop=True).then_inc(gate_mm, 1)
                        if m in of_gate:
                            v = of_gate[m]
                            at_least(pe, val_sb, NV * t + v - 1)
                            pe.matmul(VB[(NV * j + v) % 2][:, :], w(values[v]), h[:, j % 2, :], start=True,
                                      stop=True).then_inc(val_mm, 1)

            def both(g, e):
                normalise(g + 1, 1 - e)
                spread(g, e)
            pe.wait_ge(zeroed, 1)
            schedule(normalise, both, spread, pe.Fori)

        @block.scalar
        def _(act):
            def normalise(g, e):
                for j in range(J):
                    t = g * J + j
                    act.wait_ge(u_sb, t + 1)
                    at_least(act, sum_mm, t - 1)
                    nc.scalar.activation(sq[:, j % 2, :], u[:, e * J + j, :], ACT.Square).then_inc(sq_sb, 1)
                act.wait_ge(sum_mm, J * g + J)
                at_least(act, split_s, 5 * g - 4)
                nc.scalar.activation(sd[0:32, :], STAT[0:32, :], ACT.Sqrt, bias=eps).then_inc(sd_sb, 1)

            def spread(g, e):
                for j in range(J):
                    t = g * J + j
                    for m in range(NG):
                        n = NG * t + m
                        act.wait_ge(gate_mm, n + 1)
                        if j % 2 == 0 and m == 0:
                            at_least(act, stored[j // 2], 16 * NG * g)
                        nc.scalar.activation(res[:, j // 2, m, j % 2 * T:j % 2 * T + T], GB[(NG * j + m) % 2][:, :],
                                             ACT.Sigmoid, bias=bias(gates[m])).then_inc(gate_sb, 1)

            def both(g, e):
                normalise(g + 1, 1 - e)
                spread(g, e)
            schedule(normalise, both, spread, act.Fori)

        @block.vector
        def _(dve):
            def centred(g, e):
                for j in range(J):
                    t = g * J + j
                    dve.wait_ge(u_mm, t + 1)
                    at_least(dve, sq_sb, t - 2 * J + 1)
                    at_least(dve, h_sb, t - 2 * J + 1)
                    dve.tensor_scalar(u[:, e * J + j, :], U[j % 2][:, :], ub, None, ALU.add).then_inc(u_sb, 1)

            def split(g, e):
                a, b, c = (parts[32 * n:32 * n + 32, e, :] for n in range(3))
                dve.wait_ge(sd_sb, g + 1)
                at_least(dve, fac_mm, J * (g - 1))
                dve.reciprocal(rec[0:32, :], sd[0:32, :]).then_inc(split_s, 1)
                dve.wait_ge(split_s, 5 * g + 1)
                dve.tensor_copy(a, rec[0:32, :]).then_inc(split_s, 1)
                dve.wait_ge(split_s, 5 * g + 2)
                dve.tensor_tensor(rest[32:64, :], rec[0:32, :], a, ALU.subtract).then_inc(split_s, 1)
                dve.wait_ge(split_s, 5 * g + 3)
                dve.tensor_copy(b, rest[32:64, :]).then_inc(split_s, 1)
                dve.wait_ge(split_s, 5 * g + 4)
                dve.tensor_tensor(c, rest[32:64, :], b, ALU.subtract).then_inc(split_s, 1)

            def normed(g, e, j):
                t = g * J + j
                dve.wait_ge(fac_mm, t + 1)
                at_least(dve, gate_mm, NG * (t - 1))
                at_least(dve, val_mm, NV * (t - 1))
                dve.tensor_tensor(h[:, j % 2, :], FAC[:, :], u[:, e * J + j, :], ALU.mult).then_inc(h_sb, 1)

            def spread(g, e, and_split):
                normed(g, e, 0)
                for j in range(J):
                    t = g * J + j
                    if j < J - 1:
                        normed(g, e, j + 1)
                    for m in range(NV):
                        n = NV * t + m
                        dve.wait_ge(val_mm, n + 1)
                        dve.wait_ge(gate_sb, NG * t + gate_of[m] + 1)
                        r = res[:, j // 2, gate_of[m], j % 2 * T:j % 2 * T + T]
                        dve.scalar_tensor_tensor(out=r, in0=VB[(NV * j + m) % 2][:, :], scalar=bias(values[m]),
                                                 in1=r, op0=ALU.add, op1=ALU.mult).then_inc(val_sb, 1)
                    if and_split and j == 0:
                        split(g + 1, 1 - e)

            def first(g, e):
                centred(g, e)
                split(g, e)

            def both(g, e):
                centred(g + 1, 1 - e)
                spread(g, e, True)
            dve.memset(parts, 0.0).then_inc(zeroed, 1)
            dve.wait_ge(zeroed, 1)
            schedule(first, both, lambda g, e: spread(g, e, False), dve.Fori)

        @block.sync
        def _(sp):
            with sp.Fori(0, groups) as g:
                for k in range(2):
                    at = known(sp, (g * J + 2 * k) * T)
                    sp.wait_ge(val_sb, g * (J * NV) + NV * (2 * k + 2))
                    for m in range(NG):
                        sp.dma_start(dsts[m][:, ds(at, 2 * T)], res[:, k, m, :]).then_inc(stored[k], 16)
            for s in stored:
                sp.wait_ge(s, 16 * NG * groups)


def make_mask(core, layer, mask):
    nc = core.nc
    with ExitStack() as ctx:
        landed, rep, made = core.sems(f"mask{layer}", "landed rep made")
        block = ctx.enter_context(nc.Block())
        if layer == 1:
            @block.sync
            def _(sp):
                sp.dma_start(mask, core.ins["L1_conv_mask"].rearrange("a (h p) k -> p (a h) k", h=2)).then_inc(landed, 16)
                sp.wait_ge(landed, 16)
            return
        m = core.ins["L3_conv_src_mask"]
        m2, at = core.area([P], 6000)
        m1, at = core.area([N], at)
        ones, at = core.area([P], at)
        mcol = core.fold[:, 12:14]

        @block.sync
        def _(sp):
            sp.dma_start(m2[0:2, :], m.rearrange("a (h p) -> (a h) p", h=2)).then_inc(landed, 16)
            sp.dma_start(m1[0:1, :], m).then_inc(landed, 16)

        @block.tensor
        def _(pe):
            pe.wait_ge(landed, 32)
            pe.transpose(core.bank[0][:, 0:2], m2[0:2, :], core.ident[0:2, 0:2]).then_inc(rep, 1)
            pe.wait_ge(made, 1)
            pe.matmul(core.bank[1][:, 0:N], ones[0:1, :], m1[0:1, :], start=True, stop=True).then_inc(rep, 1)

        @block.vector
        def _(dve):
            dve.memset(ones[0:1, :], 1.0).then_inc(made, 1)
            dve.wait_ge(rep, 1)
            dve.tensor_copy(mcol, core.bank[0][:, 0:2]).then_inc(made, 1)
            dve.wait_ge(rep, 2)
            dve.wait_ge(made, 2)
            for k in range(2):
                dve.tensor_scalar(mask[:, k, :], core.bank[1][:, 0:N], mcol[:, k:k + 1], None,
                                  ALU.mult).then_inc(made, 1)


def mix(core, layer, part, channels, rows, offsets, turns, z_row, cz, mask, sums):
    nc, bank = core.nc, core.bank
    z0, s1, s2 = sums
    at = 4 * 2 * N
    ab, at = core.area([8, 2 * N], at)
    masked, at = core.area([4, 2 * N], at)
    tt, at = core.area([4, 2 * N], at)
    zs, at = core.area([2, 2 * N], at)
    dev, at = core.area([2, 2 * N], at)
    sq, at = core.area([2, 2 * N], at)
    src = [r.rearrange("(h m) (p k) -> m p h k", h=2, k=N) for r in rows]
    zdst = core.z_d[0:2 * cz, 0:HALF].rearrange("(h m) (p k) -> m p h k", h=2, k=N)
    turn_a, turn_b = turns
    nturn = turn_a + turn_b
    TB = [[bank[0], bank[1]], [bank[2], bank[3]]]
    ZB = [bank[4], bank[5]]

    with ExitStack() as ctx:
        names = "masked_a masked_b turn_mm ta_sb tb_sb z_mm z_sb dev_sb sq_sb s1_sb s2_sb begun s2_zero"
        (masked_a, masked_b, turn_mm, ta_sb, tb_sb, z_mm, z_sb, dev_sb, sq_sb, s1_sb, s2_sb,
         begun, s2_zero) = core.sems(f"mix{layer}{part}", names)
        landed = core.sems(f"mix{layer}{part}", "in0 in1 in2 in3")
        stored = core.sems(f"mix{layer}{part}", "st0 st1")
        masked_s, t_sb = (masked_a, masked_b), (ta_sb, tb_sb)
        block = ctx.enter_context(nc.Block())

        def each_channel(loop, body):
            for b in range(4):
                body(b, b)
            with loop(1, channels // 4) as i:
                for b in range(4):
                    body(4 * i + b, b)

        def operand(o, b):
            buf = tt[:, 2 * o + b % 2, :] if turns[o] else masked[:, 2 * o + b % 2, :] if mask is not None \
                else ab[:, 2 * b + o, :]
            return buf.rearrange("p (h k) -> p h k", h=2)

        def natural(o, b):
            buf = masked[:, 2 * o + b % 2, :] if mask is not None else ab[:, 2 * b + o, :]
            return buf.rearrange("p (h k) -> p h k", h=2)

        @block.sync
        def _(sp):
            def load(c, b):
                at = [known(sp, c + offset) for offset in offsets]
                if mask is not None:
                    at_least(sp, masked_a, c - 3)
                    at_least(sp, masked_b, c - 3)
                elif nturn == 2:
                    at_least(sp, turn_mm, 2 * (c - 3))
                else:
                    at_least(sp, z_mm, c - 3)
                for o in range(2):
                    sp.dma_start(ab[:, 2 * b + o, :].rearrange("p (h k) -> p h k", h=2),
                                 src[o][ds(at[o], 1)].rearrange("m p h k -> p (m h) k")).then_inc(landed[b], 16)

            def store(c, b):
                at = known(sp, c + z_row)
                sp.wait_ge(z_sb, c + 1)
                sp.dma_start(zdst[ds(at, 1)].rearrange("m p h k -> p (m h) k"),
                             zs[:, b % 2, :].rearrange("p (h k) -> p h k", h=2)).then_inc(stored[b % 2], 16)
            for b in range(4):
                load(b, b)
            with sp.Fori(1, channels // 4) as i:
                for b in range(4):
                    load(4 * i + b, b)
                    store(4 * i + b - 4, b)
            for b in range(4):
                store(channels - 4 + b, b)
            for s in stored:
                sp.wait_ge(s, 8 * channels)

        @block.tensor
        def _(pe):
            def ready(c, b, o):
                if mask is not None:
                    pe.wait_ge(masked_s[o], c + 1)
                else:
                    pe.wait_ge(landed[b], (c - b) * 8 + 32)

            def turn(c, b):
                for o in range(2):
                    if turns[o]:
                        ready(c, b, o)
                        at_least(pe, t_sb[o], c - 1)
                        x = natural(o, b)
                        for kk in range(2):
                            for r in range(2):
                                mm = pe.transpose(TB[o][b % 2][:, kk * N + r * P:kk * N + r * P + P],
                                                  x[:, r, kk * P:kk * P + P], core.ident[:, :])
                        mm.then_inc(turn_mm, 1)

            def product(c, b):
                for o in range(2):
                    if turns[o]:
                        pe.wait_ge(t_sb[o], c + 1)
                    else:
                        ready(c, b, o)
                at_least(pe, z_sb, c - 1)
                a, x = operand(0, b), operand(1, b)
                for r in range(2):
                    for kk in range(2):
                        mm = pe.matmul(ZB[b % 2][:, r * N:r * N + N], a[:, kk, r * P:r * P + P], x[:, kk, :],
                                       start=(kk == 0), stop=(kk == 1))
                mm.then_inc(z_mm, 1)

            if not nturn:
                each_channel(pe.Fori, product)
                return
            for b in range(4):
                turn(b, b)
                if b:
                    product(b - 1, b - 1)
            with pe.Fori(1, channels // 4) as i:
                for b in range(4):
                    turn(4 * i + b, b)
                    product(4 * i + b - 1, (b - 1) % 4)
            product(channels - 1, 3)

        @block.scalar
        def _(act):
            def turned(c, b):
                if turns[0]:
                    act.wait_ge(turn_mm, nturn * c + 1)
                    at_least(act, z_mm, c - 1)
                    nc.scalar.copy(tt[:, b % 2, :], TB[0][b % 2][:, :]).then_inc(ta_sb, 1)

            def out(c, b):
                act.wait_ge(z_mm, c + 1)
                at_least(act, stored[b % 2], 8 * (c - b % 2))
                at_least(act, dev_sb, c - 1)
                nc.scalar.copy(zs[:, b % 2, :], ZB[b % 2][:, :]).then_inc(z_sb, 1)

            def square(c, b):
                act.wait_ge(dev_sb, c + 1)
                at_least(act, s2_sb, c - 1)
                nc.scalar.activation(sq[:, b % 2, :], dev[:, b % 2, :], ACT.Square).then_inc(sq_sb, 1)

            for b in range(4):
                turned(b, b)
                if b:
                    out(b - 1, b - 1)
                if b > 1:
                    square(b - 2, b - 2)
            with act.Fori(1, channels // 4) as i:
                for b in range(4):
                    turned(4 * i + b, b)
                    out(4 * i + b - 1, (b - 1) % 4)
                    square(4 * i + b - 2, (b - 2) % 4)
            out(channels - 1, 3)
            square(channels - 2, 2)
            square(channels - 1, 3)

        @block.vector
        def _(dve):
            def mask_b(c, b):
                if mask is not None:
                    dve.wait_ge(landed[b], (c - b) * 8 + 32)
                    at_least(dve, turn_mm if turn_b else z_mm, nturn * (c - 1) if turn_b else c - 1)
                    dve.tensor_tensor(masked[:, 2 + b % 2, :], ab[:, 2 * b + 1, :], mask.rearrange("p h k -> p (h k)"),
                                      ALU.mult).then_inc(masked_b, 1)

            def turned(c, b):
                if turns[1]:
                    dve.wait_ge(turn_mm, nturn * c + nturn)
                    at_least(dve, z_mm, c - 1)
                    dve.tensor_copy(tt[:, 2 + b % 2, :], TB[1][b % 2][:, :]).then_inc(tb_sb, 1)

            def deviation(c, b):
                dve.wait_ge(z_sb, c + 1)
                at_least(dve, sq_sb, c - 1)
                at_least(dve, s1_sb, c - 1)
                if isinstance(c, int) and c == 0 and part == 0:
                    dve.tensor_copy(z0, zs[:, 0, :]).then_inc(begun, 1)
                    dve.memset(s1, 0.0).then_inc(begun, 1)
                    dve.wait_ge(begun, 2)
                dve.tensor_tensor(dev[:, b % 2, :], zs[:, b % 2, :], z0, ALU.subtract).then_inc(dev_sb, 1)
                dve.wait_ge(dev_sb, c + 1)
                at_least(dve, s1_sb, c)
                dve.tensor_tensor(s1, s1, dev[:, b % 2, :], ALU.add).then_inc(s1_sb, 1)

            mask_b(0, 0)
            for b in range(4):
                if b < 3:
                    mask_b(b + 1, b + 1)
                turned(b, b)
                if b:
                    deviation(b - 1, b - 1)
            with dve.Fori(1, channels // 4) as i:
                for b in range(4):
                    if b == 0:
                        mask_b(4 * i, 0)
                    if b < 3:
                        mask_b(4 * i + b + 1, b + 1)
                    turned(4 * i + b, b)
                    deviation(4 * i + b - 1, (b - 1) % 4)
            deviation(channels - 1, 3)

        @block.gpsimd
        def _(pool):
            def mask_a(c, b):
                if mask is not None:
                    pool.wait_ge(landed[b], (c - b) * 8 + 32)
                    at_least(pool, turn_mm if turn_a else z_mm, nturn * (c - 2) + 1 if turn_a else c - 1)
                    pool.tensor_tensor(masked[:, b % 2, :], ab[:, 2 * b, :], mask.rearrange("p h k -> p (h k)"),
                                       ALU.mult).then_inc(masked_a, 1)

            def squares(c, b):
                pool.wait_ge(sq_sb, c + 1)
                at_least(pool, s2_sb, c)
                pool.tensor_tensor(s2, s2, sq[:, b % 2, :], ALU.add).then_inc(s2_sb, 1)

            if part == 0:
                pool.memset(s2, 0.0).then_inc(s2_zero, 1)
                pool.wait_ge(s2_zero, 1)
            mask_a(0, 0)
            mask_a(1, 1)
            mask_a(2, 2)
            squares(0, 0)
            mask_a(3, 3)
            squares(1, 1)
            with pool.Fori(1, channels // 4) as i:
                for b in range(4):
                    mask_a(4 * i + b, b)
                    squares(4 * i + b - 2, (b - 2) % 4)
            squares(channels - 2, 2)
            squares(channels - 1, 3)


def fold_sums(core, layer, cz, sums):
    nc = core.nc
    z0, s1, s2 = sums
    at = 4 * 2 * N
    mean, at = core.area([2 * N], at)
    var, at = core.area([2 * N], at)
    rec, at = core.area([2 * N], at)
    parts, at = core.area([3, 2 * N], at, BF16)
    eps = core.cols[:, 1:2] if layer == 3 else core.cols[:, 0:1]
    with ExitStack() as ctx:
        dve_s, root, stored = core.sems(f"var{layer}", "dve root stored")
        block = ctx.enter_context(nc.Block())

        @block.vector
        def _(dve):
            step = Steps(dve_s)

            def then(ins):
                step.done(ins)
                step.wait(dve)
            then(dve.tensor_scalar(mean, s1, 1.0 / cz, None, ALU.mult))
            then(dve.tensor_tensor(mean, mean, mean, ALU.mult))
            then(dve.scalar_tensor_tensor(out=var, in0=s2, scalar=1.0 / cz, in1=mean, op0=ALU.mult, op1=ALU.subtract))
            then(dve.tensor_scalar(var, var, 0.0, None, ALU.max))
            dve.wait_ge(root, 1)
            then(dve.reciprocal(rec, mean))
            then(dve.tensor_copy(parts[:, 0, :], rec))
            then(dve.tensor_tensor(var, rec, parts[:, 0, :], ALU.subtract))
            then(dve.tensor_copy(parts[:, 1, :], var))
            then(dve.tensor_tensor(parts[:, 2, :], var, parts[:, 1, :], ALU.subtract))

        @block.scalar
        def _(act):
            act.wait_ge(dve_s, 4)
            nc.scalar.activation(mean, var, ACT.Sqrt, bias=eps).then_inc(root, 1)

        @block.sync
        def _(sp):
            sp.wait_ge(dve_s, 9)
            for n in range(3):
                sp.dma_start(core.rstd_d[n:n + 1, :].rearrange("a (h p k) -> p (a h) k", h=2, k=N),
                             parts[:, n, :].rearrange("p (h k) -> p h k", h=2)).then_inc(stored, 16)
            sp.wait_ge(stored, 48)


def finish(core, layer, nq, bg):
    nc, bank, xT = core.nc, core.bank, core.xT
    cz = C // nq
    sets = NT // nq
    groups = sets // J
    out_w = {0: [f"wz{q}" for q in range(4)], 1: ["po0", "po1"], 2: ["pout"], 3: ["wout"]}[layer]
    stored_gate = layer >= 2
    FAC, OB, GB = [bank[0], bank[1]], [bank[2], bank[3]], [bank[4], bank[5]]
    z, at = core.area([2, J, T], 0)
    gate, at = core.area([2, J, T], at)
    parts, at = core.area([2, T], at, BF16)
    zn, at = core.area([2, T], at)
    term, at = core.area([2, T], at)
    w = lambda name: core.w[:, SLOT[name], :]
    bias = lambda name: core.bias[:, BIAS[name]:BIAS[name] + 1]
    vec = lambda name: core.vec[:, VEC[name]:VEC[name] + 1]
    out_b = vec("b_out") if layer == 3 else bias(out_w[0])
    gate_b = bg if layer == 0 else bias("go0") if layer == 1 else None
    NL = nq + 3 * nq + stored_gate

    def each_group(loop, body):
        for g in range(2):
            body(g, g % 2)
        with loop(1, groups // 2) as i:
            for e in range(2):
                body(2 * i + e, e)

    def tile_at(g, j, q):
        return q * sets * T + (g * J + j) * T

    with ExitStack() as ctx:
        fac_mm, zn_sb, gate_mm, gate_sb, out_mm, term_sb, x_sb, stat_sb, cen_mm, cen_sb, zeroed = core.sems(
            f"fin{layer}", "fac_mm zn_sb gate_mm gate_sb out_mm term_sb x_sb stat_sb cen_mm cen_sb zeroed")
        landed = core.sems(f"fin{layer}", "in0 in1")
        block = ctx.enter_context(nc.Block())
        SET = J * nq

        @block.sync
        def _(sp):
            def load(g, e):
                columns = [known(sp, tile_at(g, 0, q)) for q in range(nq)]
                tiles = [known(sp, q * sets + g * J) for q in range(nq)]
                at_least(sp, zn_sb, J * (g - 1))
                if stored_gate:
                    at_least(sp, cen_sb if layer == 3 else term_sb, SET * (g - 1))
                for q in range(nq):
                    sp.dma_start(z[q * 2 * cz:(q + 1) * 2 * cz, e, :, :].rearrange("p j t -> p (j t)"),
                                 core.z_d[0:2 * cz, ds(columns[q], J * T)]).then_inc(landed[e], 16)
                    for n in range(3):
                        r = 32 * n + q * 2 * J
                        src = core.rstd_d[n:n + 1, :].rearrange("a (h s t) -> s (a h) t", h=2, t=T)
                        sp.dma_start(parts[r:r + 2 * J, e, :], src[ds(tiles[q], J), :, :]).then_inc(landed[e], 16)
                if stored_gate:
                    sp.dma_start(gate[:, e, :, :].rearrange("p j t -> p (j t)"),
                                 core.gate_d[:, ds(columns[0], J * T)]).then_inc(landed[e], 16)
            sp.wait_ge(zeroed, 1)
            each_group(sp.Fori, load)

        @block.tensor
        def _(pe):
            def factor(g, e, j):
                s = g * J + j
                at_least(pe, zn_sb, s - 1)
                pe.matmul(FAC[j % 2][:, :], core.sel[:, SEL[nq] + j, :], parts[:, e, :], start=True,
                          stop=True).then_inc(fac_mm, 1)

            def group(g, e):
                pe.wait_ge(landed[e], 8 * NL * (g - e) + 16 * NL)
                factor(g, e, 0)
                for j in range(J):
                    s = g * J + j
                    if j < J - 1:
                        factor(g, e, j + 1)
                    if layer == 3:
                        pe.wait_ge(zn_sb, s + 1)
                        at_least(pe, cen_sb, s - 1)
                        pe.matmul(GB[j % 2][:, :], w("zc"), zn[:, j % 2, :], start=True, stop=True).then_inc(cen_mm, 1)
                        pe.wait_ge(cen_sb, s + 1)
                        at_least(pe, x_sb, s - 1)
                        pe.matmul(OB[j % 2][:, :], w("wout"), term[:, j % 2, :], start=True, stop=True).then_inc(out_mm, 1)
                        continue
                    for q in range(nq):
                        t = s * nq + q
                        if layer == 0:
                            at_least(pe, gate_sb, t - 1)
                            pe.matmul(GB[q % 2][:, :], w("wgs"), xT[:, ds(tile_at(g, j, q), T)], start=True,
                                      stop=True).then_inc(gate_mm, 1)
                        if q == 0:
                            pe.wait_ge(zn_sb, s + 1)
                        if layer == 1:
                            at_least(pe, gate_sb, t - 1)
                            pe.matmul(GB[q % 2][:, :], w(f"go{q}"), zn[:, j % 2, :], start=True,
                                      stop=True).then_inc(gate_mm, 1)
                        at_least(pe, term_sb, t - 1)
                        pe.matmul(OB[(j * nq + q) % 2][:, :], w(out_w[q]), zn[:, j % 2, :], start=True,
                                  stop=True).then_inc(out_mm, 1)
            each_group(pe.Fori, group)

        if not stored_gate:
            @block.scalar
            def _(act):
                def group(g, e):
                    for j in range(J):
                        for q in range(nq):
                            t = (g * J + j) * nq + q
                            act.wait_ge(gate_mm, t + 1)
                            at_least(act, term_sb, t - 1)
                            nc.scalar.activation(gate[:, 0, q % 2, :], GB[q % 2][:, :], ACT.Sigmoid,
                                                 bias=gate_b).then_inc(gate_sb, 1)
                each_group(act.Fori, group)

        @block.gpsimd
        def _(pool):
            def group(g, e):
                for j in range(J):
                    for q in range(nq):
                        t = (g * J + j) * nq + q
                        x = xT[:, ds(tile_at(g, j, q), T)]
                        pool.wait_ge(term_sb, t + 1)
                        pool.tensor_tensor(x, x, term[:, (j * nq + q) % 2, :], ALU.add).then_inc(x_sb, 1)
            if layer < 3:
                each_group(pool.Fori, group)

        @block.vector
        def _(dve):
            def statistics(t, x):
                dve.wait_ge(x_sb, t + 1)
                dve.bn_stats(core.stats[:, ds(t, 1), :].rearrange("p a s -> p (a s)"), x).then_inc(stat_sb, 1)

            def group(g, e, first=False):
                dve.wait_ge(landed[e], 8 * NL * (g - e) + 16 * NL)
                for j in range(J):
                    s = g * J + j
                    dve.wait_ge(fac_mm, s + 1)
                    at_least(dve, out_mm if layer < 3 else cen_mm, nq * (s - 1))
                    dve.tensor_tensor(zn[:, j % 2, :], FAC[j % 2][:, :], z[:, e, j, :], ALU.mult).then_inc(zn_sb, 1)
                    if layer == 3:
                        dve.wait_ge(cen_mm, s + 1)
                        at_least(dve, out_mm, s - 1)
                        dve.scalar_tensor_tensor(out=term[:, j % 2, :], in0=GB[j % 2][:, :], scalar=vec("out_norm_bias"),
                                                 in1=gate[:, e, j, :], op0=ALU.add, op1=ALU.mult).then_inc(cen_sb, 1)
                        if not (first and g == 0 and j == 0):
                            residual(s - 1, (j - 1) % 2)
                        continue
                    for q in range(nq):
                        t = s * nq + q
                        dve.wait_ge(out_mm, t + 1)
                        if stored_gate:
                            gt = gate[:, e, j, :]
                        else:
                            dve.wait_ge(gate_sb, t + 1)
                            gt = gate[:, 0, q % 2, :]
                        at_least(dve, x_sb, t - 1)
                        dve.scalar_tensor_tensor(out=term[:, (j * nq + q) % 2, :], in0=OB[(j * nq + q) % 2][:, :],
                                                 scalar=out_b, in1=gt, op0=ALU.add, op1=ALU.mult).then_inc(term_sb, 1)
                        if not (first and g == 0 and j == 0 and q == 0):
                            pj, pq = (j, q - 1) if q else (j - 1, nq - 1)
                            at = tile_at(g, pj, pq) if pj >= 0 else tile_at(g - 1, J - 1, pq)
                            statistics(t - 1, xT[:, ds(at, T)])

            def residual(s, b):
                x = xT[:, ds(s * T, T)]
                dve.wait_ge(out_mm, s + 1)
                dve.scalar_tensor_tensor(out=x, in0=OB[b][:, :], scalar=out_b, in1=x, op0=ALU.add,
                                         op1=ALU.add).then_inc(x_sb, 1)

            dve.memset(parts, 0.0).then_inc(zeroed, 1)
            for e in range(2):
                group(e, e, first=True)
            with dve.Fori(1, groups // 2) as i:
                for e in range(2):
                    group(2 * i + e, e)
            if layer == 3:
                residual(NT - 1, (J - 1) % 2)
            else:
                statistics(NT - 1, xT[:, ds(tile_at(groups - 1, J - 1, nq - 1), T)])


def leave(core):
    nc, bank = core.nc, core.bank
    KC = 8
    dst = core.out.rearrange("a (h p) (n k) c -> (a n) p h k c", h=2, k=KC)
    stores = N // KC
    res = [core.area([2, KC, C], b * 2 * KC * C)[0] for b in range(2)]
    xT = core.xT[:, :].rearrange("q (p k) -> q p k", k=N)
    with ExitStack() as ctx:
        turned, kept_a, kept_v = core.sems("leave", "turned kept_a kept_v")
        stored = core.sems("leave", "st0 st1")
        kept = [kept_a, kept_v]
        block = ctx.enter_context(nc.Block())

        @block.tensor
        def _(pe):
            def turn(n, b):
                for half in range(2):
                    at_least(pe, kept[half], n)
                    for k in range(4):
                        mm = pe.transpose(bank[half][:, k * P:(k + 1) * P], xT[:, :, n * KC + 4 * half + k],
                                          core.ident[:, :])
                    mm.then_inc(turned, 1)
            for n in range(stores):
                turn(n, n % 2)

        def keep(half, eng, copy):
            def body(n, b):
                eng.wait_ge(turned, 2 * n + half + 1)
                at_least(eng, stored[b], 16 * (n - b))
                copy(res[b][:, :, 4 * half:4 * half + 4, :],
                     bank[half][:, :].rearrange("p (k h c) -> p h k c", k=4, h=2)).then_inc(kept[half], 1)
            for b in range(2):
                body(b, b)
            with eng.Fori(1, stores // 2) as i:
                for b in range(2):
                    body(2 * i + b, b)

        @block.scalar
        def _(act):
            keep(0, act, nc.scalar.copy)

        @block.vector
        def _(dve):
            keep(1, dve, nc.vector.tensor_copy)

        @block.sync
        def _(sp):
            with sp.Fori(0, stores // 2) as i:
                for b in range(2):
                    at = known(sp, 2 * i + b)
                    for s in kept:
                        sp.wait_ge(s, 2 * i + b + 1)
                    for h in range(2):
                        sp.dma_start(dst[ds(at, 1), :, h, :, :].rearrange("a p k c -> p (a k) c"),
                                     res[b][:, h, :, :]).then_inc(stored[b], 16)
            for s in stored:
                sp.wait_ge(s, 16 * stores)


def build(nc, ins, out):
    with ExitStack() as ctx:
        core = Core(nc, ctx, ins, out)
        sums = [core.area([2 * N], n * 2 * N)[0] for n in range(3)]
        mask, _ = core.area([2, N], 3 * 2 * N)
        rows = lambda first, n: core.hid_d[first:first + n, 0:HALF]
        load_weights(core)
        enter(core)

        b12, bg, _ = fold_group_norm(core, 0)
        project0(core, b12)
        mix(core, 0, 0, 16, (rows(0, 64), rows(0, 64)), (0, 16), (True, False), 0, 16, None, sums)
        fold_sums(core, 0, 16, sums)
        finish(core, 0, 4, bg)

        _, _, ub = fold_group_norm(core, 1)
        project(core, 1, ["gi"], ["pi"], ub)
        make_mask(core, 1, mask)
        mix(core, 1, 0, 16, (rows(0, P), rows(0, P)), (0, 16), (True, True), 0, 32, mask, sums)
        mix(core, 1, 1, 16, (rows(0, P), rows(0, P)), (32, 48), (False, False), 16, 32, mask, sums)
        fold_sums(core, 1, 32, sums)
        finish(core, 1, 2, None)

        _, _, ub = fold_group_norm(core, 2)
        project(core, 2, ["gl", "gate", "gr"], ["pl", "pr"], ub)
        mix(core, 2, 0, 64, (rows(0, P), rows(P, P)), (0, 0), (True, True), 0, 64, None, sums)
        fold_sums(core, 2, 64, sums)
        finish(core, 2, 1, None)

        _, _, ub = fold_group_norm(core, 3)
        project(core, 3, ["lg", "og", "rg"], ["left", "right"], ub)
        make_mask(core, 3, mask)
        mix(core, 3, 0, 64, (rows(0, P), rows(P, P)), (0, 0), (False, False), 0, 64, mask, sums)
        fold_sums(core, 3, 64, sums)
        finish(core, 3, 1, None)
        leave(core)


def kernel(**inputs):
    import concourse.bacc as bacc
    from concourse.bass_utils import run_bass_kernel_spmd

    nc = bacc.Bacc("TRN2", target_bir_lowering=False, num_devices=1)
    arrays, ins = {}, {}
    for name, a in {**inputs, "constants": constants()}.items():
        a = np.ascontiguousarray(a)
        arrays[f"in_{name}"] = a
        ins[name] = nc.dram_tensor(f"in_{name}", a.shape, mybir.dt.from_np(a.dtype), kind="ExternalInput").ap()
    out = nc.dram_tensor("out", (1, N, N, C), F32, kind="ExternalOutput").ap()
    build(nc, ins, out)
    r = run_bass_kernel_spmd(nc, [arrays], core_ids=[0])
    return r.results[0]["out"]
```

```python
from contextlib import ExitStack

import numpy as np

import concourse.bass as bass
from concourse import mybir

F32 = mybir.dt.float32
BF16 = mybir.dt.bfloat16
F32R = mybir.dt.float32r
ALU = mybir.AluOpType
ACT = mybir.ActivationFunctionType
ds = bass.ds

P = 128
N = 256
C = 64
HALF = N * N // 2
T = 512
NT = HALF // T
JP = 8
SETS = {1: 4, 2: 4, 4: 2}
PITCH = HALF + 1024

K_ID, K_C64, K_C32, K_C16, K_GRP, K_SUM, K_EPS5, K_EPS6, K_POW, K_SEL = (
    0, 128, 256, 384, 512, 640, 686, 687, 688, 689)
NSEL = JP + sum(SETS.values())
K_ALL = K_SEL + NSEL * P
SEL = {"project": 0, 1: JP, 2: JP + SETS[1], 4: JP + SETS[1] + SETS[2]}


def constants():
    k = np.zeros((P, K_ALL), np.float32)
    row = np.arange(P)
    k[:, K_ID:K_ID + P] = np.eye(P)
    for at, n in ((K_C64, 64), (K_C32, 32), (K_C16, 16)):
        k[:, at:at + P] = np.eye(P) - (row[:, None] // n == row[None] // n) / n
    k[:, K_GRP:K_GRP + P] = (row[:, None] % C // 2 == row[None] % C // 2) / 4
    k[row, K_SUM + 2 * (JP - 1) + row // C] = 1 / C
    k[:, K_EPS5], k[:, K_EPS6], k[:, K_POW] = 1e-5, 1e-6, -0.5
    for use, at in SEL.items():
        nq, tiles = (1, JP) if use == "project" else (use, SETS[use])
        cz = C // nq
        for j in range(tiles):
            for part in range(3):
                for q in range(nq):
                    for h in range(2):
                        col = K_SEL + (at + j) * P + q * 2 * cz + h * cz
                        k[part * 32 + q * 2 * tiles + 2 * j + h, col:col + cz] = 1
    return k


def known(eng, value):
    return value if isinstance(value, int) else eng.snap(value)


def at_least(eng, sem, value):
    if not isinstance(value, int) or value > 0:
        eng.wait_ge(sem, value)


class Steps:

    def __init__(self, sem):
        self.sem, self.n = sem, 0

    def done(self, instruction):
        instruction.then_inc(self.sem, 1)
        self.n += 1

    def wait(self, eng):
        at_least(eng, self.sem, self.n)


RAW = (["w12", "wg"] + [f"wz{q}" for q in range(4)]
       + ["gi", "pi", "po0", "po1", "go0", "go1"]
       + ["gl", "gr", "gate", "pl", "pr", "pout"]
       + ["lg", "rg", "og", "left", "right", "wout"])
WEIGHTS = RAW + ["zc"]
SLOT = {name: n for n, name in enumerate(WEIGHTS)}
SLOT["center"] = SLOT["w12"]
VECTORS = ["b12", "bg", "bz", "ln2_g", "ln2_b",
           "pi_b", "gi_b", "po_b", "go_b", "ni_w", "ni_b", "no_w", "no_b",
           "norm_in_w", "norm_in_b", "norm_out_w", "norm_out_b",
           "norm_scale", "norm_bias", "b_left", "b_right", "b_lgate", "b_rgate", "b_ogate",
           "out_norm_scale", "out_norm_bias", "b_out"]
VEC = {name: n for n, name in enumerate(VECTORS)}
FOLDS = [([f"wz{q}" for q in range(4)], ["bz"] * 4, "ln2_g", "ln2_b", K_C16),
         (["gi", "pi"], ["gi_b", "pi_b"], "ni_w", "ni_b", K_C64),
         (["po0", "po1", "go0", "go1"], ["po_b", "po_b", "go_b", "go_b"], "no_w", "no_b", K_C32),
         (["gl", "gr", "gate", "pl", "pr"], [None] * 5, "norm_in_w", "norm_in_b", K_C64),
         (["pout"], [None], "norm_out_w", "norm_out_b", K_C64),
         (["lg", "rg", "og", "left", "right"], ["b_lgate", "b_rgate", "b_ogate", "b_left", "b_right"],
          "norm_scale", "norm_bias", K_C64)]
FOLDED = [(name, b, f[3]) for f in FOLDS for name, b in zip(f[0], f[1])]
BIAS = {name: n for n, (name, _, _) in enumerate(FOLDED)}
PROJECTIONS = {1: ["gi", "pi"], 2: ["gl", "gr", "gate", "pl", "pr"], 3: ["lg", "rg", "og", "left", "right"]}


class Core:

    def __init__(self, nc, ctx, ins, out):
        self.nc, self.ins, self.out = nc, ins, out
        self.spent = []

        def sb(name, shape, dt=F32):
            return ctx.enter_context(nc.sbuf_tensor(name, shape, dt))

        self.xT = sb("xT", [P, HALF])
        self.w = sb("w", [P, len(WEIGHTS), P])
        self.ident = sb("ident", [P, P])
        self.c64 = sb("c64", [P, P])
        self.grp = sb("grp", [P, P])
        self.summer = sb("summer", [P, 2 * (JP - 1) + 32])
        self.cols = sb("cols", [P, 3])
        self.sel = sb("sel", [P, NSEL, P], BF16)
        self.vec = sb("vec", [P, len(VECTORS)])
        self.bias = sb("bias", [P, len(FOLDED)])
        self.stats = sb("stats", [P, NT, 6])
        self.fold = sb("fold", [P, 16])
        self.w_hi = sb("w_hi", [P, 5, P], F32R)
        self.w_lo = sb("w_lo", [P, 5, P], F32R)
        self.h_hi = sb("h_hi", [P, 2, T], F32R)
        self.h_lo = sb("h_lo", [P, 2, T], F32R)
        self.work = sb("work", [P, 11776])
        self.bank = [ctx.enter_context(nc.psum_tensor(f"bank{n}", [P, T], F32)) for n in range(8)]

        self.hid_d = nc.dram_tensor("hidden_rows", (2 * P, PITCH), F32).ap()
        self.z_d = nc.dram_tensor("z_rows", (P, PITCH), F32).ap()
        self.gate_d = nc.dram_tensor("gate_rows", (P, PITCH), F32).ap()
        self.rstd_d = nc.dram_tensor("rstd_parts", (3, 2 * HALF), BF16).ap()

    def area(self, shape, at, dt=F32):
        n = int(np.prod(shape))
        words = n if dt == F32 else (n + 1) // 2
        ap = self.work[:, at:at + words]
        if dt != F32:
            ap = ap.bitcast(dt)
        if len(shape) == 2:
            ap = ap.rearrange("p (a b) -> p a b", a=shape[0])
        if len(shape) == 3:
            ap = ap.rearrange("p (a b c) -> p a b c", a=shape[0], b=shape[1])
        assert at + words <= self.work.shape[1], (shape, at)
        return ap, at + words

    def sems(self, phase, names):
        if not self.spent or self.spent[-1][0] != phase:
            if len(self.spent) >= 2:
                for s in self.spent[-2][1]:
                    self.nc.gpsimd.sem_clear(s)
            if len(self.spent) >= 3:
                for s in self.spent[-3][1]:
                    self.nc.release_semaphore(s)
            self.spent.append((phase, []))
        found = [self.nc.alloc_semaphore(f"{phase}_{n}") for n in names.split()]
        self.spent[-1][1].extend(found)
        return found


def weight_layout(ins):
    w = np.zeros((P, len(RAW), P), np.float32)

    def put(name, r, c, block):
        w[r:r + block.shape[0], SLOT[name], c:c + block.shape[1]] = block
    for h in range(2):
        for s in range(2):
            for k, ab in enumerate("ab"):
                put("w12", h * C, s * 64 + h * 32 + k * 16, ins[f"L0_conv_W{ab}{s + 1}"])
        put("wg", h * C, h * C, ins["L0_conv_Wg"])
        for q in range(4):
            put(f"wz{q}", q * 32 + h * 16, h * C, ins["L0_conv_Wz"])
        for name in ("gi", "pi"):
            put(name, h * C, h * C, ins[f"L1_conv_{name}_w"].T)
        for name in ("po", "go"):
            for q in range(2):
                put(f"{name}{q}", q * 64 + h * 32, h * C, ins[f"L1_conv_{name}_w"].T)
        for name, raw, at in (("gl", "g_in_w", 0), ("gr", "g_in_w", C), ("pl", "p_in_w", 0), ("pr", "p_in_w", C),
                              ("gate", "g_out_w", 0), ("pout", "p_out_w", 0)):
            put(name, h * C, h * C, ins[f"L2_conv_{raw}"][at:at + C, :].T)
        for name, raw in (("lg", "lgate"), ("rg", "rgate"), ("og", "ogate"), ("left", "left"), ("right", "right"),
                          ("wout", "out")):
            put(name, h * C, h * C, ins[f"L3_conv_W_{raw}"])
    return w


def vector_layout(ins):
    v = np.zeros((P, len(VECTORS)), np.float32)
    for s in range(2):
        for h in range(2):
            for k, ab in enumerate("ab"):
                v[s * 64 + h * 32 + k * 16:s * 64 + h * 32 + k * 16 + 16, VEC["b12"]] = ins[f"L0_conv_b{ab}{s + 1}"]
    layer = {**dict.fromkeys(VECTORS[1:5], "L0"), **dict.fromkeys(VECTORS[5:13], "L1"),
             **dict.fromkeys(VECTORS[13:17], "L2"), **dict.fromkeys(VECTORS[17:], "L3")}
    for name, l in layer.items():
        raw = ins[f"{l}_conv_{name}"]
        v[:, VEC[name]] = np.tile(raw, P // raw.shape[0])
    return v


def load_weights(core):
    nc, ins, bank = core.nc, core.ins, core.bank
    consts, at = core.area([K_ALL], 0)
    zc_t, at = core.area([P], at)
    w = lambda name: core.w[:, SLOT[name], :]
    col = lambda name: core.vec[:, VEC[name]:VEC[name] + 1]

    def columns(names, first=0, last=None):
        at = SLOT[names[0]]
        return core.w[:, at + first:at + (last or len(names)), :].rearrange("p n m -> p (n m)")
    cuts = [(n, a, min(a + 4, len(f[0]))) for n, f in enumerate(FOLDS) for a in range(0, len(f[0]), 4)]

    with ExitStack() as ctx:
        landed, placed, zc_made, bias_mm, bias_sb, turned, scaled, centred, kept = core.sems(
            "prep", "landed placed zc_made bias_mm bias_sb turned scaled centred kept")
        block = ctx.enter_context(nc.Block())

        @block.sync
        def _(sp):
            sp.dma_start(core.w[:, 0:len(RAW), :], ins["weights"]).then_inc(landed, 16)
            sp.dma_start(core.vec[:, :], ins["vectors"]).then_inc(landed, 16)

        @block.tensor
        def _(pe):
            pe.wait_ge(landed, 48)
            for n, (name, _, shift) in enumerate(FOLDED):
                mm = pe.matmul(bank[0][:, n:n + 1], w(name), col(shift), start=True, stop=True)
            mm.then_inc(bias_mm, 1)
            pe.wait_ge(zc_made, 1)
            pe.transpose(bank[1][:, 0:P], zc_t, consts[:, K_ID:K_ID + P]).then_inc(turned, 1)
            for n, (f, first, last) in enumerate(cuts):
                names, centre = FOLDS[f][0], FOLDS[f][4]
                pe.wait_ge(scaled, f + 1)
                at_least(pe, kept, n - 3)
                pe.matmul(bank[2 + n % 4][:, 0:(last - first) * P], consts[:, centre:centre + P],
                          columns(names, first, last), start=True, stop=True).then_inc(centred, 1)

        @block.vector
        def _(dve):
            dve.wait_ge(landed, 48)
            dve.tensor_scalar(zc_t, consts[:, K_C64:K_C64 + P], col("out_norm_scale"), None,
                              ALU.mult).then_inc(zc_made, 1)
            dve.wait_ge(bias_mm, 1)
            for names, _, scale, _, _ in FOLDS:
                dve.tensor_scalar(columns(names), columns(names), col(scale), None, ALU.mult).then_inc(scaled, 1)
            for n, (name, b, _) in enumerate(FOLDED):
                if b:
                    ins_ = dve.tensor_tensor(core.bias[:, n:n + 1], bank[0][:, n:n + 1], col(b), ALU.add)
                else:
                    ins_ = dve.tensor_copy(core.bias[:, n:n + 1], bank[0][:, n:n + 1])
                ins_.then_inc(bias_sb, 1)
            dve.wait_ge(turned, 1)
            dve.tensor_copy(w("zc"), bank[1][:, 0:P]).then_inc(placed, 1)

        @block.scalar
        def _(act):
            act.dma_start(consts, ins["constants"]).then_inc(landed, 16)
            act.wait_ge(landed, 48)
            for dst, at, n in ((core.ident, K_ID, P), (core.c64, K_C64, P), (core.grp, K_GRP, P),
                               (core.summer, K_SUM, 2 * (JP - 1) + 32), (core.cols, K_EPS5, 3)):
                nc.scalar.copy(dst[:, :], consts[:, at:at + n]).then_inc(placed, 1)
            for n, (f, first, last) in enumerate(cuts):
                act.wait_ge(centred, n + 1)
                nc.scalar.copy(columns(FOLDS[f][0], first, last), bank[2 + n % 4][:, 0:(last - first) * P]
                               ).then_inc(kept, 1)

        @block.gpsimd
        def _(pool):
            pool.wait_ge(landed, 48)
            pool.tensor_copy(core.sel[:, :, :].rearrange("p a b -> p (a b)"), consts[:, K_SEL:K_ALL]).then_inc(placed, 1)


def enter(core):
    nc, bank = core.nc, core.bank
    KC = 8
    x = core.ins["x"].rearrange("a (h p) (n k) c -> (a n) p h k c", h=2, k=KC)
    loads = N // KC
    xin = [core.area([2, KC, C], b * 2 * KC * C)[0] for b in range(2)]
    xpix = [core.area([KC, 2, C], (2 + b) * 2 * KC * C)[0] for b in range(2)]
    xT = core.xT[:, :].rearrange("q (p k) -> q p k", k=N)
    with ExitStack() as ctx:
        in0, in1, paired, turned, kept, counted = core.sems("enter", "in0 in1 paired turned kept counted")
        landed = [in0, in1]
        block = ctx.enter_context(nc.Block())

        @block.sync
        def _(sp):
            def load(n, b):
                n_at = known(sp, n)
                at_least(sp, paired, n - 1)
                for h in range(2):
                    sp.dma_start(xin[b][:, h, :, :], x[ds(n_at, 1), :, h, :, :].rearrange("a p k c -> p (a k) c")
                                 ).then_inc(landed[b], 16)
            for b in range(2):
                load(b, b)
            with sp.Fori(1, loads // 2) as i:
                for b in range(2):
                    load(2 * i + b, b)

        @block.tensor
        def _(pe):
            def turn(n, b):
                pe.wait_ge(paired, n + 1)
                for half in range(2):
                    at_least(pe, kept, 2 * n + half - 1)
                    at_least(pe, counted, 2 * n + half - 1)
                    for k in range(4):
                        mm = pe.transpose(bank[half][:, k * P:(k + 1) * P], xpix[b][:, 4 * half + k, :, :].rearrange("p h c -> p (h c)"), core.ident[:, :])
                    mm.then_inc(turned, 1)
            for b in range(2):
                turn(b, b)
            with pe.Fori(1, loads // 2) as i:
                for b in range(2):
                    turn(2 * i + b, b)

        @block.scalar
        def _(act):
            with act.Fori(0, loads // 2) as i:
                for b in range(4):
                    act.wait_ge(turned, 4 * i + b + 1)
                    act.wait_ge(counted, 4 * i + b + 1)
                    nc.scalar.copy(xT[:, :, ds((4 * i + b) * 4, 4)],
                                   bank[b % 2][:, :].rearrange("q (k p) -> q p k", p=P)).then_inc(kept, 1)

        @block.vector
        def _(dve):
            def load(n, b):
                dve.wait_ge(landed[b], (n - b) * 16 + 32)
                at_least(dve, turned, 2 * n - 2)
                dve.tensor_copy(xpix[b].rearrange("p k h c -> p h k c"), xin[b]).then_inc(paired, 1)
                for half in range(2):
                    dve.wait_ge(turned, 2 * n + half + 1)
                    dve.bn_stats(core.stats[:, ds(2 * n + half, 1), :].rearrange("p a s -> p (a s)"),
                                 bank[half][:, :]).then_inc(counted, 1)
            for b in range(2):
                load(b, b)
            with dve.Fori(1, loads // 2) as i:
                for b in range(2):
                    load(2 * i + b, b)


def fold_group_norm(core, layer):
    nc, bank = core.nc, core.bank
    f = core.fold
    mean_var, gmean, dev, spread, gvar, r, b = (f[:, 0:2], f[:, 2:3], f[:, 3:4], f[:, 4:5], f[:, 5:6], f[:, 6:7], f[:, 7:8])
    b12, bg, ub = f[:, 8:9], f[:, 9:10], f[:, 10:11]
    w = lambda name: core.w[:, SLOT[name], :]
    with ExitStack() as ctx:
        dve_s, pe_s, pow_s = core.sems(f"fold{layer}", "dve pe pow")
        block = ctx.enter_context(nc.Block())

        @block.vector
        def _(dve):
            step = Steps(dve_s)
            step.done(dve.bn_aggr(mean_var, core.stats[:, :, :].rearrange("p n s -> p (n s)")))
            dve.wait_ge(pe_s, 1)
            step.done(dve.tensor_copy(gmean, bank[0][:, 0:1]))
            step.wait(dve)
            step.done(dve.tensor_tensor(dev, mean_var[:, 0:1], gmean, ALU.subtract))
            step.wait(dve)
            step.done(dve.scalar_tensor_tensor(out=spread, in0=dev, scalar=dev, in1=mean_var[:, 1:2],
                                               op0=ALU.mult, op1=ALU.add))
            dve.wait_ge(pe_s, 2)
            step.done(dve.tensor_scalar(gvar, bank[1][:, 0:1], core.cols[:, 0:1], None, ALU.add))
            dve.wait_ge(pow_s, 1)
            step.done(dve.scalar_tensor_tensor(out=b, in0=gmean, scalar=-1.0, in1=r, op0=ALU.mult, op1=ALU.mult))
            if layer == 0:
                dve.wait_ge(pe_s, 4)
                step.done(dve.tensor_scalar(w("w12"), w("w12"), r, None, ALU.mult))
                step.done(dve.tensor_scalar(w("wg"), w("wg"), r, None, ALU.mult))
                step.done(dve.tensor_tensor(b12, bank[2][:, 0:1], core.vec[:, VEC["b12"]:VEC["b12"] + 1], ALU.add))
                step.done(dve.tensor_tensor(bg, bank[3][:, 0:1], core.vec[:, VEC["bg"]:VEC["bg"] + 1], ALU.add))
            else:
                step.done(dve.tensor_scalar(w("center"), core.c64[:, :], r, None, ALU.mult))
                dve.wait_ge(pe_s, 3)
                step.done(dve.tensor_copy(ub, bank[2][:, 0:1]))
                names = PROJECTIONS[layer]
                raw = core.w[:, SLOT[names[0]]:SLOT[names[0]] + len(names), :]
                hi, lo = core.w_hi[:, 0:len(names), :], core.w_lo[:, 0:len(names), :]
                step.done(dve.tensor_scalar(hi, raw, r, None, ALU.mult))
                step.wait(dve)
                step.done(dve.scalar_tensor_tensor(out=lo, in0=raw, scalar=r, in1=hi.bitcast(F32), op0=ALU.mult,
                                                   op1=ALU.subtract))

        @block.gpsimd
        def _(pool):
            pool.wait_ge(dve_s, 5)
            pool.tensor_tensor(r, gvar, core.cols[:, 2:3], ALU.pow).then_inc(pow_s, 1)

        @block.tensor
        def _(pe):
            pe.wait_ge(dve_s, 1)
            pe.matmul(bank[0][:, 0:1], core.grp[:, :], mean_var[:, 0:1], start=True, stop=True).then_inc(pe_s, 1)
            pe.wait_ge(dve_s, 4)
            pe.matmul(bank[1][:, 0:1], core.grp[:, :], spread, start=True, stop=True).then_inc(pe_s, 1)
            pe.wait_ge(dve_s, 6)
            if layer == 0:
                pe.matmul(bank[2][:, 0:1], w("w12"), b, start=True, stop=True).then_inc(pe_s, 1)
                pe.matmul(bank[3][:, 0:1], w("wg"), b, start=True, stop=True).then_inc(pe_s, 1)
            else:
                pe.matmul(bank[2][:, 0:1], core.c64[:, :], b, start=True, stop=True).then_inc(pe_s, 1)
    return b12, bg, ub, gmean


def project0(core, b12):
    nc, bank, xT = core.nc, core.bank, core.xT
    first, at = core.area([2, T], 0)
    prod, at = core.area([2, T], at)
    hid, at = core.area([2, T], at)
    wst = core.w[:, SLOT["w12"], :]
    dst = core.hid_d[0:64, 0:HALF].rearrange("q (n s t) -> n q s t", s=4, t=T)
    with ExitStack() as ctx:
        mm, one, two, act_s, st0, st1 = core.sems("proj0", "mm one two act st0 st1")
        stored = [st0, st1]
        block = ctx.enter_context(nc.Block())

        @block.tensor
        def _(pe):
            def tile(t, b):
                at_least(pe, one, t - 1)
                at_least(pe, two, t - 1)
                pe.matmul(bank[b % 2][:, :], wst, xT[:, ds(t * T, T)], start=True, stop=True).then_inc(mm, 1)
            for b in range(4):
                tile(b, b)
            with pe.Fori(1, NT // 4) as i:
                for b in range(4):
                    tile(4 * i + b, b)

        @block.scalar
        def _(act):
            def pair(t, b):
                for k in range(2):
                    act.wait_ge(mm, t + k + 1)
                    at_least(act, two, t + k - 1)
                    nc.scalar.activation(first[0:64, k, :], bank[k][0:64, :], ACT.Identity,
                                         bias=b12[0:64, :]).then_inc(one, 1)
                act.wait_ge(two, t + 2)
                at_least(act, stored[b], 8 * (t - 2 * b))
                nc.scalar.activation(hid[:, b, :], prod[:, b, :], ACT.Sigmoid).then_inc(act_s, 1)
            for b in range(2):
                pair(2 * b, b)
            with act.Fori(1, NT // 4) as i:
                for b in range(2):
                    pair(4 * i + 2 * b, b)

        @block.vector
        def _(dve):
            def tile(t, p, b):
                k = b % 2
                dve.wait_ge(one, t + 1)
                at_least(dve, act_s, p - 1)
                dve.scalar_tensor_tensor(out=prod[64 * k:64 * k + 64, b // 2, :], in0=bank[k][64:128, :],
                                         scalar=b12[64:128, :], in1=first[0:64, k, :], op0=ALU.add,
                                         op1=ALU.mult).then_inc(two, 1)
            for b in range(4):
                tile(b, b // 2, b)
            with dve.Fori(1, NT // 4) as i:
                for b in range(4):
                    tile(4 * i + b, 2 * i + b // 2, b)

        @block.sync
        def _(sp):
            with sp.Fori(0, NT // 4) as i:
                for b in range(2):
                    i_at = known(sp, i)
                    sp.wait_ge(act_s, 2 * i + b + 1)
                    for k in range(2):
                        sp.dma_start(dst[ds(i_at, 1), :, 2 * b + k, :].rearrange("a q t -> q (a t)"),
                                     hid[64 * k:64 * k + 64, b, :]).then_inc(stored[b], 16)
            for s in stored:
                sp.wait_ge(s, 32 * (NT // 4))


def project(core, layer, gates, values, ub, gmean):
    nc, bank, xT = core.nc, core.bank, core.xT
    NG, NV = len(gates), len(values)
    AHEAD = JP + 7
    SUMMED = (2 * JP - AHEAD) % JP
    SPLIT = 6
    U, STAT, FAC, GB, VB = [bank[0], bank[1]], bank[2], bank[3], [bank[4], bank[5]], [bank[6], bank[7]]
    sq, at = core.area([2, T], 0)
    h, at = core.area([2, T], at)
    sd, at = core.area([T], at)
    rec, at = core.area([T], at)
    rest, at = core.area([T], at)
    parts, at = core.area([2, T], at, BF16)
    res, at = core.area([4, NG * T], at)
    hi, lo = core.h_hi, core.h_lo
    groups = NT // JP
    eps = core.cols[0:32, 1:2] if layer == 3 else core.cols[0:32, 0:1]
    w = lambda name: core.w[:, SLOT[name], :]
    bias = lambda name: core.bias[:, BIAS[name]:BIAS[name] + 1]
    w_part = {name: (core.w_hi[:, n, :], core.w_lo[:, n, :]) for n, name in enumerate(PROJECTIONS[layer])}
    of_gate = {0: 0, NG - 1: NV - 1}
    gate_of = [0, NG - 1][:NV]
    result = lambda j, m: res[:, j % 4, m * T:m * T + T]
    dsts = [core.hid_d[of_gate[m] * P:(of_gate[m] + 1) * P, :] if m in of_gate else core.gate_d for m in range(NG)]

    def slots(loop, body):
        for g in range(2):
            for j in range(JP):
                body(g, g % 2, j)
        with loop(1, groups // 2 - 1) as i:
            for e in range(2):
                for j in range(JP):
                    body(2 * i + e, e, j)
        for g in range(groups - 2, groups):
            for j in range(JP):
                body(g, g % 2, j)

    def within(t, n=NT):
        return not isinstance(t, int) or t < n

    with ExitStack() as ctx:
        (u_mm, sq_sb, sum_mm, sd_sb, split_s, fac_mm, h_sb, hi_sb, lo_sb, gate_mm, val_mm, gate_sb, val_sb,
         zeroed) = core.sems(f"proj{layer}", "u_mm sq_sb sum_mm sd_sb split fac_mm h_sb hi_sb lo_sb gate_mm val_mm "
                             "gate_sb val_sb zeroed")
        stored = core.sems(f"proj{layer}", "st0 st1 st2 st3")
        block = ctx.enter_context(nc.Block())

        @block.tensor
        def _(pe):
            def centre(t, j):
                at_least(pe, sq_sb, t - 1)
                pe.matmul(U[j % 2][:, :], w("center"), xT[:, ds(t * T, T)], start=True, stop=True).then_inc(u_mm, 1)

            def mean_square(t, g, j):
                pe.wait_ge(sq_sb, t + 1)
                if j == 0:
                    at_least(pe, sd_sb, g)
                pe.matmul(STAT[0:32, :], core.summer[:, 2 * (JP - 1 - j):2 * (JP - 1 - j) + 32], sq[:, j % 2, :],
                          start=(j == 0), stop=(j == JP - 1)).then_inc(sum_mm, 1)

            def factor(t, g, e, j):
                if j == 0:
                    pe.wait_ge(split_s, SPLIT * (g + 1))
                at_least(pe, h_sb, t)
                pe.matmul(FAC[:, :], core.sel[:, SEL["project"] + j, :], parts[:, e, :], start=True,
                          stop=True).then_inc(fac_mm, 1)

            def product(out, name, j):
                w_hi, w_lo = w_part[name]
                pe.matmul(out, w_hi, hi[:, j % 2, :], start=True, stop=False)
                pe.matmul(out, w_lo, hi[:, j % 2, :], start=False, stop=False)
                return pe.matmul(out, w_hi, lo[:, j % 2, :], start=False, stop=True)

            def tile(g, e, j):
                t = g * JP + j
                if j < JP - 2:
                    factor(t + 2, g, e, j + 2)
                elif within(g + 1, groups):
                    factor(t + 2, g + 1, 1 - e, j + 2 - JP)
                if within(t + AHEAD):
                    centre(t + AHEAD, j + AHEAD)
                if within(t + AHEAD - 1):
                    mean_square(t + AHEAD - 1, g + (j + AHEAD - 1) // JP, (j + AHEAD - 1) % JP)
                pe.wait_ge(lo_sb, t + 1)
                for m in range(NG):
                    n = NG * t + m
                    at_least(pe, gate_sb, n - 1)
                    product(GB[(NG * j + m) % 2][:, :], gates[m], j).then_inc(gate_mm, 1)
                    if m in of_gate:
                        v = of_gate[m]
                        at_least(pe, val_sb, NV * t + v - 1)
                        product(VB[(NV * j + v) % 2][:, :], values[v], j).then_inc(val_mm, 1)

            for t in range(AHEAD):
                centre(t, t)
                if t:
                    mean_square(t - 1, (t - 1) // JP, (t - 1) % JP)
            pe.wait_ge(zeroed, 1)
            factor(0, 0, 0, 0)
            factor(1, 0, 0, 1)
            slots(pe.Fori, tile)

        @block.scalar
        def _(act):
            def high(t, j):
                act.wait_ge(h_sb, t + 1)
                at_least(act, val_mm, NV * (t - 1))
                nc.scalar.copy(hi[:, j % 2, :], h[:, j % 2, :]).then_inc(hi_sb, 1)

            def square(t, j):
                act.wait_ge(u_mm, t + 1)
                at_least(act, sum_mm, t - 1)
                nc.scalar.activation(sq[:, j % 2, :], U[j % 2][:, :], ACT.Square, bias=ub).then_inc(sq_sb, 1)

            def root(g):
                act.wait_ge(sum_mm, JP * g + JP)
                at_least(act, split_s, SPLIT * (g - 1) + 2)
                nc.scalar.activation(sd[0:32, :], STAT[0:32, :], ACT.Sqrt, bias=eps).then_inc(sd_sb, 1)

            def tile(g, e, j):
                t = g * JP + j
                if within(t + 1):
                    high(t + 1, j + 1)
                if within(t + AHEAD):
                    square(t + AHEAD, j + AHEAD)
                if j == SUMMED and within(g + 1, groups):
                    root(g + 1)
                for m in range(NG):
                    act.wait_ge(gate_mm, NG * t + m + 1)
                    if m == 0:
                        at_least(act, stored[j % 4], 16 * NG * (2 * g + j // 4))
                    nc.scalar.activation(result(j, m), GB[(NG * j + m) % 2][:, :],
                                         ACT.Sigmoid, bias=bias(gates[m])).then_inc(gate_sb, 1)

            for t in range(AHEAD):
                square(t, t)
                if t == JP:
                    root(0)
            high(0, 0)
            slots(act.Fori, tile)

        @block.gpsimd
        def _(pool):
            def low(t, b):
                pool.wait_ge(hi_sb, t + 1)
                at_least(pool, val_mm, NV * (t - 1))
                pool.tensor_tensor(lo[:, b, :], h[:, b, :], hi[:, b, :].bitcast(F32), ALU.subtract).then_inc(lo_sb, 1)
            for b in range(2):
                low(b, b)
            with pool.Fori(1, NT // 2) as i:
                for b in range(2):
                    low(2 * i + b, b)

        @block.vector
        def _(dve):
            def invert(g, half):
                dve.wait_ge(sd_sb, g + 1)
                k = slice(half * T // 2, (half + 1) * T // 2)
                dve.reciprocal(rec[0:32, k], sd[0:32, k]).then_inc(split_s, 1)

            def split(g, e, part):
                a, b, c = (parts[32 * n:32 * n + 32, e, :] for n in range(3))
                if part == 0:
                    dve.wait_ge(split_s, SPLIT * g + 2)
                    at_least(dve, fac_mm, JP * (g - 1))
                    dve.tensor_copy(a, rec[0:32, :]).then_inc(split_s, 1)
                    dve.wait_ge(split_s, SPLIT * g + 3)
                    dve.tensor_tensor(rest[32:64, :], rec[0:32, :], a, ALU.subtract).then_inc(split_s, 1)
                else:
                    dve.wait_ge(split_s, SPLIT * g + 4)
                    dve.tensor_copy(b, rest[32:64, :]).then_inc(split_s, 1)
                    dve.wait_ge(split_s, SPLIT * g + 5)
                    dve.tensor_tensor(c, rest[32:64, :], b, ALU.subtract).then_inc(split_s, 1)

            def normed(t, j):
                dve.wait_ge(fac_mm, t + 1)
                at_least(dve, lo_sb, t - 1)
                dve.scalar_tensor_tensor(out=h[:, j % 2, :], in0=xT[:, ds(t * T, T)], scalar=gmean,
                                         in1=FAC[:, :], op0=ALU.subtract, op1=ALU.mult).then_inc(h_sb, 1)

            def tile(g, e, j):
                t = g * JP + j
                if within(t + 2):
                    normed(t + 2, j)
                for m in range(NV):
                    dve.wait_ge(val_mm, NV * t + m + 1)
                    dve.wait_ge(gate_sb, NG * t + gate_of[m] + 1)
                    r = result(j, gate_of[m])
                    dve.scalar_tensor_tensor(out=r, in0=VB[(NV * j + m) % 2][:, :], scalar=bias(values[m]),
                                             in1=r, op0=ALU.add, op1=ALU.mult).then_inc(val_sb, 1)
                step = j - SUMMED
                if step in (0, 1) and within(g + 1, groups):
                    invert(g + 1, step)
                if step in (2, 3) and within(g + 1, groups):
                    split(g + 1, 1 - e, step - 2)
            dve.memset(parts, 0.0).then_inc(zeroed, 1)
            dve.wait_ge(zeroed, 1)
            invert(0, 0)
            invert(0, 1)
            split(0, 0, 0)
            split(0, 0, 1)
            normed(0, 0)
            normed(1, 1)
            slots(dve.Fori, tile)

        @block.sync
        def _(sp):
            with sp.Fori(0, NT // 4) as i:
                for k in range(4):
                    at = known(sp, (4 * i + k) * T)
                    sp.wait_ge(val_sb, i * (4 * NV) + NV * (k + 1))
                    for m in range(NG):
                        sp.dma_start(dsts[m][:, ds(at, T)], result(k, m)).then_inc(stored[k], 16)
            for s in stored:
                sp.wait_ge(s, 16 * NG * (NT // 4))


def make_mask(core, layer, mask):
    nc = core.nc
    with ExitStack() as ctx:
        landed, rep, made = core.sems(f"mask{layer}", "landed rep made")
        block = ctx.enter_context(nc.Block())
        if layer == 1:
            @block.sync
            def _(sp):
                sp.dma_start(mask, core.ins["L1_conv_mask"].rearrange("a (h p) k -> p (a h) k", h=2)).then_inc(landed, 16)
                sp.wait_ge(landed, 16)
            return
        m = core.ins["L3_conv_src_mask"]
        m2, at = core.area([P], 6000)
        m1, at = core.area([N], at)
        ones, at = core.area([P], at)
        mcol = core.fold[:, 12:14]

        @block.sync
        def _(sp):
            sp.dma_start(m2[0:2, :], m.rearrange("a (h p) -> (a h) p", h=2)).then_inc(landed, 16)
            sp.dma_start(m1[0:1, :], m).then_inc(landed, 16)

        @block.tensor
        def _(pe):
            pe.wait_ge(landed, 32)
            pe.transpose(core.bank[0][:, 0:2], m2[0:2, :], core.ident[0:2, 0:2]).then_inc(rep, 1)
            pe.wait_ge(made, 1)
            pe.matmul(core.bank[1][:, 0:N], ones[0:1, :], m1[0:1, :], start=True, stop=True).then_inc(rep, 1)

        @block.vector
        def _(dve):
            dve.memset(ones[0:1, :], 1.0).then_inc(made, 1)
            dve.wait_ge(rep, 1)
            dve.tensor_copy(mcol, core.bank[0][:, 0:2]).then_inc(made, 1)
            dve.wait_ge(rep, 2)
            dve.wait_ge(made, 2)
            for k in range(2):
                dve.tensor_scalar(mask[:, k, :], core.bank[1][:, 0:N], mcol[:, k:k + 1], None,
                                  ALU.mult).then_inc(made, 1)


def mix(core, layer, part, channels, rows, offsets, turns, z_row, cz, mask, sums):
    nc, bank = core.nc, core.bank
    z0, s1, s2 = sums
    at = 4 * 2 * N
    ab, at = core.area([8, 2 * N], at)
    tt, at = core.area([4, 2 * N], at)
    zs, at = core.area([2, 2 * N], at)
    dev, at = core.area([4, 2 * N], at)
    src = [r.rearrange("(h m) (p k) -> m p h k", h=2, k=N) for r in rows]
    zdst = core.z_d[0:2 * cz, 0:HALF].rearrange("(h m) (p k) -> m p h k", h=2, k=N)
    turn_a, turn_b = turns
    nturn = turn_a + turn_b
    TB = [[bank[0], bank[1]], [bank[2], bank[3]]]
    ZB = [bank[4], bank[5]]

    with ExitStack() as ctx:
        (masked_a, masked_b, turn_mm, ta_sb, tb_sb, z_mm, z_sb, dev_sb, sq_sb, s1_sb, s2_sb, begun,
         s2_zero) = core.sems(f"mix{layer}{part}", "masked_a masked_b turn_mm ta_sb tb_sb z_mm z_sb dev_sb sq_sb "
                              "s1_sb s2_sb begun s2_zero")
        landed = core.sems(f"mix{layer}{part}", "in0 in1 in2 in3")
        stored = core.sems(f"mix{layer}{part}", "st0 st1")
        masked_s, t_sb = (masked_a, masked_b), (ta_sb, tb_sb)
        block = ctx.enter_context(nc.Block())

        def each_channel(loop, body):
            for b in range(4):
                body(b, b)
            with loop(1, channels // 4 - 1) as i:
                for b in range(4):
                    body(4 * i + b, b)
            for b in range(4):
                body(channels - 4 + b, b)

        def exists(c):
            return not isinstance(c, int) or 0 <= c < channels

        def loaded(o, b):
            return ab[:, 2 * b + o, :]

        def operand(o, b):
            buf = tt[:, 2 * o + b % 2, :] if turns[o] else loaded(o, b)
            return buf.rearrange("p (h k) -> p h k", h=2)

        @block.sync
        def _(sp):
            def load(c, b):
                at = [known(sp, c + offset) for offset in offsets]
                if nturn == 2:
                    at_least(sp, turn_mm, 2 * (c - 3))
                else:
                    at_least(sp, z_mm, c - 3)
                for o in range(2):
                    sp.dma_start(loaded(o, b).rearrange("p (h k) -> p h k", h=2),
                                 src[o][ds(at[o], 1)].rearrange("m p h k -> p (m h) k")).then_inc(landed[b], 16)
            each_channel(sp.Fori, load)
            for s in stored:
                sp.wait_ge(s, 8 * channels)

        @block.tensor
        def _(pe):
            def ready(c, b, o):
                if mask is not None:
                    pe.wait_ge(masked_s[o], c + 1)
                else:
                    pe.wait_ge(landed[b], (c - b) * 8 + 32)

            def turn(c, b):
                for o in range(2):
                    if turns[o]:
                        ready(c, b, o)
                        at_least(pe, t_sb[o], c - 1)
                        x = loaded(o, b).rearrange("p (h k) -> p h k", h=2)
                        for kk in range(2):
                            for r in range(2):
                                mm = pe.transpose(TB[o][b % 2][:, kk * N + r * P:kk * N + r * P + P],
                                                  x[:, r, kk * P:kk * P + P], core.ident[:, :])
                        mm.then_inc(turn_mm, 1)

            def product(c, b):
                for o in range(2):
                    if turns[o]:
                        pe.wait_ge(t_sb[o], c + 1)
                    else:
                        ready(c, b, o)
                at_least(pe, z_sb, c - 1)
                a, x = operand(0, b), operand(1, b)
                for r in range(2):
                    for kk in range(2):
                        mm = pe.matmul(ZB[b % 2][:, r * N:r * N + N], a[:, kk, r * P:r * P + P], x[:, kk, :],
                                       start=(kk == 0), stop=(kk == 1))
                mm.then_inc(z_mm, 1)

            def channel(c, b):
                turn(c, b)
                if exists(c - 1):
                    product(c - 1, (b - 1) % 4)

            each_channel(pe.Fori, channel)
            product(channels - 1, 3)

        @block.scalar
        def _(act):
            def turned(c, b):
                if turns[0]:
                    act.wait_ge(turn_mm, nturn * c + 1)
                    at_least(act, z_mm, c - 1)
                    nc.scalar.copy(tt[:, b % 2, :], TB[0][b % 2][:, :]).then_inc(ta_sb, 1)

            def out(c, b):
                act.wait_ge(z_mm, c + 1)
                at_least(act, stored[b % 2], 8 * (c - b % 2))
                at_least(act, dev_sb, c - 1)
                nc.scalar.copy(zs[:, b % 2, :], ZB[b % 2][:, :]).then_inc(z_sb, 1)

            def square(c, b):
                act.wait_ge(s1_sb, c + 1)
                nc.scalar.activation(dev[:, b, :], dev[:, b, :], ACT.Square).then_inc(sq_sb, 1)

            def store(c, b):
                at = known(act, c + z_row)
                act.wait_ge(z_sb, c + 1)
                act.dma_start(zdst[ds(at, 1)].rearrange("m p h k -> p (m h) k"),
                              zs[:, b % 2, :].rearrange("p (h k) -> p h k", h=2)).then_inc(stored[b % 2], 16)

            def channel(c, b):
                turned(c, b)
                if exists(c - 1):
                    out(c - 1, (b - 1) % 4)
                if exists(c - 3):
                    square(c - 3, (b - 3) % 4)
                if exists(c - 1):
                    store(c - 1, (b - 1) % 4)

            each_channel(act.Fori, channel)
            out(channels - 1, 3)
            store(channels - 1, 3)
            for b in range(1, 4):
                square(channels - 4 + b, b)

        @block.vector
        def _(dve):
            def mask_b(c, b):
                if mask is not None:
                    dve.wait_ge(landed[b], (c - b) * 8 + 32)
                    dve.tensor_tensor(loaded(1, b), loaded(1, b), mask.rearrange("p h k -> p (h k)"),
                                      ALU.mult).then_inc(masked_b, 1)

            def turned(c, b):
                if turns[1]:
                    dve.wait_ge(turn_mm, nturn * c + nturn)
                    at_least(dve, z_mm, c - 1)
                    dve.tensor_copy(tt[:, 2 + b % 2, :], TB[1][b % 2][:, :]).then_inc(tb_sb, 1)

            def deviation(c, b):
                dve.wait_ge(z_sb, c + 1)
                at_least(dve, s2_sb, c - 3)
                if isinstance(c, int) and c == 0 and part == 0:
                    dve.tensor_copy(z0, zs[:, 0, :]).then_inc(begun, 1)
                    dve.memset(s1, 0.0).then_inc(begun, 1)
                    dve.wait_ge(begun, 2)
                dve.tensor_tensor(dev[:, b, :], zs[:, b % 2, :], z0, ALU.subtract).then_inc(dev_sb, 1)
                dve.wait_ge(dev_sb, c + 1)
                at_least(dve, s1_sb, c)
                dve.tensor_tensor(s1, s1, dev[:, b, :], ALU.add).then_inc(s1_sb, 1)

            def channel(c, b):
                if exists(c + 2):
                    mask_b(c + 2, (b + 2) % 4)
                turned(c, b)
                if exists(c - 1):
                    deviation(c - 1, (b - 1) % 4)

            for b in range(2):
                mask_b(b, b)
            each_channel(dve.Fori, channel)
            deviation(channels - 1, 3)

        @block.gpsimd
        def _(pool):
            def mask_a(c, b):
                if mask is not None:
                    pool.wait_ge(landed[b], (c - b) * 8 + 32)
                    pool.tensor_tensor(loaded(0, b), loaded(0, b), mask.rearrange("p h k -> p (h k)"),
                                       ALU.mult).then_inc(masked_a, 1)

            def squares(c, b):
                pool.wait_ge(sq_sb, c + 1)
                at_least(pool, s2_sb, c)
                pool.tensor_tensor(s2, s2, dev[:, b, :], ALU.add).then_inc(s2_sb, 1)

            def channel(c, b):
                if exists(c + 2):
                    mask_a(c + 2, (b + 2) % 4)
                if exists(c - 3):
                    squares(c - 3, (b - 3) % 4)

            if part == 0:
                pool.memset(s2, 0.0).then_inc(s2_zero, 1)
                pool.wait_ge(s2_zero, 1)
            for b in range(2):
                mask_a(b, b)
            each_channel(pool.Fori, channel)
            for b in range(1, 4):
                squares(channels - 4 + b, b)


def fold_sums(core, layer, cz, sums):
    nc = core.nc
    z0, s1, s2 = sums
    at = 4 * 2 * N
    mean, at = core.area([2 * N], at)
    var, at = core.area([2 * N], at)
    rec, at = core.area([2 * N], at)
    parts, at = core.area([3, 2 * N], at, BF16)
    eps = core.cols[:, 1:2] if layer == 3 else core.cols[:, 0:1]
    with ExitStack() as ctx:
        dve_s, root, stored = core.sems(f"var{layer}", "dve root stored")
        block = ctx.enter_context(nc.Block())

        @block.vector
        def _(dve):
            step = Steps(dve_s)

            def then(ins):
                step.done(ins)
                step.wait(dve)
            then(dve.tensor_scalar(mean, s1, 1.0 / cz, None, ALU.mult))
            then(dve.tensor_tensor(mean, mean, mean, ALU.mult))
            then(dve.scalar_tensor_tensor(out=var, in0=s2, scalar=1.0 / cz, in1=mean, op0=ALU.mult, op1=ALU.subtract))
            then(dve.tensor_scalar(var, var, 0.0, None, ALU.max))
            dve.wait_ge(root, 1)
            then(dve.reciprocal(rec, mean))
            then(dve.tensor_copy(parts[:, 0, :], rec))
            then(dve.tensor_tensor(var, rec, parts[:, 0, :], ALU.subtract))
            then(dve.tensor_copy(parts[:, 1, :], var))
            then(dve.tensor_tensor(parts[:, 2, :], var, parts[:, 1, :], ALU.subtract))

        @block.scalar
        def _(act):
            act.wait_ge(dve_s, 4)
            nc.scalar.activation(mean, var, ACT.Sqrt, bias=eps).then_inc(root, 1)

        @block.sync
        def _(sp):
            sp.wait_ge(dve_s, 9)
            for n in range(3):
                sp.dma_start(core.rstd_d[n:n + 1, :].rearrange("a (h p k) -> p (a h) k", h=2, k=N),
                             parts[:, n, :].rearrange("p (h k) -> p h k", h=2)).then_inc(stored, 16)
            sp.wait_ge(stored, 48)


def finish(core, layer, nq, bg):
    nc, bank, xT = core.nc, core.bank, core.xT
    cz = C // nq
    J = SETS[nq]
    sets = NT // nq
    groups = sets // J
    out_w = {0: [f"wz{q}" for q in range(4)], 1: ["po0", "po1"], 2: ["pout"], 3: ["wout"]}[layer]
    stored_gate = layer >= 2
    FAC, GB, OB = [bank[0], bank[1]], [bank[2], bank[3]], bank[4:8]
    z, at = core.area([2, J, T], 0)
    gate, at = core.area([2, J, T] if stored_gate else [4, T], at)
    parts, at = core.area([2, T], at, BF16)
    zn, at = core.area([2, T], at)
    term, at = core.area([2 if layer == 3 else 4, T], at)
    w = lambda name: core.w[:, SLOT[name], :]
    bias = lambda name: core.bias[:, BIAS[name]:BIAS[name] + 1]
    vec = lambda name: core.vec[:, VEC[name]:VEC[name] + 1]
    out_b = vec("b_out") if layer == 3 else bias(out_w[0])
    gate_b = bg if layer == 0 else bias("go0") if layer == 1 else None
    z_loads = 4 * nq

    def each_set(loop, body):
        for g in range(2):
            for j in range(J):
                body(g, g % 2, j)
        with loop(1, groups // 2 - 1) as i:
            for e in range(2):
                for j in range(J):
                    body(2 * i + e, e, j)
        for g in range(groups - 2, groups):
            for j in range(J):
                body(g, g % 2, j)

    def later(g, e, j, n):
        j += n
        if j >= J:
            g, e, j = g + 1, 1 - e, j - J
        return None if isinstance(g, int) and g >= groups else (g, e, j)

    def earlier(g, j, q, n):
        at = j * nq + q - n
        if at < 0:
            g, at = g - 1, at + J * nq
        return None if isinstance(g, int) and g < 0 else (g, at // nq, at % nq)

    def number(g, j, q=0):
        return (g * J + j) * nq + q

    def columns(g, j, q):
        return ds(q * sets * T + (g * J + j) * T, T)

    def ring(j, q, n):
        return (j * nq + q) % n

    with ExitStack() as ctx:
        fac_mm, zn_sb, gate_mm, gate_sb, out_mm, term_sb, x_sb, stat_sb, cen_mm, cen_sb, zeroed = core.sems(
            f"fin{layer}", "fac_mm zn_sb gate_mm gate_sb out_mm term_sb x_sb stat_sb cen_mm cen_sb zeroed")
        landed = core.sems(f"fin{layer}", "in0 in1")
        gates_in = core.sems(f"fin{layer}", "gate0 gate1")
        block = ctx.enter_context(nc.Block())

        @block.sync
        def _(sp):
            def load(g, e):
                column = [known(sp, (q * sets + g * J) * T) for q in range(nq)]
                tile = [known(sp, q * sets + g * J) for q in range(nq)]
                at_least(sp, zn_sb, J * (g - 1))
                for q in range(nq):
                    sp.dma_start(z[q * 2 * cz:(q + 1) * 2 * cz, e, :, :].rearrange("p j t -> p (j t)"),
                                 core.z_d[0:2 * cz, ds(column[q], J * T)]).then_inc(landed[e], 16)
                    for n in range(3):
                        r = 32 * n + q * 2 * J
                        src = core.rstd_d[n:n + 1, :].rearrange("a (h s t) -> s (a h) t", h=2, t=T)
                        sp.dma_start(parts[r:r + 2 * J, e, :], src[ds(tile[q], J), :, :]).then_inc(landed[e], 16)
                if stored_gate:
                    at_least(sp, cen_sb if layer == 3 else term_sb, J * (g - 1))
                    sp.dma_start(gate[:, e, :, :].rearrange("p j t -> p (j t)"),
                                 core.gate_d[:, ds(column[0], J * T)]).then_inc(gates_in[e], 16)
            sp.wait_ge(zeroed, 1)
            for g in range(2):
                load(g, g)
            with sp.Fori(1, groups // 2) as i:
                for e in range(2):
                    load(2 * i + e, e)

        @block.tensor
        def _(pe):
            def factor(g, e, j):
                if j == 0:
                    pe.wait_ge(landed[e], 8 * z_loads * (g - e) + 16 * z_loads)
                at_least(pe, zn_sb, g * J + j - 1)
                pe.matmul(FAC[j % 2][:, :], core.sel[:, SEL[nq] + j, :], parts[:, e, :], start=True,
                          stop=True).then_inc(fac_mm, 1)

            def gate_product(g, j, q, name, moving):
                at_least(pe, gate_sb, number(g, j, q) - 1)
                pe.matmul(GB[q % 2][:, :], w(name), moving, start=True, stop=True).then_inc(gate_mm, 1)

            def out_product(g, j, q, moving):
                at_least(pe, x_sb if layer == 3 else term_sb, number(g, j, q) - 3)
                pe.matmul(OB[ring(j, q, 4)][:, :], w(out_w[q]), moving, start=True, stop=True).then_inc(out_mm, 1)

            def gated_out(g, j):
                pe.wait_ge(cen_sb, g * J + j + 1)
                out_product(g, j, 0, term[:, j % 2, :])

            def one_set(g, e, j):
                ahead = later(g, e, j, 2)
                if ahead:
                    factor(*ahead)
                if layer == 3:
                    pe.wait_ge(zn_sb, g * J + j + 1)
                    at_least(pe, cen_sb, g * J + j - 1)
                    pe.matmul(GB[j % 2][:, :], w("zc"), zn[:, j % 2, :], start=True, stop=True).then_inc(cen_mm, 1)
                    before = earlier(g, j, 0, 1)
                    if before:
                        gated_out(before[0], before[1])
                    return
                for q in range(nq):
                    if layer == 0:
                        gate_product(g, j, q, "wg", xT[:, columns(g, j, q)])
                    if q == 0:
                        pe.wait_ge(zn_sb, g * J + j + 1)
                    if layer == 1:
                        gate_product(g, j, q, f"go{q}", zn[:, j % 2, :])
                    out_product(g, j, q, zn[:, j % 2, :])

            factor(0, 0, 0)
            factor(0, 0, 1)
            each_set(pe.Fori, one_set)
            if layer == 3:
                gated_out(groups - 1, J - 1)

        if not stored_gate:
            @block.scalar
            def _(act):
                def one_set(g, e, j):
                    for q in range(nq):
                        t = number(g, j, q)
                        act.wait_ge(gate_mm, t + 1)
                        at_least(act, term_sb, t - 3)
                        nc.scalar.activation(gate[:, ring(j, q, 4), :], GB[q % 2][:, :], ACT.Sigmoid,
                                             bias=gate_b).then_inc(gate_sb, 1)
                each_set(act.Fori, one_set)

        if layer < 3:
            @block.gpsimd
            def _(pool):
                def one_set(g, e, j):
                    for q in range(nq):
                        x = xT[:, columns(g, j, q)]
                        pool.wait_ge(term_sb, number(g, j, q) + 1)
                        pool.tensor_tensor(x, x, term[:, ring(j, q, 4), :], ALU.add).then_inc(x_sb, 1)
                each_set(pool.Fori, one_set)

        @block.vector
        def _(dve):
            def statistics(g, j, q):
                t = number(g, j, q)
                dve.wait_ge(x_sb, t + 1)
                dve.bn_stats(core.stats[:, ds(t, 1), :].rearrange("p a s -> p (a s)"),
                             xT[:, columns(g, j, q)]).then_inc(stat_sb, 1)

            def normed(g, e, j):
                s = g * J + j
                if j == 0:
                    dve.wait_ge(landed[e], 8 * z_loads * (g - e) + 16 * z_loads)
                dve.wait_ge(fac_mm, s + 1)
                at_least(dve, out_mm if layer < 3 else cen_mm, nq * (s - 1))
                dve.tensor_tensor(zn[:, j % 2, :], FAC[j % 2][:, :], z[:, e, j, :], ALU.mult).then_inc(zn_sb, 1)

            def gate_of(g, e, j, q):
                if stored_gate:
                    if j == 0:
                        dve.wait_ge(gates_in[e], 8 * (g - e) + 16)
                    return gate[:, e, j, :]
                dve.wait_ge(gate_sb, number(g, j, q) + 1)
                return gate[:, ring(j, q, 4), :]

            def gated(g, e, j):
                dve.wait_ge(cen_mm, g * J + j + 1)
                at_least(dve, out_mm, g * J + j - 1)
                dve.scalar_tensor_tensor(out=term[:, j % 2, :], in0=GB[j % 2][:, :], scalar=vec("out_norm_bias"),
                                         in1=gate_of(g, e, j, 0), op0=ALU.add, op1=ALU.mult).then_inc(cen_sb, 1)

            def residual(g, j):
                x = xT[:, columns(g, j, 0)]
                dve.wait_ge(out_mm, g * J + j + 1)
                dve.scalar_tensor_tensor(out=x, in0=OB[j % 4][:, :], scalar=out_b, in1=x, op0=ALU.add,
                                         op1=ALU.add).then_inc(x_sb, 1)

            def one_set(g, e, j):
                ahead = later(g, e, j, 1)
                if ahead:
                    normed(*ahead)
                if layer == 3:
                    gated(g, e, j)
                    before = earlier(g, j, 0, 2)
                    if before:
                        residual(before[0], before[1])
                    return
                for q in range(nq):
                    t = number(g, j, q)
                    gt = gate_of(g, e, j, q)
                    dve.wait_ge(out_mm, t + 1)
                    at_least(dve, x_sb, t - 3)
                    dve.scalar_tensor_tensor(out=term[:, ring(j, q, 4), :], in0=OB[ring(j, q, 4)][:, :],
                                             scalar=out_b, in1=gt, op0=ALU.add, op1=ALU.mult).then_inc(term_sb, 1)
                    before = earlier(g, j, q, 2)
                    if before:
                        statistics(*before)

            dve.memset(parts, 0.0).then_inc(zeroed, 1)
            normed(0, 0, 0)
            each_set(dve.Fori, one_set)
            for n in (2, 1):
                g, j, q = earlier(groups, 0, 0, n)
                if layer == 3:
                    residual(g, j)
                else:
                    statistics(g, j, q)


def leave(core):
    nc, bank = core.nc, core.bank
    KC = 8
    dst = core.out.rearrange("a (h p) (n k) c -> (a n) p h k c", h=2, k=KC)
    stores = N // KC
    res = [core.area([2, KC, C], b * 2 * KC * C)[0] for b in range(2)]
    xT = core.xT[:, :].rearrange("q (p k) -> q p k", k=N)
    with ExitStack() as ctx:
        turned, kept_a, kept_v = core.sems("leave", "turned kept_a kept_v")
        stored = core.sems("leave", "st0 st1")
        kept = [kept_a, kept_v]
        block = ctx.enter_context(nc.Block())

        @block.tensor
        def _(pe):
            def turn(n, b):
                for half in range(2):
                    at_least(pe, kept[half], n)
                    for k in range(4):
                        mm = pe.transpose(bank[half][:, k * P:(k + 1) * P], xT[:, :, n * KC + 4 * half + k],
                                          core.ident[:, :])
                    mm.then_inc(turned, 1)
            for n in range(stores):
                turn(n, n % 2)

        def keep(half, eng, copy):
            def body(n, b):
                eng.wait_ge(turned, 2 * n + half + 1)
                at_least(eng, stored[b], 16 * (n - b))
                copy(res[b][:, :, 4 * half:4 * half + 4, :],
                     bank[half][:, :].rearrange("p (k h c) -> p h k c", k=4, h=2)).then_inc(kept[half], 1)
            for b in range(2):
                body(b, b)
            with eng.Fori(1, stores // 2) as i:
                for b in range(2):
                    body(2 * i + b, b)

        @block.scalar
        def _(act):
            keep(0, act, nc.scalar.copy)

        @block.vector
        def _(dve):
            keep(1, dve, nc.vector.tensor_copy)

        @block.sync
        def _(sp):
            with sp.Fori(0, stores // 2) as i:
                for b in range(2):
                    at = known(sp, 2 * i + b)
                    for s in kept:
                        sp.wait_ge(s, 2 * i + b + 1)
                    for h in range(2):
                        sp.dma_start(dst[ds(at, 1), :, h, :, :].rearrange("a p k c -> p (a k) c"),
                                     res[b][:, h, :, :]).then_inc(stored[b], 16)
            for s in stored:
                sp.wait_ge(s, 16 * stores)


def build(nc, ins, out):
    with ExitStack() as ctx:
        core = Core(nc, ctx, ins, out)
        sums = [core.area([2 * N], n * 2 * N)[0] for n in range(3)]
        mask, _ = core.area([2, N], 3 * 2 * N)
        rows = lambda first, n: core.hid_d[first:first + n, 0:HALF]
        load_weights(core)
        enter(core)

        b12, bg, _, _ = fold_group_norm(core, 0)
        project0(core, b12)
        mix(core, 0, 0, 16, (rows(0, 64), rows(0, 64)), (0, 16), (True, False), 0, 16, None, sums)
        fold_sums(core, 0, 16, sums)
        finish(core, 0, 4, bg)

        _, _, ub, gmean = fold_group_norm(core, 1)
        project(core, 1, ["gi"], ["pi"], ub, gmean)
        make_mask(core, 1, mask)
        mix(core, 1, 0, 16, (rows(0, P), rows(0, P)), (0, 16), (True, True), 0, 32, mask, sums)
        mix(core, 1, 1, 16, (rows(0, P), rows(0, P)), (32, 48), (False, False), 16, 32, mask, sums)
        fold_sums(core, 1, 32, sums)
        finish(core, 1, 2, None)

        _, _, ub, gmean = fold_group_norm(core, 2)
        project(core, 2, ["gl", "gate", "gr"], ["pl", "pr"], ub, gmean)
        mix(core, 2, 0, 64, (rows(0, P), rows(P, P)), (0, 0), (True, True), 0, 64, None, sums)
        fold_sums(core, 2, 64, sums)
        finish(core, 2, 1, None)

        _, _, ub, gmean = fold_group_norm(core, 3)
        project(core, 3, ["lg", "og", "rg"], ["left", "right"], ub, gmean)
        make_mask(core, 3, mask)
        mix(core, 3, 0, 64, (rows(0, P), rows(P, P)), (0, 0), (False, False), 0, 64, mask, sums)
        fold_sums(core, 3, 64, sums)
        finish(core, 3, 1, None)
        leave(core)


def kernel(**inputs):
    import concourse.bacc as bacc
    from concourse.bass_utils import run_bass_kernel_spmd

    nc = bacc.Bacc("TRN2", target_bir_lowering=False, num_devices=1)
    arrays, ins = {}, {}
    inputs = {name: np.asarray(a) for name, a in inputs.items()}
    used = {name: inputs[name] for name in ("x", "L1_conv_mask", "L3_conv_src_mask")}
    for name, a in {**used, "weights": weight_layout(inputs), "vectors": vector_layout(inputs),
                    "constants": constants()}.items():
        a = np.ascontiguousarray(a)
        arrays[f"in_{name}"] = a
        ins[name] = nc.dram_tensor(f"in_{name}", a.shape, mybir.dt.from_np(a.dtype), kind="ExternalInput").ap()
    out = nc.dram_tensor("out", (1, N, N, C), F32, kind="ExternalOutput").ap()
    build(nc, ins, out)
    r = run_bass_kernel_spmd(nc, [arrays], core_ids=[0])
    return r.results[0]["out"]
```

```python
from contextlib import ExitStack

import numpy as np

import concourse.bass as bass
from concourse import mybir

F32 = mybir.dt.float32
BF16 = mybir.dt.bfloat16
F32R = mybir.dt.float32r
ALU = mybir.AluOpType
ACT = mybir.ActivationFunctionType
ds = bass.ds

P = 128
N = 256
C = 64
HALF = N * N // 2
T = 512
NT = HALF // T
JP = 16
SETS = {1: 4, 2: 4, 4: 2}
PITCH = HALF + 1024

K_ID, K_C64, K_C32, K_C16, K_GRP, K_SUM, K_EPS5, K_EPS6, K_POW, K_SEL = (
    0, 128, 256, 384, 512, 640, 702, 703, 704, 705)
NSEL = JP + SETS[2] + SETS[4]
K_ALL = K_SEL + NSEL * P
SEL = {1: 0, 2: JP, 4: JP + SETS[2]}


def constants():
    k = np.zeros((P, K_ALL), np.float32)
    row = np.arange(P)
    k[:, K_ID:K_ID + P] = np.eye(P)
    for at, n in ((K_C64, 64), (K_C32, 32), (K_C16, 16)):
        k[:, at:at + P] = np.eye(P) - (row[:, None] // n == row[None] // n) / n
    k[:, K_GRP:K_GRP + P] = (row[:, None] % C // 2 == row[None] % C // 2) / 4
    k[row, K_SUM + 2 * (JP - 1) + row // C] = 1 / C
    k[:, K_EPS5], k[:, K_EPS6], k[:, K_POW] = 1e-5, 1e-6, -0.5
    for nq, at in SEL.items():
        cz, tiles = C // nq, SETS[nq]
        for j in range(JP if nq == 1 else tiles):
            for part in range(3):
                for q in range(nq):
                    for h in range(2):
                        col = K_SEL + (at + j) * P + q * 2 * cz + h * cz
                        if nq == 1:
                            r = 32 * part + 2 * j + h
                        else:
                            r = q * 6 * tiles + (2 * part + h) * tiles + j
                        k[r, col:col + cz] = 1
    return k


def known(eng, value):
    return value if isinstance(value, int) else eng.snap(value)


def at_least(eng, sem, value):
    if not isinstance(value, int) or value > 0:
        eng.wait_ge(sem, value)


class Steps:

    def __init__(self, sem):
        self.sem, self.n = sem, 0

    def done(self, instruction):
        instruction.then_inc(self.sem, 1)
        self.n += 1

    def wait(self, eng):
        at_least(eng, self.sem, self.n)


RAW = (["w12", "wg"] + [f"wz{q}" for q in range(4)]
       + ["gi", "pi", "po0", "po1", "go0", "go1"]
       + ["g2", "p2", "go2", "pout"]
       + ["g3", "p3", "go3", "wout"])
WEIGHTS = RAW + ["zc"]
SLOT = {name: n for n, name in enumerate(WEIGHTS)}
SLOT["center"] = SLOT["w12"]
VECTORS = ["b12", "bg", "bz", "ln2_g", "ln2_b",
           "pi_b", "gi_b", "po_b", "go_b", "ni_w", "ni_b", "no_w", "no_b",
           "norm_in_w", "norm_in_b", "norm_out_w", "norm_out_b",
           "norm_scale", "norm_bias", "b_gates", "b_values", "b_ogate",
           "out_norm_scale", "out_norm_bias", "b_out"]
VEC = {name: n for n, name in enumerate(VECTORS)}
FOLDS = [([f"wz{q}" for q in range(4)], ["bz"] * 4, "ln2_g", "ln2_b", K_C16),
         (["gi", "pi"], ["gi_b", "pi_b"], "ni_w", "ni_b", K_C64),
         (["po0", "po1", "go0", "go1"], ["po_b", "po_b", "go_b", "go_b"], "no_w", "no_b", K_C32),
         (["g2", "p2", "go2"], [None] * 3, "norm_in_w", "norm_in_b", K_C64),
         (["pout"], [None], "norm_out_w", "norm_out_b", K_C64),
         (["g3", "p3", "go3"], ["b_gates", "b_values", "b_ogate"], "norm_scale", "norm_bias", K_C64)]
FOLDED = [(name, b, f[3]) for f in FOLDS for name, b in zip(f[0], f[1])]
BIAS = {name: n for n, (name, _, _) in enumerate(FOLDED)}
PROJECTIONS = {1: ["gi", "pi"], 2: ["g2", "p2"], 3: ["g3", "p3"]}
OUTPUT_GATE = {2: "go2", 3: "go3"}
STACKED = ["g2", "p2", "g3", "p3"]


class Core:

    def __init__(self, nc, ctx, ins, out):
        self.nc, self.ins, self.out = nc, ins, out
        self.spent = []

        def sb(name, shape, dt=F32):
            return ctx.enter_context(nc.sbuf_tensor(name, shape, dt))

        self.xT = sb("xT", [P, HALF])
        self.w = sb("w", [P, len(WEIGHTS), P])
        self.ident = sb("ident", [P, P])
        self.c64 = sb("c64", [P, P])
        self.grp = sb("grp", [P, P])
        self.summer = sb("summer", [P, 2 * (JP - 1) + 32], F32R)
        self.cols = sb("cols", [P, 3])
        self.sel = sb("sel", [P, NSEL, P], BF16)
        self.vec = sb("vec", [P, len(VECTORS)])
        self.bias = sb("bias", [P, len(FOLDED)])
        self.stats = sb("stats", [P, NT, 6])
        self.fold = sb("fold", [P, 16])
        self.w_hi = sb("w_hi", [P, 2, P], F32R)
        self.w_lo = sb("w_lo", [P, 2, P], F32R)
        self.x_parts = sb("x_parts", [P, 4, 2, T], F32R)
        self.work = sb("work", [P, 10752])
        self.bank = [ctx.enter_context(nc.psum_tensor(f"bank{n}", [P, T], F32)) for n in range(8)]

        self.hid_d = nc.dram_tensor("hidden_rows", (2 * P, PITCH), F32).ap()
        self.z_d = nc.dram_tensor("z_rows", (P, PITCH), F32).ap()
        self.gate_d = nc.dram_tensor("gate_rows", (P, PITCH), F32).ap()
        self.rstd_d = nc.dram_tensor("rstd_parts", (3, 2 * HALF), BF16).ap()

    def area(self, shape, at, dt=F32):
        n = int(np.prod(shape))
        words = n if dt == F32 else (n + 1) // 2
        ap = self.work[:, at:at + words]
        if dt != F32:
            ap = ap.bitcast(dt)
        if len(shape) == 2:
            ap = ap.rearrange("p (a b) -> p a b", a=shape[0])
        if len(shape) == 3:
            ap = ap.rearrange("p (a b c) -> p a b c", a=shape[0], b=shape[1])
        assert at + words <= self.work.shape[1], (shape, at)
        return ap, at + words

    def sems(self, phase, names):
        if not self.spent or self.spent[-1][0] != phase:
            if len(self.spent) >= 2:
                for s in self.spent[-2][1]:
                    self.nc.gpsimd.sem_clear(s)
            if len(self.spent) >= 3:
                for s in self.spent[-3][1]:
                    self.nc.release_semaphore(s)
            self.spent.append((phase, []))
        found = [self.nc.alloc_semaphore(f"{phase}_{n}") for n in names.split()]
        self.spent[-1][1].extend(found)
        return found


def weight_layout(ins):
    w = np.zeros((P, len(RAW), P), np.float32)

    def put(name, r, c, block):
        w[r:r + block.shape[0], SLOT[name], c:c + block.shape[1]] = block
    for h in range(2):
        for s in range(2):
            for k, ab in enumerate("ab"):
                put("w12", h * C, s * 64 + h * 32 + k * 16, ins[f"L0_conv_W{ab}{s + 1}"])
        put("wg", h * C, h * C, ins["L0_conv_Wg"])
        for q in range(4):
            put(f"wz{q}", q * 32 + h * 16, h * C, ins["L0_conv_Wz"])
        for name in ("gi", "pi"):
            put(name, h * C, h * C, ins[f"L1_conv_{name}_w"].T)
        for name in ("po", "go"):
            for q in range(2):
                put(f"{name}{q}", q * 64 + h * 32, h * C, ins[f"L1_conv_{name}_w"].T)
        for name, raw, at in (("g2", "g_in_w", 0), ("p2", "p_in_w", 0), ("go2", "g_out_w", h * C),
                              ("pout", "p_out_w", h * C)):
            put(name, h * C, at, ins[f"L2_conv_{raw}"].T)
        for name, raw, at in (("g3", "lgate", 0), ("g3", "rgate", C), ("p3", "left", 0), ("p3", "right", C),
                              ("go3", "ogate", h * C), ("wout", "out", h * C)):
            put(name, h * C, at, ins[f"L3_conv_W_{raw}"])
    return w


def vector_layout(ins):
    v = np.zeros((P, len(VECTORS)), np.float32)
    for s in range(2):
        for h in range(2):
            for k, ab in enumerate("ab"):
                v[s * 64 + h * 32 + k * 16:s * 64 + h * 32 + k * 16 + 16, VEC["b12"]] = ins[f"L0_conv_b{ab}{s + 1}"]
    layer = {**dict.fromkeys(VECTORS[1:5], "L0"), **dict.fromkeys(VECTORS[5:13], "L1"),
             **dict.fromkeys(VECTORS[13:17], "L2"), **dict.fromkeys(VECTORS[17:], "L3")}
    for name, l in layer.items():
        sides = {"b_gates": ("b_lgate", "b_rgate"), "b_values": ("b_left", "b_right")}.get(name, (name,))
        raw = np.concatenate([ins[f"{l}_conv_{side}"] for side in sides])
        v[:, VEC[name]] = np.tile(raw, P // raw.shape[0])
    return v


def load_weights(core):
    nc, ins, bank = core.nc, core.ins, core.bank
    consts, at = core.area([K_ALL], 0)
    zc_t, at = core.area([P], at)
    w = lambda name: core.w[:, SLOT[name], :]
    col = lambda name: core.vec[:, VEC[name]:VEC[name] + 1]

    def columns(names, first=0, last=None):
        at = SLOT[names[0]]
        return core.w[:, at + first:at + (last or len(names)), :].rearrange("p n m -> p (n m)")
    cuts = [(n, a, min(a + 4, len(f[0]))) for n, f in enumerate(FOLDS) for a in range(0, len(f[0]), 4)]

    with ExitStack() as ctx:
        landed, placed, zc_made, bias_mm, bias_sb, turned, scaled, centred, kept = core.sems(
            "prep", "landed placed zc_made bias_mm bias_sb turned scaled centred kept")
        block = ctx.enter_context(nc.Block())

        @block.sync
        def _(sp):
            sp.dma_start(core.w[:, 0:len(RAW), :], ins["weights"]).then_inc(landed, 16)
            sp.dma_start(core.vec[:, :], ins["vectors"]).then_inc(landed, 16)

        @block.tensor
        def _(pe):
            pe.wait_ge(landed, 48)
            for n, (name, _, shift) in enumerate(FOLDED):
                rows = slice(0, C if name in STACKED else P)
                mm = pe.matmul(bank[0][:, n:n + 1], w(name)[rows, :], col(shift)[rows, :], start=True, stop=True)
            mm.then_inc(bias_mm, 1)
            pe.wait_ge(zc_made, 1)
            pe.transpose(bank[1][:, 0:P], zc_t, consts[:, K_ID:K_ID + P]).then_inc(turned, 1)
            for n, (f, first, last) in enumerate(cuts):
                names, centre = FOLDS[f][0], FOLDS[f][4]
                pe.wait_ge(scaled, f + 1)
                at_least(pe, kept, n - 3)
                pe.matmul(bank[2 + n % 4][:, 0:(last - first) * P], consts[:, centre:centre + P],
                          columns(names, first, last), start=True, stop=True).then_inc(centred, 1)

        @block.vector
        def _(dve):
            dve.wait_ge(landed, 48)
            dve.tensor_scalar(zc_t, consts[:, K_C64:K_C64 + P], col("out_norm_scale"), None,
                              ALU.mult).then_inc(zc_made, 1)
            dve.wait_ge(bias_mm, 1)
            for names, _, scale, _, _ in FOLDS:
                dve.tensor_scalar(columns(names), columns(names), col(scale), None, ALU.mult).then_inc(scaled, 1)
            for n, (name, b, _) in enumerate(FOLDED):
                if b:
                    ins_ = dve.tensor_tensor(core.bias[:, n:n + 1], bank[0][:, n:n + 1], col(b), ALU.add)
                else:
                    ins_ = dve.tensor_copy(core.bias[:, n:n + 1], bank[0][:, n:n + 1])
                ins_.then_inc(bias_sb, 1)
            dve.wait_ge(turned, 1)
            dve.tensor_copy(w("zc"), bank[1][:, 0:P]).then_inc(placed, 1)
            dve.tensor_copy(core.sel[:, :, :].rearrange("p a b -> p (a b)"), consts[:, K_SEL:K_ALL]).then_inc(placed, 1)

        @block.scalar
        def _(act):
            act.dma_start(consts, ins["constants"]).then_inc(landed, 16)
            act.wait_ge(landed, 48)
            for dst, at, n in ((core.ident, K_ID, P), (core.c64, K_C64, P), (core.grp, K_GRP, P),
                               (core.summer, K_SUM, 2 * (JP - 1) + 32), (core.cols, K_EPS5, 3)):
                nc.scalar.copy(dst[:, :], consts[:, at:at + n]).then_inc(placed, 1)
            for n, (f, first, last) in enumerate(cuts):
                act.wait_ge(centred, n + 1)
                nc.scalar.copy(columns(FOLDS[f][0], first, last), bank[2 + n % 4][:, 0:(last - first) * P]
                               ).then_inc(kept, 1)


def enter(core):
    nc, bank = core.nc, core.bank
    KC = 8
    x = core.ins["x"].rearrange("a (h p) (n k) c -> (a n) p h k c", h=2, k=KC)
    loads = N // KC
    xin, at = core.area([4, 2 * KC * C], 0)
    xpix, at = core.area([4, KC * 2 * C], at)
    xT = core.xT[:, :].rearrange("q (p k) -> q p k", k=N)
    with ExitStack() as ctx:
        paired_v, paired_a, turned, kept, counted = core.sems("enter", "paired_v paired_a turned kept counted")
        landed = core.sems("enter", "in0 in1 in2 in3")
        block = ctx.enter_context(nc.Block())

        def each_load(loop, body):
            for b in range(4):
                body(0, b)
            with loop(1, loads // 4) as i:
                for b in range(4):
                    body(i, b)

        def pairs(i, b):
            return (paired_v, paired_a)[b % 2], 2 * i + b // 2 + 1

        def pair(eng, copy, i, b):
            eng.wait_ge(landed[b], 32 * i + 32)
            at_least(eng, turned, 8 * i + 2 * b - 6)
            copy(xpix[:, b, :].rearrange("p (k h c) -> p h k c", k=KC, h=2),
                 xin[:, b, :].rearrange("p (h k c) -> p h k c", k=KC, h=2)).then_inc(pairs(i, b)[0], 1)

        def two_behind(i, b):
            if b < 2:
                i, b = i - 1, b + 4
            return None if isinstance(i, int) and i < 0 else (i, b - 2)

        @block.sync
        def _(sp):
            def load(i, b):
                n_at = known(sp, 4 * i + b)
                if not isinstance(i, int):
                    sem, value = pairs(i, b)
                    sp.wait_ge(sem, value - 2)
                for h in range(2):
                    sp.dma_start(xin[:, b, h * KC * C:(h + 1) * KC * C],
                                 x[ds(n_at, 1), :, h, :, :].rearrange("a p k c -> p (a k c)")
                                 ).then_inc(landed[b], 16)
            each_load(sp.Fori, load)

        @block.tensor
        def _(pe):
            def turn(i, b):
                sem, value = pairs(i, b)
                pe.wait_ge(sem, value)
                for half in range(2):
                    at_least(pe, kept, 8 * i + 2 * b + half - 7)
                    for k in range(4):
                        at = (4 * half + k) * P
                        mm = pe.transpose(bank[2 * b + half][:, k * P:(k + 1) * P], xpix[:, b, at:at + P],
                                          core.ident[:, :])
                    mm.then_inc(turned, 1)
            each_load(pe.Fori, turn)

        @block.vector
        def _(dve):
            def count(i, b):
                for half in range(2):
                    t = 8 * i + 2 * b + half
                    dve.wait_ge(turned, t + 1)
                    dve.bn_stats(core.stats[:, ds(t, 1), :].rearrange("p a s -> p (a s)"),
                                 bank[2 * b + half][:, :]).then_inc(counted, 1)

            def load(i, b):
                if b % 2 == 0:
                    pair(dve, nc.vector.tensor_copy, i, b)
                if two_behind(i, b):
                    count(*two_behind(i, b))
            each_load(dve.Fori, load)
            for b in (2, 3):
                count(loads // 4 - 1, b)

        @block.scalar
        def _(act):
            def keep(i, b):
                for half in range(2):
                    t = 8 * i + 2 * b + half
                    act.wait_ge(counted, t + 1)
                    nc.scalar.copy(xT[:, :, ds(4 * t, 4)],
                                   bank[2 * b + half][:, :].rearrange("q (k p) -> q p k", p=P)).then_inc(kept, 1)

            def load(i, b):
                if b % 2:
                    pair(act, nc.scalar.copy, i, b)
                if two_behind(i, b):
                    keep(*two_behind(i, b))
            each_load(act.Fori, load)
            for b in (2, 3):
                keep(loads // 4 - 1, b)


def fold_group_norm(core, layer):
    nc, bank = core.nc, core.bank
    f = core.fold
    mean_var, gmean, dev, spread, gvar, r, b = (f[:, 0:2], f[:, 2:3], f[:, 3:4], f[:, 4:5], f[:, 5:6], f[:, 6:7], f[:, 7:8])
    b12, bg, ub = f[:, 8:9], f[:, 9:10], f[:, 10:11]
    w = lambda name: core.w[:, SLOT[name], :]
    with ExitStack() as ctx:
        dve_s, pe_s, pow_s = core.sems(f"fold{layer}", "dve pe pow")
        block = ctx.enter_context(nc.Block())

        @block.vector
        def _(dve):
            step = Steps(dve_s)
            step.done(dve.bn_aggr(mean_var, core.stats[:, :, :].rearrange("p n s -> p (n s)")))
            dve.wait_ge(pe_s, 1)
            step.done(dve.tensor_copy(gmean, bank[0][:, 0:1]))
            step.wait(dve)
            step.done(dve.tensor_tensor(dev, mean_var[:, 0:1], gmean, ALU.subtract))
            step.wait(dve)
            step.done(dve.scalar_tensor_tensor(out=spread, in0=dev, scalar=dev, in1=mean_var[:, 1:2],
                                               op0=ALU.mult, op1=ALU.add))
            dve.wait_ge(pe_s, 2)
            step.done(dve.tensor_scalar(gvar, bank[1][:, 0:1], core.cols[:, 0:1], None, ALU.add))
            dve.wait_ge(pow_s, 1)
            step.done(dve.scalar_tensor_tensor(out=b, in0=gmean, scalar=-1.0, in1=r, op0=ALU.mult, op1=ALU.mult))
            if layer == 0:
                dve.wait_ge(pe_s, 4)
                step.done(dve.tensor_scalar(w("w12"), w("w12"), r, None, ALU.mult))
                step.done(dve.tensor_scalar(w("wg"), w("wg"), r, None, ALU.mult))
                step.done(dve.tensor_tensor(b12, bank[2][:, 0:1], core.vec[:, VEC["b12"]:VEC["b12"] + 1], ALU.add))
                step.done(dve.tensor_tensor(bg, bank[3][:, 0:1], core.vec[:, VEC["bg"]:VEC["bg"] + 1], ALU.add))
            else:
                step.done(dve.tensor_scalar(w("center"), core.c64[:, :], r, None, ALU.mult))
                dve.wait_ge(pe_s, 3)
                step.done(dve.tensor_copy(ub, bank[2][:, 0:1]))
                names = PROJECTIONS[layer]
                raw = core.w[:, SLOT[names[0]]:SLOT[names[0]] + len(names), :]
                hi, lo = core.w_hi[:, 0:len(names), :], core.w_lo[:, 0:len(names), :]
                step.done(dve.tensor_scalar(hi, raw, r, None, ALU.mult))
                step.wait(dve)
                step.done(dve.scalar_tensor_tensor(out=lo, in0=raw, scalar=r, in1=hi.bitcast(F32), op0=ALU.mult,
                                                   op1=ALU.subtract))
                if layer in OUTPUT_GATE:
                    name = OUTPUT_GATE[layer]
                    step.done(dve.tensor_scalar(w(name), w(name), r, None, ALU.mult))

        @block.gpsimd
        def _(pool):
            pool.wait_ge(dve_s, 5)
            pool.tensor_tensor(r, gvar, core.cols[:, 2:3], ALU.pow).then_inc(pow_s, 1)

        @block.tensor
        def _(pe):
            pe.wait_ge(dve_s, 1)
            pe.matmul(bank[0][:, 0:1], core.grp[:, :], mean_var[:, 0:1], start=True, stop=True).then_inc(pe_s, 1)
            pe.wait_ge(dve_s, 4)
            pe.matmul(bank[1][:, 0:1], core.grp[:, :], spread, start=True, stop=True).then_inc(pe_s, 1)
            pe.wait_ge(dve_s, 6)
            if layer == 0:
                pe.matmul(bank[2][:, 0:1], w("w12"), b, start=True, stop=True).then_inc(pe_s, 1)
                pe.matmul(bank[3][:, 0:1], w("wg"), b, start=True, stop=True).then_inc(pe_s, 1)
            else:
                pe.matmul(bank[2][:, 0:1], core.c64[:, :], b, start=True, stop=True).then_inc(pe_s, 1)
    return b12, bg, ub, gmean


def project0(core, b12):
    nc, bank, xT = core.nc, core.bank, core.xT
    first, at = core.area([4, T], 0)
    prod, at = core.area([4, T], at)
    hid, at = core.area([4, T], at)
    wst = core.w[:, SLOT["w12"], :]
    dst = core.hid_d[0:64, 0:HALF].rearrange("q (n s t) -> n q s t", s=8, t=T)

    def each_pair(loop, body):
        for b in range(4):
            body(b, b)
        with loop(1, NT // 8) as i:
            for b in range(4):
                body(4 * i + b, b)

    with ExitStack() as ctx:
        mm, one, two, act_s = core.sems("proj0", "mm one two act")
        stored = core.sems("proj0", "st0 st1 st2 st3")
        block = ctx.enter_context(nc.Block())

        @block.tensor
        def _(pe):
            def pair(p, b):
                for k in range(2):
                    t = 2 * p + k
                    at_least(pe, two, t - 3)
                    pe.matmul(bank[2 * (b % 2) + k][:, :], wst, xT[:, ds(t * T, T)], start=True,
                              stop=True).then_inc(mm, 1)
            each_pair(pe.Fori, pair)

        @block.scalar
        def _(act):
            def factors(p, b):
                for k in range(2):
                    t, f = 2 * p + k, 2 * (b % 2) + k
                    act.wait_ge(mm, t + 1)
                    at_least(act, two, t - 3)
                    nc.scalar.activation(first[0:64, f, :], bank[f][0:64, :], ACT.Identity,
                                         bias=b12[0:64, :]).then_inc(one, 1)

            def sigmoid(p, b):
                act.wait_ge(two, 2 * p + 2)
                at_least(act, stored[b], 8 * (p - b))
                nc.scalar.activation(hid[:, b, :], prod[:, b, :], ACT.Sigmoid).then_inc(act_s, 1)

            def pair(p, b):
                factors(p, b)
                if not (isinstance(p, int) and p == 0):
                    sigmoid(p - 1, (b - 1) % 4)
            each_pair(act.Fori, pair)
            sigmoid(NT // 2 - 1, 3)

        @block.vector
        def _(dve):
            def pair(p, b):
                for k in range(2):
                    f = 2 * (b % 2) + k
                    dve.wait_ge(one, 2 * p + k + 1)
                    at_least(dve, act_s, p - 3)
                    dve.scalar_tensor_tensor(out=prod[64 * k:64 * k + 64, b, :], in0=bank[f][64:128, :],
                                             scalar=b12[64:128, :], in1=first[0:64, f, :], op0=ALU.add,
                                             op1=ALU.mult).then_inc(two, 1)
            each_pair(dve.Fori, pair)

        @block.sync
        def _(sp):
            with sp.Fori(0, NT // 8) as i:
                for b in range(4):
                    i_at = known(sp, i)
                    sp.wait_ge(act_s, 4 * i + b + 1)
                    for k in range(2):
                        sp.dma_start(dst[ds(i_at, 1), :, 2 * b + k, :].rearrange("a q t -> q (a t)"),
                                     hid[64 * k:64 * k + 64, b, :]).then_inc(stored[b], 16)
            for s in stored:
                sp.wait_ge(s, 32 * (NT // 8))


def project(core, layer, gates, values, ub, gmean):
    nc, bank, xT = core.nc, core.bank, core.xT
    stacked = layer >= 2
    NG, NV = len(gates), len(values)
    LAG = 3
    SPLIT = 9
    PARTS = 2 if stacked else 1
    U, STAT, VB = bank[0:2], bank[2], bank[6:8]
    FAC = [bank[3], bank[2]]
    GB = [bank[4], bank[5], bank[0], bank[1]]
    h, at = core.area([4, T], 0)
    sq = h
    rows, at = core.area([T], at)
    rec, rest, sd = (rows[32 * n:32 * n + 32, :] for n in range(3))
    three, at = core.area([T], at, BF16)
    parts, at = core.area([NT // JP, T], at, BF16)
    res, at = core.area([4, NG * T], at)
    x_parts = core.x_parts
    groups = NT // JP
    eps = core.cols[0:32, 1:2] if layer == 3 else core.cols[0:32, 0:1]
    w = lambda name: core.w[:, SLOT[name], :]
    bias = lambda name: core.bias[:, BIAS[name]:BIAS[name] + 1]
    w_part = {name: (core.w_hi[:, n, :], core.w_lo[:, n, :]) for n, name in enumerate(PROJECTIONS[layer])}
    of_gate = {0: 0, NG - 1: NV - 1}
    gate_of = [0, NG - 1][:NV]
    result = lambda j, m: res[:, j % 4, m * T:m * T + T]
    group_parts = lambda g: parts[:, ds(g, 1), :].rearrange("p a t -> p (a t)")
    dsts = ([core.hid_d[0:P, :], core.gate_d, core.hid_d[P:2 * P, :]] if stacked else [core.hid_d[0:P, :]])

    def statistics(loop, body):
        for g in range(2):
            for j in range(JP):
                body(g, j)
        with loop(2, groups) as g:
            for j in range(JP):
                body(g, j)

    def projections(loop, body):
        for j in range(JP):
            body(0, j)
        with loop(1, groups - 1) as g:
            for j in range(JP):
                body(g, j)
        for j in range(JP):
            body(groups - 1, j)

    def within(t, n=NT):
        return not isinstance(t, int) or t < n

    with ExitStack() as ctx:
        (u_mm, sq_sb, sq_hi_sb, sq_lo_sb, sum_mm, sd_sb, split_s, fac_mm, h_sb, hi_a, hi_v, lo_sb, gate_mm, val_mm,
         gate_sb, val_sb, zeroed) = core.sems(f"proj{layer}", "u_mm sq_sb sq_hi_sb sq_lo_sb sum_mm sd_sb split fac_mm "
                                              "h_sb hi_a hi_v lo_sb gate_mm val_mm gate_sb val_sb zeroed")
        hi_sb = [hi_a, hi_v]
        stored = core.sems(f"proj{layer}", "st0 st1 st2 st3")
        block = ctx.enter_context(nc.Block())

        def buffer_free(eng, t):
            if isinstance(t, int) and t < 4:
                eng.wait_ge(sum_mm, NT - 3 + t)
            else:
                eng.wait_ge(val_mm, NV * (t - 3))

        def high(eng, copy, t, j, half):
            eng.wait_ge(h_sb, t + 1)
            buffer_free(eng, t)
            r = slice(half * C, half * C + C) if stacked else slice(0, P)
            copy(x_parts[r, j % 4, half, :], h[r, j % 4, :]).then_inc(hi_sb[half], 1)

        @block.tensor
        def _(pe):
            def mean_square(t, g, j):
                pe.wait_ge(sq_lo_sb, t + 1)
                if j == 0:
                    at_least(pe, sd_sb, g)
                window = core.summer[:, 2 * (JP - 1 - j):2 * (JP - 1 - j) + 32]
                pe.matmul(STAT[0:32, :], window, x_parts[:, j % 4, 0, :], start=(j == 0), stop=False)
                pe.matmul(STAT[0:32, :], window, x_parts[:, j % 4, 1, :], start=False,
                          stop=(j == JP - 1)).then_inc(sum_mm, 1)

            def statistic(g, j):
                t = g * JP + j
                at_least(pe, sq_sb, t - 1)
                pe.matmul(U[j % 2][:, :], w("center"), xT[:, ds(t * T, T)], start=True, stop=True).then_inc(u_mm, 1)
                if j >= LAG:
                    mean_square(t - LAG, g, j - LAG)
                elif not (isinstance(g, int) and g == 0):
                    mean_square(t - LAG, g - 1, j - LAG + JP)

            def factor(t, g, j):
                if j == 0:
                    pe.wait_ge(split_s, SPLIT * (g + 1))
                if isinstance(t, int) and t == 1:
                    pe.wait_ge(sd_sb, groups)
                at_least(pe, h_sb, t - 1)
                pe.matmul(FAC[j % 2][:, :], core.sel[:, SEL[1] + j, :], group_parts(g), start=True,
                          stop=True).then_inc(fac_mm, 1)

            def product(out, name, half, j):
                w_hi, w_lo = w_part[name]
                if stacked:
                    x = x_parts[:, j % 4, half, :]
                    pe.matmul(out, w_hi, x, start=True, stop=False)
                    return pe.matmul(out, w_lo, x, start=False, stop=True)
                hi, lo = x_parts[:, j % 4, 0, :], x_parts[:, j % 4, 1, :]
                pe.matmul(out, w_hi, hi, start=True, stop=False)
                pe.matmul(out, w_lo, hi, start=False, stop=False)
                return pe.matmul(out, w_hi, lo, start=False, stop=True)

            def projection(g, j):
                t = g * JP + j
                if j < JP - 3:
                    factor(t + 3, g, j + 3)
                elif within(g + 1, groups):
                    factor(t + 3, g + 1, j + 3 - JP)
                pe.wait_ge(lo_sb, PARTS * (t + 1))
                for m in range(NG):
                    n = NG * t + m
                    at_least(pe, gate_sb, n - 3)
                    out = GB[(NG * j + m) % 4][:, :]
                    if m in of_gate:
                        v = of_gate[m]
                        product(out, gates[m], v, j).then_inc(gate_mm, 1)
                        at_least(pe, val_sb, NV * t + v - 1)
                        product(VB[(NV * j + v) % 2][:, :], values[v], v, j).then_inc(val_mm, 1)
                    else:
                        pe.matmul(out, w(gates[m]), h[:, j % 4, :], start=True, stop=True).then_inc(gate_mm, 1)

            statistics(pe.Fori, statistic)
            factor(0, 0, 0)
            for t in range(NT - LAG, NT):
                mean_square(t, groups - 1, t % JP)
            factor(1, 0, 1)
            factor(2, 0, 2)
            projections(pe.Fori, projection)

        @block.scalar
        def _(act):
            def high_square(t, j):
                act.wait_ge(sq_sb, t + 1)
                at_least(act, sum_mm, t - 3)
                nc.scalar.copy(x_parts[:, j % 4, 0, :], sq[:, j % 4, :]).then_inc(sq_hi_sb, 1)

            def root(g):
                act.wait_ge(sum_mm, JP * g + JP)
                at_least(act, split_s, SPLIT * (g - 1) + 4)
                nc.scalar.activation(sd, STAT[0:32, :], ACT.Sqrt, bias=eps).then_inc(sd_sb, 1)

            def statistic(g, j):
                t = g * JP + j
                behind = not (isinstance(g, int) and g == 0)
                if j == LAG and behind:
                    root(g - 1)
                act.wait_ge(u_mm, t + 1)
                at_least(act, sq_lo_sb, t - 3)
                nc.scalar.activation(sq[:, j % 4, :], U[j % 2][:, :], ACT.Square, bias=ub).then_inc(sq_sb, 1)
                if j or behind:
                    high_square(t - 1, j - 1)

            def projection(g, j):
                t = g * JP + j
                if within(t + 2):
                    high(act, nc.scalar.copy, t + 2, j + 2, 0)
                for m in range(NG):
                    act.wait_ge(gate_mm, NG * t + m + 1)
                    if m == 0:
                        at_least(act, stored[j % 4], 16 * NG * (JP // 4 * g + j // 4))
                    nc.scalar.activation(result(j, m), GB[(NG * j + m) % 4][:, :],
                                         ACT.Sigmoid, bias=bias(gates[m])).then_inc(gate_sb, 1)

            statistics(act.Fori, statistic)
            high_square(NT - 1, NT - 1)
            high(act, nc.scalar.copy, 0, 0, 0)
            root(groups - 1)
            high(act, nc.scalar.copy, 1, 1, 0)
            projections(act.Fori, projection)

        @block.gpsimd
        def _(pool):
            def low(t, j):
                for n in range(PARTS):
                    pool.wait_ge(hi_sb[n], t + 1)
                    if n == 0:
                        buffer_free(pool, t)
                    if stacked:
                        r, to = slice(n * C, n * C + C), slice((1 - n) * C, (1 - n) * C + C)
                        out, hi = x_parts[to, j % 4, n, :], x_parts[r, j % 4, n, :]
                    else:
                        r = slice(0, P)
                        out, hi = x_parts[:, j % 4, 1, :], x_parts[:, j % 4, 0, :]
                    pool.tensor_tensor(out, h[r, j % 4, :], hi.bitcast(F32), ALU.subtract).then_inc(lo_sb, 1)

            def projection(g, j):
                if within(g * JP + j + 2):
                    low(g * JP + j + 2, j + 2)
            low(0, 0)
            low(1, 1)
            projections(pool.Fori, projection)

        @block.vector
        def _(dve):
            def split(g, step):
                a, b, c = (three[32 * n:32 * n + 32, :] for n in range(3))
                if step < 4:
                    if step == 0:
                        dve.wait_ge(sd_sb, g + 1)
                    k = slice(step * T // 4, (step + 1) * T // 4)
                    dve.reciprocal(rec[:, k], sd[:, k]).then_inc(split_s, 1)
                    return
                dve.wait_ge(split_s, SPLIT * g + step)
                if step == 4:
                    dve.tensor_copy(a, rec).then_inc(split_s, 1)
                if step == 5:
                    dve.tensor_tensor(rest, rec, a, ALU.subtract).then_inc(split_s, 1)
                if step == 6:
                    dve.tensor_copy(b, rest).then_inc(split_s, 1)
                if step == 7:
                    dve.tensor_tensor(c, rest, b, ALU.subtract).then_inc(split_s, 1)
                if step == 8:
                    dve.tensor_copy(group_parts(g)[0:96, :], three[0:96, :]).then_inc(split_s, 1)

            def statistic(g, j):
                t = g * JP + j
                dve.wait_ge(sq_hi_sb, t + 1)
                at_least(dve, sum_mm, t - 3)
                dve.tensor_tensor(x_parts[:, j % 4, 1, :], sq[:, j % 4, :], x_parts[:, j % 4, 0, :].bitcast(F32),
                                  ALU.subtract).then_inc(sq_lo_sb, 1)
                if LAG < j <= LAG + SPLIT and not (isinstance(g, int) and g == 0):
                    split(g - 1, j - LAG - 1)

            def normed(t, j):
                dve.wait_ge(fac_mm, t + 1)
                if isinstance(t, int) and t < 4:
                    dve.wait_ge(sum_mm, NT - 3 + t)
                elif stacked:
                    dve.wait_ge(gate_mm, NG * (t - 3))
                else:
                    dve.wait_ge(lo_sb, t - 3)
                dve.scalar_tensor_tensor(out=h[:, j % 4, :], in0=xT[:, ds(t * T, T)], scalar=gmean,
                                         in1=FAC[j % 2][:, :], op0=ALU.subtract, op1=ALU.mult).then_inc(h_sb, 1)

            def projection(g, j):
                t = g * JP + j
                if stacked and within(t + 2):
                    high(dve, nc.vector.tensor_copy, t + 2, j + 2, 1)
                if within(t + 3):
                    normed(t + 3, j + 3)
                if isinstance(g, int) and g == 0 and j < SPLIT:
                    split(groups - 1, j)
                for m in range(NV):
                    dve.wait_ge(val_mm, NV * t + m + 1)
                    dve.wait_ge(gate_sb, NG * t + gate_of[m] + 1)
                    r = result(j, gate_of[m])
                    dve.scalar_tensor_tensor(out=r, in0=VB[(NV * j + m) % 2][:, :], scalar=bias(values[m]),
                                             in1=r, op0=ALU.add, op1=ALU.mult).then_inc(val_sb, 1)

            dve.memset(parts, 0.0).then_inc(zeroed, 1)
            dve.wait_ge(zeroed, 1)
            statistics(dve.Fori, statistic)
            for t in range(3):
                normed(t, t)
                if stacked and t < 2:
                    high(dve, nc.vector.tensor_copy, t, t, 1)
            projections(dve.Fori, projection)

        @block.sync
        def _(sp):
            with sp.Fori(0, NT // 4) as i:
                for k in range(4):
                    at = known(sp, (4 * i + k) * T)
                    sp.wait_ge(val_sb, i * (4 * NV) + NV * (k + 1))
                    for m in range(NG):
                        sp.dma_start(dsts[m][:, ds(at, T)], result(k, m)).then_inc(stored[k], 16)
            for s in stored:
                sp.wait_ge(s, 16 * NG * (NT // 4))


def make_mask(core, layer, mask):
    nc = core.nc
    with ExitStack() as ctx:
        landed, rep, made = core.sems(f"mask{layer}", "landed rep made")
        block = ctx.enter_context(nc.Block())
        if layer == 1:
            @block.sync
            def _(sp):
                sp.dma_start(mask, core.ins["L1_conv_mask"].rearrange("a (h p) k -> p (a h) k", h=2)).then_inc(landed, 16)
                sp.wait_ge(landed, 16)
            return
        m = core.ins["L3_conv_src_mask"]
        m2, at = core.area([P], 6000)
        m1, at = core.area([N], at)
        ones, at = core.area([P], at)
        mcol = core.fold[:, 12:14]

        @block.sync
        def _(sp):
            sp.dma_start(m2[0:2, :], m.rearrange("a (h p) -> (a h) p", h=2)).then_inc(landed, 16)
            sp.dma_start(m1[0:1, :], m).then_inc(landed, 16)

        @block.tensor
        def _(pe):
            pe.wait_ge(landed, 32)
            pe.transpose(core.bank[0][:, 0:2], m2[0:2, :], core.ident[0:2, 0:2]).then_inc(rep, 1)
            pe.wait_ge(made, 1)
            pe.matmul(core.bank[1][:, 0:N], ones[0:1, :], m1[0:1, :], start=True, stop=True).then_inc(rep, 1)

        @block.vector
        def _(dve):
            dve.memset(ones[0:1, :], 1.0).then_inc(made, 1)
            dve.wait_ge(rep, 1)
            dve.tensor_copy(mcol, core.bank[0][:, 0:2]).then_inc(made, 1)
            dve.wait_ge(rep, 2)
            dve.wait_ge(made, 2)
            for k in range(2):
                dve.tensor_scalar(mask[:, k, :], core.bank[1][:, 0:N], mcol[:, k:k + 1], None,
                                  ALU.mult).then_inc(made, 1)


def mix(core, layer, part, channels, rows, offsets, turns, z_row, cz, mask, sums):
    nc, bank = core.nc, core.bank
    z0, s1, s2 = sums
    at = 4 * 2 * N
    ab, at = core.area([8, 2 * N], at)
    tt, at = core.area([4, 2 * N], at)
    zs, at = core.area([2, 2 * N], at)
    dev, at = core.area([2, 2 * N], at)
    src = [r.rearrange("(h m) (p k) -> m p h k", h=2, k=N) for r in rows]
    zdst = core.z_d[0:2 * cz, 0:HALF].rearrange("(h m) (p k) -> m p h k", h=2, k=N)
    turn_a, turn_b = turns
    nturn = turn_a + turn_b
    TB = [[bank[0], bank[1]], [bank[2], bank[3]]]
    ZB = [bank[4], bank[5]]

    with ExitStack() as ctx:
        (masked_a, masked_a_even, masked_b, turn_mm, ta_sb, tb_sb, z_mm, z_sb, dev_sb, sq_sb, s1_sb, s2_sb, begun,
         s2_zero) = core.sems(f"mix{layer}{part}", "masked_a masked_a_even masked_b turn_mm ta_sb tb_sb z_mm z_sb dev_sb sq_sb "
                              "s1_sb s2_sb begun s2_zero")
        landed = core.sems(f"mix{layer}{part}", "in0 in1 in2 in3")
        stored = core.sems(f"mix{layer}{part}", "st0 st1")
        t_sb = (ta_sb, tb_sb)
        share = mask is not None and not nturn
        block = ctx.enter_context(nc.Block())

        def each_channel(loop, body):
            for b in range(4):
                body(b, b)
            with loop(1, channels // 4 - 1) as i:
                for b in range(4):
                    body(4 * i + b, b)
            for b in range(4):
                body(channels - 4 + b, b)

        def exists(c):
            return not isinstance(c, int) or 0 <= c < channels

        def loaded(o, b):
            return ab[:, 2 * b + o, :]

        def operand(o, b):
            buf = tt[:, 2 * o + b % 2, :] if turns[o] else loaded(o, b)
            return buf.rearrange("p (h k) -> p h k", h=2)

        @block.sync
        def _(sp):
            def load(c, b):
                at = [known(sp, c + offset) for offset in offsets]
                if nturn == 2:
                    at_least(sp, turn_mm, 2 * (c - 3))
                else:
                    at_least(sp, z_mm, c - 3)
                for o in range(2):
                    sp.dma_start(loaded(o, b).rearrange("p (h k) -> p h k", h=2),
                                 src[o][ds(at[o], 1)].rearrange("m p h k -> p (m h) k")).then_inc(landed[b], 16)
            each_channel(sp.Fori, load)
            for s in stored:
                sp.wait_ge(s, 8 * channels)

        @block.tensor
        def _(pe):
            def ready(c, b, o):
                if mask is not None and o:
                    pe.wait_ge(masked_b, c + 1)
                elif share:
                    pe.wait_ge(masked_a if b % 2 else masked_a_even, c + 2 - b % 2)
                elif mask is not None:
                    pe.wait_ge(masked_a, c + 1)
                else:
                    pe.wait_ge(landed[b], (c - b) * 8 + 32)

            def turn(c, b):
                for o in range(2):
                    if turns[o]:
                        ready(c, b, o)
                        at_least(pe, t_sb[o], c - 1)
                        x = loaded(o, b).rearrange("p (h k) -> p h k", h=2)
                        for kk in range(2):
                            for r in range(2):
                                mm = pe.transpose(TB[o][b % 2][:, kk * N + r * P:kk * N + r * P + P],
                                                  x[:, r, kk * P:kk * P + P], core.ident[:, :])
                        mm.then_inc(turn_mm, 1)

            def product(c, b):
                for o in range(2):
                    if turns[o]:
                        pe.wait_ge(t_sb[o], c + 1)
                    else:
                        ready(c, b, o)
                at_least(pe, z_sb, c - 1)
                a, x = operand(0, b), operand(1, b)
                for r in range(2):
                    for kk in range(2):
                        mm = pe.matmul(ZB[b % 2][:, r * N:r * N + N], a[:, kk, r * P:r * P + P], x[:, kk, :],
                                       start=(kk == 0), stop=(kk == 1))
                mm.then_inc(z_mm, 1)

            def channel(c, b):
                turn(c, b)
                if exists(c - 1):
                    product(c - 1, (b - 1) % 4)

            each_channel(pe.Fori, channel)
            product(channels - 1, 3)

        @block.scalar
        def _(act):
            def turned(c, b):
                if turns[0]:
                    act.wait_ge(turn_mm, nturn * c + 1)
                    at_least(act, z_mm, c - 1)
                    nc.scalar.copy(tt[:, b % 2, :], TB[0][b % 2][:, :]).then_inc(ta_sb, 1)

            def out(c, b):
                act.wait_ge(z_mm, c + 1)
                at_least(act, stored[b % 2], 8 * (c - b % 2))
                at_least(act, dev_sb, c - 1)
                nc.scalar.copy(zs[:, b % 2, :], ZB[b % 2][:, :]).then_inc(z_sb, 1)

            def square(c, b):
                act.wait_ge(s1_sb, c + 1)
                nc.scalar.activation(dev[:, b % 2, :], dev[:, b % 2, :], ACT.Square).then_inc(sq_sb, 1)

            def store(c, b):
                at = known(act, c + z_row)
                act.wait_ge(z_sb, c + 1)
                act.dma_start(zdst[ds(at, 1)].rearrange("m p h k -> p (m h) k"),
                              zs[:, b % 2, :].rearrange("p (h k) -> p h k", h=2)).then_inc(stored[b % 2], 16)

            def channel(c, b):
                turned(c, b)
                if exists(c - 1):
                    out(c - 1, (b - 1) % 4)
                if exists(c - 2):
                    square(c - 2, (b - 2) % 4)
                if exists(c - 1):
                    store(c - 1, (b - 1) % 4)

            each_channel(act.Fori, channel)
            out(channels - 1, 3)
            store(channels - 1, 3)
            for b in range(2, 4):
                square(channels - 4 + b, b)

        @block.vector
        def _(dve):
            def mask_b(c, b):
                if mask is not None:
                    dve.wait_ge(landed[b], (c - b) * 8 + 32)
                    if share and b % 2 == 0:
                        dve.tensor_tensor(loaded(0, b), loaded(0, b), mask.rearrange("p h k -> p (h k)"),
                                          ALU.mult).then_inc(masked_a_even, 2)
                    dve.tensor_tensor(loaded(1, b), loaded(1, b), mask.rearrange("p h k -> p (h k)"),
                                      ALU.mult).then_inc(masked_b, 1)

            def turned(c, b):
                if turns[1]:
                    dve.wait_ge(turn_mm, nturn * c + nturn)
                    at_least(dve, z_mm, c - 1)
                    dve.tensor_copy(tt[:, 2 + b % 2, :], TB[1][b % 2][:, :]).then_inc(tb_sb, 1)

            def deviation(c, b):
                dve.wait_ge(z_sb, c + 1)
                at_least(dve, s2_sb, c - 1)
                if isinstance(c, int) and c == 0 and part == 0:
                    dve.tensor_copy(z0, zs[:, 0, :]).then_inc(begun, 1)
                    dve.memset(s1, 0.0).then_inc(begun, 1)
                    dve.wait_ge(begun, 2)
                dve.tensor_tensor(dev[:, b % 2, :], zs[:, b % 2, :], z0, ALU.subtract).then_inc(dev_sb, 1)
                dve.wait_ge(dev_sb, c + 1)
                at_least(dve, s1_sb, c)
                dve.tensor_tensor(s1, s1, dev[:, b % 2, :], ALU.add).then_inc(s1_sb, 1)

            def channel(c, b):
                if exists(c + 2):
                    mask_b(c + 2, (b + 2) % 4)
                turned(c, b)
                if exists(c - 1):
                    deviation(c - 1, (b - 1) % 4)

            for b in range(2):
                mask_b(b, b)
            each_channel(dve.Fori, channel)
            deviation(channels - 1, 3)

        @block.gpsimd
        def _(pool):
            def mask_a(c, b):
                if mask is not None and not (share and b % 2 == 0):
                    pool.wait_ge(landed[b], (c - b) * 8 + 32)
                    pool.tensor_tensor(loaded(0, b), loaded(0, b), mask.rearrange("p h k -> p (h k)"),
                                       ALU.mult).then_inc(masked_a, 2 if share else 1)

            def squares(c, b):
                pool.wait_ge(sq_sb, c + 1)
                at_least(pool, s2_sb, c)
                pool.tensor_tensor(s2, s2, dev[:, b % 2, :], ALU.add).then_inc(s2_sb, 1)

            def channel(c, b):
                if exists(c + 2):
                    mask_a(c + 2, (b + 2) % 4)
                if exists(c - 2):
                    squares(c - 2, (b - 2) % 4)

            if part == 0:
                pool.memset(s2, 0.0).then_inc(s2_zero, 1)
                pool.wait_ge(s2_zero, 1)
            for b in range(2):
                mask_a(b, b)
            each_channel(pool.Fori, channel)
            for b in range(2, 4):
                squares(channels - 4 + b, b)


def fold_sums(core, layer, cz, sums):
    nc = core.nc
    z0, s1, s2 = sums
    at = 4 * 2 * N
    root, at = core.area([2 * N], at)
    var, at = core.area([2 * N], at)
    rec, at = core.area([2 * N], at)
    parts, at = core.area([3, 2 * N], at, BF16)
    eps = core.cols[:, 1:2] if layer == 3 else core.cols[:, 0:1]
    with ExitStack() as ctx:
        dve_s, rooted, stored = core.sems(f"var{layer}", "dve rooted stored")
        block = ctx.enter_context(nc.Block())

        @block.vector
        def _(dve):
            step = Steps(dve_s)

            def then(ins):
                step.done(ins)
                step.wait(dve)
            then(dve.scalar_tensor_tensor(out=root, in0=s1, scalar=1.0 / cz ** 2, in1=s1, op0=ALU.mult, op1=ALU.mult))
            then(dve.scalar_tensor_tensor(out=var, in0=s2, scalar=1.0 / cz, in1=root, op0=ALU.mult, op1=ALU.subtract))
            then(dve.tensor_scalar(var, var, 0.0, None, ALU.max))
            dve.wait_ge(rooted, 1)
            then(dve.reciprocal(rec, root))
            then(dve.tensor_copy(parts[:, 0, :], rec))
            then(dve.tensor_tensor(var, rec, parts[:, 0, :], ALU.subtract))
            then(dve.tensor_copy(parts[:, 1, :], var))
            then(dve.tensor_tensor(parts[:, 2, :], var, parts[:, 1, :], ALU.subtract))

        @block.scalar
        def _(act):
            nc.scalar.activation(core.fold[:, 14:15], core.cols[:, 0:1], ACT.Sqrt)
            act.wait_ge(dve_s, 3)
            nc.scalar.activation(root, var, ACT.Sqrt, bias=eps).then_inc(rooted, 1)

        @block.sync
        def _(sp):
            for n, made in enumerate((5, 7, 8)):
                sp.wait_ge(dve_s, made)
                sp.dma_start(core.rstd_d[n:n + 1, :].rearrange("a (h p k) -> p (a h) k", h=2, k=N),
                             parts[:, n, :].rearrange("p (h k) -> p h k", h=2)).then_inc(stored, 16)
            sp.wait_ge(stored, 48)


def finish(core, layer, nq, bg):
    nc, bank, xT = core.nc, core.bank, core.xT
    cz = C // nq
    J = SETS[nq]
    sets = NT // nq
    groups = sets // J
    out_w = {0: [f"wz{q}" for q in range(4)], 1: ["po0", "po1"], 2: ["pout"], 3: ["wout"]}[layer]
    stored_gate = layer >= 2
    FAC, GB, OB = [bank[0], bank[1]], [bank[2], bank[3]], bank[4:8]
    z, at = core.area([2, J, T], 0)
    gate, at = core.area([2, J, T] if stored_gate else [4, T], at)
    parts, at = core.area([2, T], at, BF16)
    zn, at = core.area([2, T], at)
    TERMS = 2 if stored_gate else 4
    term, at = core.area([TERMS, T], at)
    w = lambda name: core.w[:, SLOT[name], :]
    bias = lambda name: core.bias[:, BIAS[name]:BIAS[name] + 1]
    vec = lambda name: core.vec[:, VEC[name]:VEC[name] + 1]
    out_b = vec("b_out") if layer == 3 else bias(out_w[0])
    gate_b = bg if layer == 0 else bias("go0") if layer == 1 else None
    z_loads = 4 if nq == 1 else 2 * nq

    def each_set(loop, body):
        for g in range(2):
            for j in range(J):
                body(g, g % 2, j)
        with loop(1, groups // 2 - 1) as i:
            for e in range(2):
                for j in range(J):
                    body(2 * i + e, e, j)
        for g in range(groups - 2, groups):
            for j in range(J):
                body(g, g % 2, j)

    def later(g, e, j, n):
        j += n
        if j >= J:
            g, e, j = g + 1, 1 - e, j - J
        return None if isinstance(g, int) and g >= groups else (g, e, j)

    def earlier(g, j, q, n):
        at = j * nq + q - n
        if at < 0:
            g, at = g - 1, at + J * nq
        return None if isinstance(g, int) and g < 0 else (g, at // nq, at % nq)

    def number(g, j, q=0):
        return (g * J + j) * nq + q

    def columns(g, j, q):
        return ds(q * sets * T + (g * J + j) * T, T)

    def ring(j, q, n):
        return (j * nq + q) % n

    with ExitStack() as ctx:
        fac_mm, zn_sb, gate_mm, gate_sb, out_mm, term_sb, x_sb, stat_sb, cen_mm, cen_sb, zeroed = core.sems(
            f"fin{layer}", "fac_mm zn_sb gate_mm gate_sb out_mm term_sb x_sb stat_sb cen_mm cen_sb zeroed")
        landed = core.sems(f"fin{layer}", "in0 in1")
        gates_in = core.sems(f"fin{layer}", "gate0 gate1")
        block = ctx.enter_context(nc.Block())

        @block.sync
        def _(sp):
            def load(g, e):
                column = [known(sp, (q * sets + g * J) * T) for q in range(nq)]
                tile = [known(sp, q * sets + g * J) for q in range(nq)]
                at_least(sp, zn_sb, J * (g - 1))
                for q in range(nq):
                    sp.dma_start(z[q * 2 * cz:(q + 1) * 2 * cz, e, :, :].rearrange("p j t -> p (j t)"),
                                 core.z_d[0:2 * cz, ds(column[q], J * T)]).then_inc(landed[e], 16)
                    if nq > 1:
                        src = core.rstd_d.rearrange("n (h s t) -> (n h) s t", h=2, t=T)
                        sp.dma_start(parts[q * 6 * J:(q + 1) * 6 * J, e, :],
                                     src[:, ds(tile[q], J), :]).then_inc(landed[e], 16)
                        continue
                    for n in range(3):
                        src = core.rstd_d[n:n + 1, :].rearrange("a (h s t) -> s (a h) t", h=2, t=T)
                        sp.dma_start(parts[32 * n:32 * n + 2 * J, e, :],
                                     src[ds(tile[q], J), :, :]).then_inc(landed[e], 16)
                if stored_gate:
                    at_least(sp, cen_sb if layer == 3 else term_sb, J * (g - 1))
                    sp.dma_start(gate[:, e, :, :].rearrange("p j t -> p (j t)"),
                                 core.gate_d[:, ds(column[0], J * T)]).then_inc(gates_in[e], 16)
            sp.wait_ge(zeroed, 1)
            for g in range(2):
                load(g, g)
            with sp.Fori(1, groups // 2) as i:
                for e in range(2):
                    load(2 * i + e, e)

        @block.tensor
        def _(pe):
            def factor(g, e, j):
                if j == 0:
                    pe.wait_ge(landed[e], 8 * z_loads * (g - e) + 16 * z_loads)
                at_least(pe, zn_sb, g * J + j - 1)
                pe.matmul(FAC[j % 2][:, :], core.sel[:, SEL[nq] + j, :], parts[:, e, :], start=True,
                          stop=True).then_inc(fac_mm, 1)

            def gate_product(g, j, q, name, moving):
                at_least(pe, gate_sb, number(g, j, q) - 1)
                pe.matmul(GB[q % 2][:, :], w(name), moving, start=True, stop=True).then_inc(gate_mm, 1)

            def out_product(g, j, q, moving):
                at_least(pe, x_sb if layer == 3 else term_sb, number(g, j, q) - 3)
                pe.matmul(OB[ring(j, q, 4)][:, :], w(out_w[q]), moving, start=True, stop=True).then_inc(out_mm, 1)

            def gated_out(g, j):
                pe.wait_ge(cen_sb, g * J + j + 1)
                out_product(g, j, 0, term[:, j % 2, :])

            def one_set(g, e, j):
                ahead = later(g, e, j, 2)
                if ahead:
                    factor(*ahead)
                if layer == 3:
                    pe.wait_ge(zn_sb, g * J + j + 1)
                    at_least(pe, cen_sb, g * J + j - 1)
                    pe.matmul(GB[j % 2][:, :], w("zc"), zn[:, j % 2, :], start=True, stop=True).then_inc(cen_mm, 1)
                    before = earlier(g, j, 0, 1)
                    if before:
                        gated_out(before[0], before[1])
                    return
                for q in range(nq):
                    if layer == 0:
                        gate_product(g, j, q, "wg", xT[:, columns(g, j, q)])
                    if q == 0:
                        pe.wait_ge(zn_sb, g * J + j + 1)
                    if layer == 1:
                        gate_product(g, j, q, f"go{q}", zn[:, j % 2, :])
                    out_product(g, j, q, zn[:, j % 2, :])

            factor(0, 0, 0)
            factor(0, 0, 1)
            each_set(pe.Fori, one_set)
            if layer == 3:
                gated_out(groups - 1, J - 1)

        if not stored_gate:
            @block.scalar
            def _(act):
                def one_set(g, e, j):
                    for q in range(nq):
                        t = number(g, j, q)
                        act.wait_ge(gate_mm, t + 1)
                        at_least(act, term_sb, t - 3)
                        nc.scalar.activation(gate[:, ring(j, q, 4), :], GB[q % 2][:, :], ACT.Sigmoid,
                                             bias=gate_b).then_inc(gate_sb, 1)
                each_set(act.Fori, one_set)

        if layer < 3:
            @block.gpsimd
            def _(pool):
                def one_set(g, e, j):
                    for q in range(nq):
                        x = xT[:, columns(g, j, q)]
                        pool.wait_ge(term_sb, number(g, j, q) + 1)
                        pool.tensor_tensor(x, x, term[:, ring(j, q, TERMS), :], ALU.add).then_inc(x_sb, 1)
                each_set(pool.Fori, one_set)

        @block.vector
        def _(dve):
            def statistics(g, j, q):
                t = number(g, j, q)
                dve.wait_ge(x_sb, t + 1)
                dve.bn_stats(core.stats[:, ds(t, 1), :].rearrange("p a s -> p (a s)"),
                             xT[:, columns(g, j, q)]).then_inc(stat_sb, 1)

            def normed(g, e, j):
                s = g * J + j
                if j == 0:
                    dve.wait_ge(landed[e], 8 * z_loads * (g - e) + 16 * z_loads)
                dve.wait_ge(fac_mm, s + 1)
                at_least(dve, out_mm if layer < 3 else cen_mm, nq * (s - 1))
                dve.tensor_tensor(zn[:, j % 2, :], FAC[j % 2][:, :], z[:, e, j, :], ALU.mult).then_inc(zn_sb, 1)

            def gate_of(g, e, j, q):
                if stored_gate:
                    if j == 0:
                        dve.wait_ge(gates_in[e], 8 * (g - e) + 16)
                    return gate[:, e, j, :]
                dve.wait_ge(gate_sb, number(g, j, q) + 1)
                return gate[:, ring(j, q, 4), :]

            def gated(g, e, j):
                dve.wait_ge(cen_mm, g * J + j + 1)
                at_least(dve, out_mm, g * J + j - 1)
                dve.scalar_tensor_tensor(out=term[:, j % 2, :], in0=GB[j % 2][:, :], scalar=vec("out_norm_bias"),
                                         in1=gate_of(g, e, j, 0), op0=ALU.add, op1=ALU.mult).then_inc(cen_sb, 1)

            def residual(g, j):
                x = xT[:, columns(g, j, 0)]
                dve.wait_ge(out_mm, g * J + j + 1)
                dve.scalar_tensor_tensor(out=x, in0=OB[j % 4][:, :], scalar=out_b, in1=x, op0=ALU.add,
                                         op1=ALU.add).then_inc(x_sb, 1)

            def one_set(g, e, j):
                ahead = later(g, e, j, 1)
                if ahead:
                    normed(*ahead)
                if layer == 3:
                    gated(g, e, j)
                    before = earlier(g, j, 0, 2)
                    if before:
                        residual(before[0], before[1])
                    return
                for q in range(nq):
                    t = number(g, j, q)
                    gt = gate_of(g, e, j, q)
                    dve.wait_ge(out_mm, t + 1)
                    at_least(dve, x_sb, t - TERMS + 1)
                    dve.scalar_tensor_tensor(out=term[:, ring(j, q, TERMS), :], in0=OB[ring(j, q, 4)][:, :],
                                             scalar=out_b, in1=gt, op0=ALU.add, op1=ALU.mult).then_inc(term_sb, 1)
                    before = earlier(g, j, q, 2)
                    if before:
                        statistics(*before)

            dve.memset(parts, 0.0).then_inc(zeroed, 1)
            normed(0, 0, 0)
            each_set(dve.Fori, one_set)
            for n in (2, 1):
                g, j, q = earlier(groups, 0, 0, n)
                if layer == 3:
                    residual(g, j)
                else:
                    statistics(g, j, q)


def leave(core):
    nc, bank = core.nc, core.bank
    KC = 8
    dst = core.out.rearrange("a (h p) (n k) c -> (a n) p h k c", h=2, k=KC)
    stores = N // KC
    res, at = core.area([4, 2 * KC * C], 0)
    xT = core.xT[:, :].rearrange("q (p k) -> q p k", k=N)

    def each_store(loop, body):
        for b in range(4):
            body(b, b)
        with loop(1, stores // 4) as i:
            for b in range(4):
                body(4 * i + b, b)

    with ExitStack() as ctx:
        turned, kept_a, kept_v = core.sems("leave", "turned kept_a kept_v")
        stored = core.sems("leave", "st0 st1 st2 st3")
        kept = [kept_a, kept_v]
        block = ctx.enter_context(nc.Block())

        @block.tensor
        def _(pe):
            for n in range(stores):
                for half in range(2):
                    at_least(pe, kept[half], n - 3)
                    for k in range(4):
                        mm = pe.transpose(bank[2 * (n % 4) + half][:, k * P:(k + 1) * P],
                                          xT[:, :, n * KC + 4 * half + k], core.ident[:, :])
                    mm.then_inc(turned, 1)

        def keep(half, eng, copy):
            def one(n, b):
                eng.wait_ge(turned, 2 * n + half + 1)
                at_least(eng, stored[b], 8 * (n - b))
                to = res[:, b, :].rearrange("p (h k c) -> p h k c", h=2, k=KC)
                copy(to[:, :, 4 * half:4 * half + 4, :],
                     bank[2 * b + half][:, :].rearrange("p (k h c) -> p h k c", k=4, h=2)).then_inc(kept[half], 1)
            each_store(eng.Fori, one)

        @block.scalar
        def _(act):
            keep(0, act, nc.scalar.copy)

        @block.vector
        def _(dve):
            keep(1, dve, nc.vector.tensor_copy)

        @block.sync
        def _(sp):
            with sp.Fori(0, stores // 4) as i:
                for b in range(4):
                    at = known(sp, 4 * i + b)
                    for s in kept:
                        sp.wait_ge(s, 4 * i + b + 1)
                    for h in range(2):
                        sp.dma_start(dst[ds(at, 1), :, h, :, :].rearrange("a p k c -> p (a k c)"),
                                     res[:, b, h * KC * C:(h + 1) * KC * C]).then_inc(stored[b], 16)
            for s in stored:
                sp.wait_ge(s, 8 * stores)


def build(nc, ins, out):
    with ExitStack() as ctx:
        core = Core(nc, ctx, ins, out)
        sums = [core.area([2 * N], n * 2 * N)[0] for n in range(3)]
        mask, _ = core.area([2, N], 3 * 2 * N)
        rows = lambda first, n: core.hid_d[first:first + n, 0:HALF]
        load_weights(core)
        enter(core)

        b12, bg, _, _ = fold_group_norm(core, 0)
        project0(core, b12)
        mix(core, 0, 0, 16, (rows(0, 64), rows(0, 64)), (0, 16), (True, False), 0, 16, None, sums)
        fold_sums(core, 0, 16, sums)
        finish(core, 0, 4, bg)

        _, _, ub, gmean = fold_group_norm(core, 1)
        project(core, 1, ["gi"], ["pi"], ub, gmean)
        make_mask(core, 1, mask)
        mix(core, 1, 0, 16, (rows(0, P), rows(0, P)), (0, 16), (True, True), 0, 32, mask, sums)
        mix(core, 1, 1, 16, (rows(0, P), rows(0, P)), (32, 48), (False, False), 16, 32, mask, sums)
        fold_sums(core, 1, 32, sums)
        finish(core, 1, 2, None)

        _, _, ub, gmean = fold_group_norm(core, 2)
        project(core, 2, ["g2", OUTPUT_GATE[2], "g2"], ["p2", "p2"], ub, gmean)
        mix(core, 2, 0, 64, (rows(0, 2 * P), rows(0, 2 * P)), (0, C), (True, True), 0, 64, None, sums)
        fold_sums(core, 2, 64, sums)
        finish(core, 2, 1, None)

        _, _, ub, gmean = fold_group_norm(core, 3)
        project(core, 3, ["g3", OUTPUT_GATE[3], "g3"], ["p3", "p3"], ub, gmean)
        make_mask(core, 3, mask)
        mix(core, 3, 0, 64, (rows(0, 2 * P), rows(0, 2 * P)), (0, C), (False, False), 0, 64, mask, sums)
        fold_sums(core, 3, 64, sums)
        finish(core, 3, 1, None)
        leave(core)


def kernel(**inputs):
    import concourse.bacc as bacc
    from concourse.bass_utils import run_bass_kernel_spmd

    nc = bacc.Bacc("TRN2", target_bir_lowering=False, num_devices=1)
    arrays, ins = {}, {}
    inputs = {name: np.asarray(a) for name, a in inputs.items()}
    used = {name: inputs[name] for name in ("x", "L1_conv_mask", "L3_conv_src_mask")}
    for name, a in {**used, "weights": weight_layout(inputs), "vectors": vector_layout(inputs),
                    "constants": constants()}.items():
        a = np.ascontiguousarray(a)
        arrays[f"in_{name}"] = a
        ins[name] = nc.dram_tensor(f"in_{name}", a.shape, mybir.dt.from_np(a.dtype), kind="ExternalInput").ap()
    out = nc.dram_tensor("out", (1, N, N, C), F32, kind="ExternalOutput").ap()
    build(nc, ins, out)
    r = run_bass_kernel_spmd(nc, [arrays], core_ids=[0])
    return r.results[0]["out"]
```
